# Optimizing a Trainium2 kernel written in Bass

```python
import numpy as np
import jax
import jax.numpy as jnp

def _softmax(x, axis=-1):
    return jax.nn.softmax(x, axis=axis)

def _gelu(x):
    return jax.nn.gelu(x, approximate=True)

def _silu(x):
    return jax.nn.silu(x)

def _sigmoid(x):
    return jax.nn.sigmoid(x)

def _layernorm(x, axis=-1, eps=1e-05):
    m = jnp.mean(x, axis=axis, keepdims=True)
    v = jnp.var(x, axis=axis, keepdims=True)
    return (x - m) / jnp.sqrt(v + eps)

def _scatter_add(tgt, idx, src, axis=0):
    return tgt.at[idx].add(src)

def _segment_sum(src, seg, n):
    return jax.ops.segment_sum(src, seg, n)
kernel_name = 'mk_decoder_preln_d1_seqx_r8_2bc330'

def setup_inputs(seed: int=0):
    np.random.seed(seed)
    _w = jnp.asarray

    def _rec_inputs():
        import jax
        import jax.numpy as jnp
        _rk = jax.random.key(seed)
        x = -0.000125 + 0.9999 * jax.random.normal(jax.random.fold_in(_rk, 1), (64, 64, 256), jnp.float32)
        _lenS = 64 - jax.random.randint(jax.random.fold_in(_rk, 7), (64,), 0, max(1, 64 // 4) + 1, jnp.int32)
        _lenS2 = 64 - jax.random.randint(jax.random.fold_in(_rk, 8), (64,), 0, max(1, 64 // 4) + 1, jnp.int32)
        _ctx_2048P = jax.random.normal(jax.random.fold_in(_rk, 11), (64, 16, 256), jnp.float32)
        _ctx_2048c = jax.random.dirichlet(jax.random.fold_in(_rk, 511), 0.3 * jnp.ones((16,), jnp.float32), (64, 64))
        _ctx_2048t = jnp.einsum('bsk,bkd->bsd', _ctx_2048c, _ctx_2048P)
        _ctx_2048t = _ctx_2048t * jax.lax.rsqrt(jnp.mean(jnp.square(_ctx_2048t)) + 1e-12) * 0.953939
        ctx_2048 = -1.52775e-05 + 0.999936 * (_ctx_2048t + 0.3 * jax.random.normal(jax.random.fold_in(_rk, 611), (64, 64, 256), jnp.float32))
        return (x, ctx_2048)
    x, ctx_2048 = _rec_inputs()

    def _L0_attn_setup():
        import jax, jax.numpy as jnp
        import numpy as np
        H = 16
        CHUNK = 64
        EPS = 1e-05

        def _forward(x, wq, wk, wv, wo, fq1_w, fq1_b, fq2_w, fq2_b, fk1_w, fk1_b, fk2_w, fk2_b, norm_w):
            B, L, D = x.shape
            dk = D // H

            def proj(w):
                return (x @ w.T).reshape(B, L, H, dk).transpose(0, 2, 1, 3)
            q, k, v = (proj(wq), proj(wk), proj(wv))
            q = (q @ fq1_w.T + fq1_b) * (q @ fq2_w.T + fq2_b)
            k = (k @ fk1_w.T + fk1_b) * (k @ fk2_w.T + fk2_b)
            scale = dk ** (-0.5)
            n = L // CHUNK
            qc = q.reshape(B, H, n, CHUNK, dk) * scale
            kc = k.reshape(B, H, n, CHUNK, dk)
            vc = v.reshape(B, H, n, CHUNK, dk)
            kv = jnp.einsum('bhncd,bhnce->bhnde', kc, vc)
            kv = jnp.cumsum(kv, axis=2)
            kv = jnp.concatenate([jnp.zeros_like(kv[:, :, :1]), kv[:, :, :-1]], axis=2)
            inter = jnp.einsum('bhncd,bhnde->bhnce', qc, kv)
            s = jnp.einsum('bhncd,bhnmd->bhncm', qc, kc)
            mask = jnp.tril(jnp.ones((CHUNK, CHUNK), bool))
            s = jnp.where(mask, s, 0.0)
            intra = jnp.einsum('bhncm,bhnmd->bhncd', s, vc)
            o = (inter + intra).reshape(B, H, L, dk)
            o = o * jax.lax.rsqrt(jnp.mean(o * o, axis=-1, keepdims=True) + EPS) * norm_w
            o = o.transpose(0, 2, 1, 3).reshape(B, L, D)
            return o @ wo.T
        key = jax.random.key(seed)
        ks = jax.random.split(key, 16)
        B, L, D = (2, 512, 256)
        dk = D // H
        g = 2 ** (-2.5)

        def xav(k, n):
            lim = g * np.sqrt(6.0 / (2 * n))
            return jax.random.uniform(k, (n, n), jnp.float32, -lim, lim)
        return {'x': jax.random.normal(ks[0], (B, L, D), jnp.float32), 'wq': xav(ks[1], D), 'wk': xav(ks[2], D), 'wv': xav(ks[3], D), 'wo': xav(ks[4], D), 'fq1_w': xav(ks[5], dk), 'fq1_b': jnp.zeros((dk,), jnp.float32), 'fq2_w': xav(ks[6], dk), 'fq2_b': jnp.zeros((dk,), jnp.float32), 'fk1_w': xav(ks[7], dk), 'fk1_b': jnp.zeros((dk,), jnp.float32), 'fk2_w': xav(ks[8], dk), 'fk2_b': jnp.zeros((dk,), jnp.float32), 'norm_w': jnp.ones((dk,), jnp.float32)}
    _L0_attn_all = _L0_attn_setup()
    _L0_attn_in = {k: v for k, v in _L0_attn_all.items() if k in ('wq', 'wk', 'wv', 'wo', 'fq1_w', 'fq1_b', 'fq2_w', 'fq2_b', 'fk1_w', 'fk1_b', 'fk2_w', 'fk2_b', 'norm_w')}
    del _L0_attn_all

    def _L0_xattn_setup():
        import jax, jax.numpy as jnp
        import numpy as np
        B, S, D, H = (4, 512, 256, 16)
        HD = D // H
        key = jax.random.key(seed)
        ks = jax.random.split(key, 12)
        sc = 1.0 / np.sqrt(D)
        inp = {'q': jax.random.normal(ks[0], (B, S, D), jnp.float32), 'k': jax.random.normal(ks[1], (B, S, D), jnp.float32), 'v': jax.random.normal(ks[2], (B, S, D), jnp.float32), 'Wq': jax.random.normal(ks[3], (D, D), jnp.float32) * sc, 'bq': jnp.zeros((D,), jnp.float32), 'Wk': jax.random.normal(ks[4], (D, D), jnp.float32) * sc, 'bk': jnp.zeros((D,), jnp.float32), 'Wv': jax.random.normal(ks[5], (D, D), jnp.float32) * sc, 'bv': jnp.zeros((D,), jnp.float32), 'Wo': jax.random.normal(ks[6], (D, D), jnp.float32) * sc, 'bo': jnp.zeros((D,), jnp.float32)}
        return inp
    _L0_xattn_all = _L0_xattn_setup()
    _L0_xattn_in = {k: v for k, v in _L0_xattn_all.items() if k in ('Wq', 'bq', 'Wk', 'bk', 'Wv', 'bv', 'Wo', 'bo')}
    del _L0_xattn_all

    def _L0_ffn_setup():
        import jax, jax.numpy as jnp
        import numpy as np
        H = 256
        I = 128
        E = 32
        K = 4
        N_SHARED = 1
        EPS = 1e-06

        def _rmsnorm(x, w, eps=EPS):
            var = jnp.mean(jnp.square(x), axis=-1, keepdims=True)
            return x * jax.lax.rsqrt(var + eps) * w

        def _moe_core(x, gate_w, w13, w2):
            T = x.shape[0]
            N = T * K
            C = 2 * N // E
            logits = jnp.einsum('th,eh->te', x.astype(jnp.float32), gate_w.astype(jnp.float32))
            scores = jax.nn.softmax(logits, axis=-1)
            topk_w, topk_ids = jax.lax.top_k(scores, K)
            topk_w = topk_w / jnp.sum(topk_w, axis=-1, keepdims=True)
            flat_ids = topk_ids.reshape(-1)
            flat_w = topk_w.reshape(-1)
            order = jnp.argsort(flat_ids)
            sorted_eid = flat_ids[order]
            tok = order // K
            counts = jnp.zeros((E,), jnp.int32).at[flat_ids].add(1)
            starts = jnp.cumsum(counts) - counts
            pos = jnp.arange(N) - starts[sorted_eid]
            buf = jnp.zeros((E, C, x.shape[1]), x.dtype).at[sorted_eid, pos].set(x[tok], mode='drop')
            gu = jnp.einsum('ech,ehf->ecf', buf, w13)
            g, u = jnp.split(gu, 2, axis=-1)
            act = jax.nn.silu(g) * u
            eo = jnp.einsum('eci,eih->ech', act, w2)
            out_slots = eo[sorted_eid, pos]
            routed = jnp.zeros_like(x).at[tok].add(out_slots * flat_w[order][:, None])
            return routed
        key = jax.random.key(seed)
        ks = jax.random.split(key, 8)
        s = 1.0 / np.sqrt(H)
        si = 1.0 / np.sqrt(I)
        return {'hidden_states': jax.random.normal(ks[0], (1, 512, H), jnp.float32), 'norm_w': jnp.ones((H,), jnp.float32), 'gate_w': jax.random.normal(ks[1], (E, H), jnp.float32) * s, 'w13': jax.random.normal(ks[2], (E, H, 2 * I), jnp.float32) * s, 'w2': jax.random.normal(ks[3], (E, I, H), jnp.float32) * si, 'shared_gate_w': jax.random.normal(ks[4], (H, I * N_SHARED), jnp.float32) * s, 'shared_up_w': jax.random.normal(ks[5], (H, I * N_SHARED), jnp.float32) * s, 'shared_down_w': jax.random.normal(ks[6], (I * N_SHARED, H), jnp.float32) * si}
    _L0_ffn_all = _L0_ffn_setup()
    _L0_ffn_in = {k: v for k, v in _L0_ffn_all.items() if k in ('norm_w', 'gate_w', 'w13', 'w2', 'shared_gate_w', 'shared_up_w', 'shared_down_w')}
    del _L0_ffn_all
    return {'x': x, 'ctx_2048': ctx_2048, 'L0_attn_wq': _L0_attn_in['wq'], 'L0_attn_wk': _L0_attn_in['wk'], 'L0_attn_wv': _L0_attn_in['wv'], 'L0_attn_wo': _L0_attn_in['wo'], 'L0_attn_fq1_w': _L0_attn_in['fq1_w'], 'L0_attn_fq1_b': _L0_attn_in['fq1_b'], 'L0_attn_fq2_w': _L0_attn_in['fq2_w'], 'L0_attn_fq2_b': _L0_attn_in['fq2_b'], 'L0_attn_fk1_w': _L0_attn_in['fk1_w'], 'L0_attn_fk1_b': _L0_attn_in['fk1_b'], 'L0_attn_fk2_w': _L0_attn_in['fk2_w'], 'L0_attn_fk2_b': _L0_attn_in['fk2_b'], 'L0_attn_norm_w': _L0_attn_in['norm_w'], 'L0_xattn_Wq': _L0_xattn_in['Wq'], 'L0_xattn_bq': _L0_xattn_in['bq'], 'L0_xattn_Wk': _L0_xattn_in['Wk'], 'L0_xattn_bk': _L0_xattn_in['bk'], 'L0_xattn_Wv': _L0_xattn_in['Wv'], 'L0_xattn_bv': _L0_xattn_in['bv'], 'L0_xattn_Wo': _L0_xattn_in['Wo'], 'L0_xattn_bo': _L0_xattn_in['bo'], 'L0_ffn_norm_w': _L0_ffn_in['norm_w'], 'L0_ffn_gate_w': _L0_ffn_in['gate_w'], 'L0_ffn_w13': _L0_ffn_in['w13'], 'L0_ffn_w2': _L0_ffn_in['w2'], 'L0_ffn_shared_gate_w': _L0_ffn_in['shared_gate_w'], 'L0_ffn_shared_up_w': _L0_ffn_in['shared_up_w'], 'L0_ffn_shared_down_w': _L0_ffn_in['shared_down_w']}

def reference(x, ctx_2048, L0_attn_wq, L0_attn_wk, L0_attn_wv, L0_attn_wo, L0_attn_fq1_w, L0_attn_fq1_b, L0_attn_fq2_w, L0_attn_fq2_b, L0_attn_fk1_w, L0_attn_fk1_b, L0_attn_fk2_w, L0_attn_fk2_b, L0_attn_norm_w, L0_xattn_Wq, L0_xattn_bq, L0_xattn_Wk, L0_xattn_bk, L0_xattn_Wv, L0_xattn_bv, L0_xattn_Wo, L0_xattn_bo, L0_ffn_norm_w, L0_ffn_gate_w, L0_ffn_w13, L0_ffn_w2, L0_ffn_shared_gate_w, L0_ffn_shared_up_w, L0_ffn_shared_down_w):
    import jax
    import jax.numpy as jnp

    def _L0_attn_ref(x, wq, wk, wv, wo, fq1_w, fq1_b, fq2_w, fq2_b, fk1_w, fk1_b, fk2_w, fk2_b, norm_w):
        import jax, jax.numpy as jnp
        import numpy as np
        H = 16
        CHUNK = 64
        EPS = 1e-05

        def _forward(x, wq, wk, wv, wo, fq1_w, fq1_b, fq2_w, fq2_b, fk1_w, fk1_b, fk2_w, fk2_b, norm_w):
            B, L, D = x.shape
            dk = D // H

            def proj(w):
                return (x @ w.T).reshape(B, L, H, dk).transpose(0, 2, 1, 3)
            q, k, v = (proj(wq), proj(wk), proj(wv))
            q = (q @ fq1_w.T + fq1_b) * (q @ fq2_w.T + fq2_b)
            k = (k @ fk1_w.T + fk1_b) * (k @ fk2_w.T + fk2_b)
            scale = dk ** (-0.5)
            n = L // CHUNK
            qc = q.reshape(B, H, n, CHUNK, dk) * scale
            kc = k.reshape(B, H, n, CHUNK, dk)
            vc = v.reshape(B, H, n, CHUNK, dk)
            kv = jnp.einsum('bhncd,bhnce->bhnde', kc, vc)
            kv = jnp.cumsum(kv, axis=2)
            kv = jnp.concatenate([jnp.zeros_like(kv[:, :, :1]), kv[:, :, :-1]], axis=2)
            inter = jnp.einsum('bhncd,bhnde->bhnce', qc, kv)
            s = jnp.einsum('bhncd,bhnmd->bhncm', qc, kc)
            mask = jnp.tril(jnp.ones((CHUNK, CHUNK), bool))
            s = jnp.where(mask, s, 0.0)
            intra = jnp.einsum('bhncm,bhnmd->bhncd', s, vc)
            o = (inter + intra).reshape(B, H, L, dk)
            o = o * jax.lax.rsqrt(jnp.mean(o * o, axis=-1, keepdims=True) + EPS) * norm_w
            o = o.transpose(0, 2, 1, 3).reshape(B, L, D)
            return o @ wo.T
        return _forward(x, wq, wk, wv, wo, fq1_w, fq1_b, fq2_w, fq2_b, fk1_w, fk1_b, fk2_w, fk2_b, norm_w)

    def _L0_xattn_ref(q, k, v, Wq, bq, Wk, bk, Wv, bv, Wo, bo):
        import jax, jax.numpy as jnp
        import numpy as np
        B, S, D, H = (4, 512, 256, 16)
        HD = D // H
        bs, sl, nf = q.shape
        Q = (q @ Wq.T + bq).reshape(bs, sl, H, HD)
        K = (k @ Wk.T + bk).reshape(bs, sl, H, HD)
        V = (v @ Wv.T + bv).reshape(bs, sl, H, HD)
        score = jnp.einsum('bshd,bsgd->bshg', Q, K)
        weight = jax.nn.softmax(score, axis=-1)
        attn = jnp.einsum('bshg,bsgd->bshd', weight, V).reshape(bs, sl, nf)
        return attn @ Wo.T + bo

    def _L0_ffn_ref(hidden_states, norm_w, gate_w, w13, w2, shared_gate_w, shared_up_w, shared_down_w):
        import jax, jax.numpy as jnp
        import numpy as np
        H = 256
        I = 128
        E = 32
        K = 4
        N_SHARED = 1
        EPS = 1e-06

        def _rmsnorm(x, w, eps=EPS):
            var = jnp.mean(jnp.square(x), axis=-1, keepdims=True)
            return x * jax.lax.rsqrt(var + eps) * w

        def _moe_core(x, gate_w, w13, w2):
            T = x.shape[0]
            N = T * K
            C = 2 * N // E
            logits = jnp.einsum('th,eh->te', x.astype(jnp.float32), gate_w.astype(jnp.float32))
            scores = jax.nn.softmax(logits, axis=-1)
            topk_w, topk_ids = jax.lax.top_k(scores, K)
            topk_w = topk_w / jnp.sum(topk_w, axis=-1, keepdims=True)
            flat_ids = topk_ids.reshape(-1)
            flat_w = topk_w.reshape(-1)
            order = jnp.argsort(flat_ids)
            sorted_eid = flat_ids[order]
            tok = order // K
            counts = jnp.zeros((E,), jnp.int32).at[flat_ids].add(1)
            starts = jnp.cumsum(counts) - counts
            pos = jnp.arange(N) - starts[sorted_eid]
            buf = jnp.zeros((E, C, x.shape[1]), x.dtype).at[sorted_eid, pos].set(x[tok], mode='drop')
            gu = jnp.einsum('ech,ehf->ecf', buf, w13)
            g, u = jnp.split(gu, 2, axis=-1)
            act = jax.nn.silu(g) * u
            eo = jnp.einsum('eci,eih->ech', act, w2)
            out_slots = eo[sorted_eid, pos]
            routed = jnp.zeros_like(x).at[tok].add(out_slots * flat_w[order][:, None])
            return routed
        B, S, Hd = hidden_states.shape
        residual = hidden_states
        h = _rmsnorm(hidden_states, norm_w)
        x = h.reshape(-1, Hd)
        routed = _moe_core(x, gate_w, w13, w2)
        shared = jax.nn.silu(x @ shared_gate_w) * (x @ shared_up_w) @ shared_down_w
        out = residual + (routed + shared).reshape(B, S, Hd)
        return out
    x = x + _L0_attn_ref(_layernorm(x, axis=-1), L0_attn_wq, L0_attn_wk, L0_attn_wv, L0_attn_wo, L0_attn_fq1_w, L0_attn_fq1_b, L0_attn_fq2_w, L0_attn_fq2_b, L0_attn_fk1_w, L0_attn_fk1_b, L0_attn_fk2_w, L0_attn_fk2_b, L0_attn_norm_w)
    x = x + _L0_xattn_ref(_layernorm(x, axis=-1), ctx_2048, ctx_2048, L0_xattn_Wq, L0_xattn_bq, L0_xattn_Wk, L0_xattn_bk, L0_xattn_Wv, L0_xattn_bv, L0_xattn_Wo, L0_xattn_bo)
    x = x + _L0_ffn_ref(_layernorm(x, axis=-1), L0_ffn_norm_w, L0_ffn_gate_w, L0_ffn_w13, L0_ffn_w2, L0_ffn_shared_gate_w, L0_ffn_shared_up_w, L0_ffn_shared_down_w)
    return x

_drawn_inputs = setup_inputs


def setup_inputs(seed=0):
    import zlib

    import numpy as np

    out = dict(_drawn_inputs(seed))
    spreads = {'L0_attn_fq1_b': (0.0, 0.729),
     'L0_attn_fq2_b': (0.0, 0.681),
     'L0_attn_fk1_b': (0.0, 0.667),
     'L0_attn_fk2_b': (0.0, 0.799),
     'L0_attn_norm_w': (1.0, 0.6),
     'L0_xattn_bq': (0.0, 0.1),
     'L0_xattn_bk': (0.0, 0.1),
     'L0_xattn_bv': (0.0, 0.1),
     'L0_xattn_bo': (0.0, 0.1),
     'L0_ffn_norm_w': (1.0, 0.2)}
    factors = {'L0_attn_wq': 7.779,
     'L0_attn_wk': 7.239,
     'L0_attn_wv': 5.401,
     'L0_attn_wo': 5.454,
     'L0_attn_fq1_w': 6.84,
     'L0_attn_fq2_w': 8.0,
     'L0_attn_fk1_w': 8.0,
     'L0_attn_fk2_w': 7.515}
    for name, (base, spread) in spreads.items():
        noise = np.random.default_rng([zlib.crc32(name.encode()), seed]).standard_normal(out[name].shape)
        drawn = base * np.exp(spread * noise) if base else spread * noise
        out[name] = jnp.asarray(drawn.astype(out[name].dtype))
    for name, factor in factors.items():
        out[name] = (out[name] * factor).astype(out[name].dtype)
    return out
```

```python
from contextlib import ExitStack

import concourse.bass as bass
from concourse import mybir

F32 = mybir.dt.float32
BF16 = mybir.dt.bfloat16
I32 = mybir.dt.int32
U32 = mybir.dt.uint32
ALU = mybir.AluOpType
ACT = mybir.ActivationFunctionType
X = mybir.AxisListType.X

P = 128
L = 64
D = 256
H = 16
DK = D // H
KC = D // P
E = 32
TOPK = 4
FF = 128
NCH = 4
HC = H // NCH
LN_EPS = 1e-5
RMS_EPS = 1e-6
HEAD_EPS = 1e-5


def decoder_layer_kernel(nc, a, out):
    NB, _, _ = a["x"].shape
    T = NB * L
    NT = T // P
    CAP = TOPK * T * 2 // E
    J = (CAP + P - 1) // P
    EJ = E * J
    EC = (EJ + P - 1) // P
    ER = min(EJ, P)
    MT = min(EJ, (TOPK * T + E * (P - 1)) // P)
    MT += -MT % 4
    TRASH = E * CAP
    assert NT >= 10 and NT % 4 == 0 and CAP % P == 0 and EJ % ER == 0

    x_d = a["x"].rearrange("b l d -> (b l) d")
    out_d = out.rearrange("b l d -> (b l) d")
    ctxT_d = a["ctxT"].rearrange("(k p) t -> p k t", p=P)
    h_d = nc.dram_tensor("h_rows", (T, D), F32, kind="Internal").ap()
    list_d = nc.dram_tensor("token_lists", (E * CAP + TOPK * T, 1), I32, kind="Internal").ap()
    acc_d = nc.dram_tensor("acc_rows", (T, D), F32, kind="Internal").ap()
    eo_d = nc.dram_tensor("expert_rows", (MT * P, D), F32, kind="Internal").ap()

    with ExitStack() as ctx:
        def sb(name, shape, dt=F32):
            return ctx.enter_context(nc.sbuf_tensor(name, shape, dt))

        def ps(name, shape, dt=F32):
            return ctx.enter_context(nc.psum_tensor(name, shape, dt))

        def sem(name):
            return ctx.enter_context(nc.semaphore(name))

        ident = sb("ident", [P, P])
        ones = sb("ones", [P, P])
        causal = sb("causal", [P, L])
        headmask = sb("headmask", [P, P])
        evens = sb("evens", [P, 4])
        parmask = sb("parmask", [P, 2])
        before = sb("before", [P, P], BF16)
        ones_h = sb("ones_h", [P, P], BF16)
        expert_row = sb("expert_row", [P, E])
        eps = sb("eps", [P, 2])
        tok_id = sb("tok_id", [P, NT], I32)
        trash_row = sb("trash_row", [P, NT, TOPK])
        zeros_i = sb("zeros_i", [P, (E * CAP + P - 1) // P], I32)
        w_f = sb("w_f", [P, 4, KC, D])
        f_b = sb("f_b", [P, 4])
        f_b2 = sb("f_b2", [P, 3])
        hn_w = sb("hn_w", [P, 1])
        w_v = sb("w_v", [P, KC, D])
        w_o = sb("w_o", [P, KC, D])
        W_q = sb("W_q", [P, KC, D])
        W_kv = sb("W_kv", [P, KC, 2, D])
        W_o = sb("W_o", [P, KC, D])
        b_x = sb("b_x", [P, 4, D])
        nw = sb("nw", [P, D])
        w_gate = sb("w_gate", [P, KC, E])
        w_sgu = sb("w_sgu", [P, KC, 2, FF])
        w_sd = sb("w_sd", [P, D])
        w13 = sb("w13", [P, E, KC, 2 * FF])
        w2 = sb("w2", [P, E, D])

        x_t = sb("x_t", [P, 2, D])
        st_a = sb("st_a", [P, 6])
        mv_a = sb("mv_a", [P, 2])
        r_a = sb("r_a", [P, 2])
        xn = sb("xn", [P, D])
        xT = sb("xT", [P, KC, P])
        tq = sb("tq", [P, KC, P])
        tk = sb("tk", [P, 2, KC, P])
        qf = sb("qf", [P, KC, P])
        kblk = sb("kblk", [P, KC * 2, 2, L])
        vblk = sb("vblk", [P, 2, H // 2, 2 * DK])
        sm = sb("sm", [P, 4, 2 * KC, L])
        osq = sb("osq", [P, D])
        r_o = sb("r_o", [P, 2, D])
        oT = sb("oT", [P, KC, P])
        x1 = sb("x1", [P, 2, D])
        st_b = sb("st_b", [P, 6])
        mv_b = sb("mv_b", [P, 2])
        r_b = sb("r_b", [P, 2])
        x1n = sb("x1n", [P, D])
        x1T = sb("x1T", [P, KC, P])
        c_t = sb("c_t", [P, 2, KC, P])
        qkv_raw = sb("qkv_raw", [P, 3, D])
        qkv = sb("qkv", [P, 2, 3, D])
        xb = sb("xb", [P, 2, D])
        prod = sb("prod", [P, 2, HC * H * DK])
        sc = sb("sc", [P, H, H])
        mx = sb("mx", [P, H])
        scm = sb("scm", [P, H, H])
        pr = sb("pr", [P, H, H])
        psm = sb("psm", [P, H])
        pri = sb("pri", [P, H])
        ao = sb("ao", [P, H, DK])
        att = sb("att", [P, D])
        attT = sb("attT", [P, KC, P])
        x2 = sb("x2", [P, D])
        st_c = sb("st_c", [P, 6])
        mv_c = sb("mv_c", [P, 2])
        r_c = sb("r_c", [P, 2])
        v2 = sb("v2", [P, 1])
        r2 = sb("r2", [P, 2])
        y = sb("y", [P, D])
        hrow = sb("hrow", [P, 2, D])
        res = sb("res", [P, 2, D])
        hT = sb("hT", [P, KC, P])
        eg = sb("eg", [P, P])
        gs = sb("gs", [P, P])
        act_s = sb("act_s", [P, P])
        top = sb("top", [P, 8])
        topi = sb("topi", [P, 8], U32)
        topf = sb("topf", [P, TOPK])
        dl = sb("dl", [P, TOPK])
        ew = sb("ew", [P, TOPK])
        es = sb("es", [P, 1])
        rs = sb("rs", [P, 1])
        oh = sb("oh", [P, TOPK, E])
        mask_h = sb("mask_h", [P, E], BF16)
        seen = sb("seen", [P, 2, E], BF16)
        pk = sb("pk", [P, TOPK, E])
        pos = sb("pos", [P, TOPK])
        over = sb("over", [P, TOPK])
        row = sb("row", [P, TOPK])
        gap = sb("gap", [P, TOPK])
        slot = sb("slot", [P, 2, TOPK], U32)
        tid = sb("tid", [P, 2], I32)
        route = sb("route", [P, NT, 3, TOPK])
        acc = sb("acc", [P, 2, D])
        cnt_c = sb("cnt_c", [E, 1])
        jrow = sb("jrow", [E, J])
        have = sb("have", [E, J])
        nt_c = sb("nt_c", [E, 1])
        nt_b = sb("nt_b", [E, P])
        e_lt = sb("e_lt", [E, E])
        r_lt = sb("r_lt", [E, EJ])
        r_eq = sb("r_eq", [E, EJ])
        rcol = sb("rcol", [P, EC])
        past = sb("past", [P, EC, E])
        jend = sb("jend", [P, E])
        ecol = sb("ecol", [P, EC, 2])
        jcol = sb("jcol", [P, EC])
        base = sb("base", [P, E])
        dst = sb("dst", [P, EC])
        nov = sb("nov", [P, EC])
        dstv = sb("dstv", [P, EC])
        tcol = sb("tcol", [P, MT])
        hot = sb("hot", [P, EC, MT])
        list_i = sb("list_i", [P, EC, P], I32)
        list_f = sb("list_f", [P, EC, P])
        gidx = sb("gidx", [P, MT + 4], U32)
        eid = sb("eid", [2, MT], I32)
        gcol = sb("gcol", [P, 4], U32)
        sg = sb("sg", [P, 2, FF])
        ag = sb("ag", [P, 2, FF])
        agT = sb("agT", [P, 2, P])
        cb = sb("cb", [P, NT, TOPK])
        cidx = sb("cidx", [P, NT, TOPK], U32)
        ccol = sb("ccol", [P, 2, TOPK], U32)
        wcol = sb("wcol", [P, 2, TOPK])

        early = w13[:].rearrange("p e k f -> p (e k f)")
        w_nat = early[:, 0:2 * KC * D].rearrange("p (n k d) -> p n k d", n=2, k=KC)
        early = early[:, 2 * KC * D:]
        w_o_raw = early[:, 0:KC * D].rearrange("p (k d) -> p k d", k=KC)
        early = early[:, KC * D:]
        f_t = early[:, 0:4 * P].rearrange("p (n m) -> p n m", n=4)
        f_bd = early[:, 4 * P:8 * P].rearrange("p (n m) -> p n m", n=4)
        er = prod[:].rearrange("p b (k d) -> p b k d", k=TOPK)
        part = sm[:].rearrange("p j c l -> p (j c l)").rearrange("p (k d) -> p k d", k=4)
        fin = x1
        xg = qkv[:].rearrange("p b n d -> p (b n) d")
        xgT = kblk[:].rearrange("p c m l -> p (c m l)").rearrange("p (n k t) -> p n k t", n=2, k=KC)
        eo = xb
        bk_e = W_kv[:].rearrange("p k n d -> p (k n d)")[:, 0:NT * TOPK // 4 * E].rearrange("p (t e) -> p t e", e=E)

        TA = ps("TA", [P, 512])
        TB = ps("TB", [P, 512])
        QQ = ps("QQ", [P, 512])
        KK = ps("KK", [P, 512])
        S = ps("S", [P, 4, 512])

        names = """w_in fold_in zero_in experts_in c_setup c_bd fold_ps fold_done setup_done
            st_a_ok mv_a_ok ln_a_ok r_a_ok xn_ok xT_ps xT_ok q_ps k_ps v_ps tq_ok tk_ok v_ok qf_ok kf_ok s_ps s_ok
            o_ps osq_ok ms_ps ln_o_ok r_o_ok oT_ok wo_ps x1_ok
            st_b_ok mv_b_ok ln_b_ok r_b_ok x1n_ok x1T_ps x1T_ok kv_ps kv_cp Q_ps Q_cp kvb_ok qb_ok xb_ok
            kp1 kp2 kp3 ks0 ks1 sc_ok mx_ok scm_ok pr_ok psm_ok pri_ok vp1 vp2 vp3 vs0 vs1 ao_ok att_ok
            attT_ps attT_ok Wo_ps x2_ok st_c_ok mv_c_ok ln_c_ok r_c_ok y_ok v2_ok ln_2_ok r2_ok h_ok res_ok
            hT_ps hT_ok gu_ps lg_ps eg_ok lne_ok sig_ok gs_ok act_ok top_ok topi_ok dl_ok ew_ok rs_ok
            topf_ok oh_ok mask_ok seen_ok dn_ps acc_ok pos_ps pk_ok pos_ok row_ok gap_ok gapo_ok slot_ok
            tick lists_in c_small
            table_ps table_ok linked plan_ok
            gcol_ok gx_ps gx_ok gg_ps sg_ok ag_ok agT_ps agT_ok dn2_ps eo_ok
            cidx_ok ccol_ok part_ok fin_ok""".split()
        s = {n: sem(n) for n in names}
        x_in = [sem("x_in0"), sem("x_in1")]
        c_in = [sem("c_in0"), sem("c_in1")]
        h_out = [sem("h_out0"), sem("h_out1")]
        acc_out = [sem("acc_out0"), sem("acc_out1")]
        acc_in = [sem("acc_in0"), sem("acc_in1")]
        sent = [sem("sent0"), sem("sent1")]
        g_in = [sem(f"g_in{n}") for n in range(4)]
        eo_out = [sem("eo_out0"), sem("eo_out1")]
        er_in = [sem("er_in0"), sem("er_in1")]
        out_done = [sem("out_done0"), sem("out_done1")]

        class Step:

            def __init__(self, eng, turn, q, unroll=2, count=NT):
                self.eng, self.turn, self.q, self.unroll, self.count = eng, turn, q, unroll, count
                self.n = turn * unroll + q
                self.fixed = isinstance(turn, int)
                self.kept = {}

            def on(self, lag):
                return not self.fixed or 0 <= self.n - lag < self.count

            def tile(self, lag):
                return self.n - lag

            def par(self, lag, of=2):
                return (self.q - lag) % of

            def done(self, lag):
                if self.fixed:
                    return self.n - lag + 1
                if lag not in self.kept:
                    self.kept[lag] = self.eng.snap(self.n - lag + 1)
                return self.kept[lag]

            def dma(self, lag):
                return (self.turn + (self.q - lag) // self.unroll + 1) * 16

            def wait(self, name, lag):
                if self.on(lag):
                    self.eng.wait_ge(s[name], self.done(lag))

        A1, A2, B, TT, C1, C2 = range(6)
        STEPS = NT + C2
        HEAD = 8

        def pipeline(eng, step):
            for n in range(HEAD):
                step(Step(eng, n // 2, n % 2))
            with eng.Fori(HEAD // 2, NT // 2) as half:
                for q in range(2):
                    step(Step(eng, half, q))
            for n in range(NT, STEPS):
                step(Step(eng, n // 2, n % 2))

        def row_tiles(eng, step):
            for n in range(4):
                step(Step(eng, 0, n, 4, MT))
            with eng.Fori(1, MT // 4) as turn:
                for q in range(4):
                    step(Step(eng, turn, q, 4, MT))
            for n in range(3):
                step(Step(eng, MT // 4, n, 4, MT))

        def token_tiles(eng, step):
            for q in range(2):
                step(Step(eng, 0, q))
            with eng.Fori(1, NT // 2) as turn:
                for q in range(2):
                    step(Step(eng, turn, q))

        def gate(eng, tick):
            eng.sem_inc(tick, 1)

        block = ctx.enter_context(nc.Block())

        @block.sync
        def _(sp):
            sp.dma_start(w_nat[:, 0, :, :], a["wq"].rearrange("(k p) d -> p k d", p=P)).then_inc(s["fold_in"], 16)
            sp.dma_start(w_nat[:, 1, :, :], a["wk"].rearrange("(k p) d -> p k d", p=P)).then_inc(s["fold_in"], 16)
            for n, name in enumerate(("fq1", "fq2", "fk1", "fk2")):
                sp.dma_start(f_t[:, n, :], a[name]).then_inc(s["fold_in"], 16)
            sp.dma_start(f_b[:], a["fb"]).then_inc(s["fold_in"], 16)
            sp.dma_start(hn_w[:], a["hn_w"]).then_inc(s["fold_in"], 16)
            sp.dma_start(w_o_raw[:], a["woT"].rearrange("(k p) d -> p k d", p=P)).then_inc(s["fold_in"], 16)
            sp.dma_start(w_v[:], a["wvT"].rearrange("(k p) d -> p k d", p=P)).then_inc(s["w_in"], 16)
            sp.dma_start(W_q[:], a["WqT"].rearrange("(k p) d -> p k d", p=P)).then_inc(s["w_in"], 16)
            sp.dma_start(W_kv[:, :, 0, :], a["WkT"].rearrange("(k p) d -> p k d", p=P)).then_inc(s["w_in"], 16)
            sp.dma_start(W_kv[:, :, 1, :], a["WvT"].rearrange("(k p) d -> p k d", p=P)).then_inc(s["w_in"], 16)
            sp.dma_start(W_o[:], a["WoT"].rearrange("(k p) d -> p k d", p=P)).then_inc(s["w_in"], 16)
            sp.dma_start(b_x[:], a["xb"].rearrange("(o n) d -> o n d", o=1).to_broadcast([P, 4, D])).then_inc(s["w_in"], 16)
            sp.dma_start(nw[:], a["nw"].to_broadcast([P, D])).then_inc(s["w_in"], 16)
            sp.dma_start(w_gate[:], a["gateT"].rearrange("(k p) e -> p k e", p=P)).then_inc(s["w_in"], 16)
            sp.dma_start(w_sgu[:, :, 0, :], a["sg"].rearrange("(k p) f -> p k f", p=P)).then_inc(s["w_in"], 16)
            sp.dma_start(w_sgu[:, :, 1, :], a["su"].rearrange("(k p) f -> p k f", p=P)).then_inc(s["w_in"], 16)
            sp.dma_start(w_sd[:], a["sd"]).then_inc(s["w_in"], 16)

            def load_tile(t, par):
                sp.dma_start(x_t[:, par, :], x_d[bass.ds(t * P, P), :]).then_inc(x_in[par], 16)
                sp.dma_start(c_t[:, par, :, :], ctxT_d[:, :, bass.ds(t * P, P)]).then_inc(c_in[par], 16)

            for t in range(2):
                load_tile(t, t)
            sp.wait_ge(s["setup_done"], 1)
            sp.wait_ge(s["fold_done"], 4)
            sp.dma_start(list_d[0:E * CAP, :].rearrange("(p c) o -> p (c o)", p=P), zeros_i[:]).then_inc(s["zero_in"], 16)
            for e in range(0, E, 8):
                sp.dma_start(w13[:, e:e + 8, :, :],
                             a["w13"][e:e + 8].rearrange("e (k p) f -> p e k f", p=P)).then_inc(s["experts_in"], 16)
                sp.dma_start(w2[:, e:e + 8, :], a["w2"][e:e + 8].rearrange("e p d -> p e d")).then_inc(s["experts_in"], 16)

            def step(st):
                if not st.fixed or 2 <= st.n + 1 < NT:
                    st.wait("x1_ok", A2)
                    gate(sp, s["tick"])
                    sp.dma_start(x_t[:, 1 - st.q, :], x_d[bass.ds((st.n + 1) * P, P), :]).then_inc(x_in[1 - st.q], 16)
                if not st.fixed or 2 <= st.n < NT:
                    st.wait("kv_ps", B)
                    gate(sp, s["tick"])
                    sp.dma_start(c_t[:, st.q, :, :], ctxT_d[:, :, bass.ds(st.n * P, P)]).then_inc(c_in[st.q], 16)
                if st.on(C1):
                    st.wait("h_ok", C1)
                    gate(sp, s["tick"])
                    sp.dma_start(h_d[bass.ds(st.tile(C1) * P, P), :], hrow[:, st.par(C1), :]).then_inc(h_out[st.par(C1)], 16)
                if st.on(C2):
                    st.wait("acc_ok", C2)
                    gate(sp, s["tick"])
                    sp.dma_start(acc_d[bass.ds(st.tile(C2) * P, P), :], acc[:, st.par(C2), :]).then_inc(acc_out[st.par(C2)], 16)

            for n in range(HEAD):
                step(Step(sp, n // 2, n % 2))
            with sp.Fori(HEAD // 2, NT // 2 - 1) as half:
                for q in range(2):
                    step(Step(sp, half, q))
            for n in range(NT - 2, STEPS):
                step(Step(sp, n // 2, n % 2))

            sp.wait_ge(sent[0], 16 * TOPK * (NT // 2))
            sp.wait_ge(sent[1], 16 * TOPK * (NT // 2))
            sp.dma_start(list_i[0:ER, :, :], list_d[0:E * CAP, :].rearrange("(c r p) o -> r c (p o)", c=EC, p=P)
                         ).then_inc(s["lists_in"], 16)
            with sp.Fori(0, MT // 2) as half:
                for q in range(2):
                    t = half * 2 + q
                    sp.wait_ge(s["eo_ok"], t + 1)
                    gate(sp, s["tick"])
                    sp.dma_start(eo_d[bass.ds(t * P, P), :], eo[:, q, :]).then_inc(eo_out[q], 16)
            for par in range(2):
                sp.wait_ge(acc_out[par], 16 * (NT // 2))
                sp.dma_start(acc[:, par, :], acc_d[par * P:(par + 1) * P, :]).then_inc(acc_in[par], 16)

            def finish(st):
                sp.wait_ge(s["fin_ok"], st.done(0))
                gate(sp, s["tick"])
                sp.dma_start(out_d[bass.ds(st.n * P, P), :], fin[:, st.q, :]).then_inc(out_done[st.q], 16)
                if not st.fixed:
                    sp.dma_start(acc[:, st.q, :], acc_d[bass.ds((st.n + 2) * P, P), :]).then_inc(acc_in[st.q], 16)

            with sp.Fori(0, NT // 2 - 1) as half:
                for q in range(2):
                    finish(Step(sp, half, q))
            for n in range(NT - 2, NT):
                finish(Step(sp, n // 2, n % 2))
            sp.wait_ge(out_done[0], 16 * (NT // 2))
            sp.wait_ge(out_done[1], 16 * (NT // 2))

        @block.tensor
        def _(pe):
            mm = nc.tensor.matmul

            pe.wait_ge(s["fold_in"], 16 * 9)
            pe.wait_ge(s["c_bd"], 1)
            for n in range(4):
                if n >= 2:
                    pe.wait_ge(s["fold_done"], n - 1)
                bank = S[:, n % 2, :].rearrange("p (k d) -> p k d", k=KC)
                for k in range(KC):
                    for c in range(KC):
                        last = mm(bank[:, k, c * P:(c + 1) * P], w_nat[:, n // 2, c, k * P:(k + 1) * P],
                                  f_bd[:, n, :], start=True, stop=True)
                last.then_inc(s["fold_ps"], 1)
            pe.wait_ge(s["setup_done"], 1)
            pe.wait_ge(s["fold_done"], 4)
            pe.wait_ge(s["w_in"], 16 * 11)

            def flip(bank, src, done):
                for k in range(KC):
                    last = nc.tensor.transpose(bank[:, k * P:(k + 1) * P], src[:, k * P:(k + 1) * P], ident[:])
                last.then_inc(s[done], 1)

            def project(bank, lhs, w, done):
                for k in range(KC):
                    last = mm(bank, lhs[:, k, :], w[:, k], start=(k == 0), stop=(k == KC - 1))
                last.then_inc(s[done], 1)

            def step(st):
                if st.on(C2):
                    st.wait("h_ok", C2)
                    st.wait("acc_ok", C2 + 1)
                    st.wait("x1T_ok", B + 1)
                    flip(TB, hrow[:, st.par(C2), :], "hT_ps")
                if st.on(A2):
                    st.wait("qf_ok", A2)
                    st.wait("kf_ok", A2)
                    st.wait("oT_ok", A2 + 1)
                    st.wait("Q_cp", B + 1)
                    st.wait("pk_ok", C2 + 1)
                    st.wait("v_ok", A1 + 1)
                    st.wait("x1_ok", A2 + 1)
                    for b in range(2):
                        for c in range(KC):
                            for j in range(4):
                                r = slice(32 * j, 32 * j + 32)
                                last = mm(S[:, j, (b * KC + c) * L:(b * KC + c + 1) * L],
                                          kblk[r, c * 2 + b].rearrange("p m l -> p (m l)"), qf[r, c, b * L:(b + 1) * L],
                                          start=True, stop=True)
                    last.then_inc(s["s_ps"], 1)
                if st.on(C2):
                    st.wait("hT_ok", C2)
                    st.wait("kf_ok", A1 + 1)
                    for f in range(2):
                        for k in range(KC):
                            last = mm(KK[:, f * P:(f + 1) * P], w_sgu[:, k, f, :], hT[:, k, :],
                                      start=(k == 0), stop=(k == KC - 1))
                    last.then_inc(s["gu_ps"], 1)
                    project(TB[:, 0:E], hT, w_gate, "lg_ps")
                if st.on(B):
                    pe.wait_ge(c_in[st.par(B)], st.dma(B))
                    st.wait("kv_cp", B + 1)
                    project(TA[:], c_t[:, st.par(B)], W_kv[:].rearrange("p k n d -> p k (n d)"), "kv_ps")
                if st.on(C1):
                    st.wait("att_ok", C1)
                    st.wait("s_ok", A2)
                    st.wait("Q_cp", B + 1)
                    flip(S[:, 1, :], att, "attT_ps")
                if st.on(A1):
                    st.wait("xn_ok", A1)
                    st.wait("s_ok", A2)
                    st.wait("v_ok", A1 + 1)
                    flip(S[:, 2, :], xn, "xT_ps")
                if st.on(B):
                    st.wait("x1n_ok", B)
                    st.wait("topi_ok", C2)
                    flip(TB, x1n, "x1T_ps")
                if st.on(C1):
                    st.wait("attT_ok", C1)
                    st.wait("qf_ok", A1 + 1)
                    project(QQ[:, 0:D], attT, W_o, "Wo_ps")
                if st.on(A2):
                    st.wait("s_ok", A2)
                    st.wait("v_ok", A2)
                    for b in range(2):
                        for c in range(KC):
                            for j in range(4):
                                last = mm(S[32 * j:32 * j + 32, 0, c * P + b * L:c * P + (b + 1) * L],
                                          vblk[:, b, 4 * c + j, :], sm[:, j, b * KC + c, :], start=True, stop=True)
                    last.then_inc(s["o_ps"], 1)
                if st.on(B):
                    st.wait("x1T_ok", B)
                    st.wait("attT_ok", C1)
                    project(S[:, 1, 0:D], x1T, W_q, "Q_ps")
                if st.on(A2):
                    st.wait("osq_ok", A2)
                    mm(S[:, 0, D:2 * D], headmask[:], osq[:], start=True, stop=True).then_inc(s["ms_ps"], 1)
                if st.on(A1):
                    st.wait("xT_ok", A1)
                    st.wait("x2_ok", C1)
                    for n, bank, done in ((0, QQ, "q_ps"), (2, KK, "k_ps")):
                        if n == 2:
                            st.wait("act_ok", C2)
                        for f in range(2):
                            for c in range(KC):
                                for k in range(KC):
                                    last = mm(bank[:, (f * KC + c) * P:(f * KC + c + 1) * P],
                                              w_f[:, n + f, k, c * P:(c + 1) * P], xT[:, k, :],
                                              start=(k == 0), stop=(k == KC - 1))
                        last.then_inc(s[done], 1)
                    project(S[:, 2, 0:D], xT, w_v, "v_ps")
                if st.on(A2):
                    st.wait("oT_ok", A2)
                    project(S[:, 3, 0:D], oT, w_o, "wo_ps")
                if st.on(C2):
                    st.wait("act_ok", C2)
                    st.wait("x1T_ok", B)
                    mm(TB[:, 0:D], act_s[:], w_sd[:], start=True, stop=True).then_inc(s["dn_ps"], 1)
                    st.wait("mask_ok", C2)
                    st.wait("seen_ok", C2 + 1)
                    st.wait("Q_cp", B)
                    mm(S[:, 1, 0:E], before[:], mask_h[:], start=True, stop=False)
                    mm(S[:, 1, 0:E], ones_h[:], seen[:, st.par(C2), :], start=False, stop=True).then_inc(s["pos_ps"], 1)

            pipeline(pe, step)

            pe.wait_ge(s["seen_ok"], NT)
            mm(TA[0:E, 0:1], seen[:, 0, :], ones_h[:, 0:1], start=True, stop=True).then_inc(s["table_ps"], 1)
            pe.wait_ge(s["table_ok"], 1)
            mm(TB[:, 0:E], nt_b[:], e_lt[:], start=True, stop=True)
            for c in range(EC):
                mm(QQ[0:ER, c:c + 1], r_lt[:, c * ER:(c + 1) * ER], nt_c[:], start=True, stop=True)
                last = mm(KK[0:ER, c:c + 1], r_eq[:, c * ER:(c + 1) * ER], nt_c[:], start=True, stop=True)
            last.then_inc(s["table_ps"], 1)
            pe.wait_ge(s["table_ok"], 2)
            pe.wait_ge(s["table_ok"], 3)
            for c in range(EC):
                mm(S[:, 0, 0:MT], list_f[0:ER, c, :], hot[0:ER, c, :], start=(c == 0), stop=(c == EC - 1))
            for c in range(EC):
                last = mm(S[0:2, 1, 0:MT], ecol[0:ER, c, :], hot[0:ER, c, :], start=(c == 0), stop=(c == EC - 1))
            last.then_inc(s["table_ps"], 1)
            pe.wait_ge(s["plan_ok"], 1)
            pe.wait_ge(s["experts_in"], 16 * 2 * (E // 8))

            def expert(st, lag):
                return pe.value_load(eid[0:1, bass.ds(st.tile(lag), 1)], min_val=0, max_val=E - 1)

            def step2(st):
                if st.on(0):
                    pe.wait_ge(g_in[st.par(0, 4)], st.dma(0))
                    st.wait("gx_ok", 2)
                    flip((TA, TB)[st.par(0)], xg[:, st.par(0, 4), :], "gx_ps")
                if st.on(1):
                    e = expert(st, 1)
                    st.wait("gx_ok", 1)
                    st.wait("ag_ok", 3)
                    bank = (QQ, KK)[st.par(1)]
                    for k in range(KC):
                        last = mm(bank[:, 0:D], xgT[:, st.par(1), k, :],
                                  w13[:, bass.ds(e, 1), k, :].rearrange("p o f -> p (o f)"),
                                  start=(k == 0), stop=(k == KC - 1))
                    last.then_inc(s["gg_ps"], 1)
                if st.on(2):
                    st.wait("ag_ok", 2)
                    st.wait("agT_ok", 4)
                    nc.tensor.transpose(S[:, st.par(2), 0:P], ag[:, st.par(2), :], ident[:]).then_inc(s["agT_ps"], 1)
                if st.on(3):
                    e = expert(st, 3)
                    st.wait("agT_ok", 3)
                    st.wait("eo_ok", 5)
                    mm(S[:, 2 + st.par(3), 0:D], agT[:, st.par(3), :],
                       w2[:, bass.ds(e, 1), :].rearrange("p o d -> p (o d)"), start=True, stop=True
                       ).then_inc(s["dn2_ps"], 1)

            row_tiles(pe, step2)

        @block.scalar
        def _(act):
            A_ = nc.scalar.activation
            act.preload_act_table_set("natural_log_exp_and_others")
            for n in range(4):
                act.wait_ge(s["fold_ps"], n + 1)
                nc.scalar.copy(w_f[:, n, :, :], S[:, n % 2, :].rearrange("p (k d) -> p k d", k=KC)
                               ).then_inc(s["fold_done"], 1)
            act.wait_ge(s["setup_done"], 1)

            def copy(dst_, src, done):
                nc.scalar.copy(dst_, src).then_inc(s[done], 1)

            def rsqrt(dst_, src, e, scale, st, ln, done, stage):
                A_(dst_[0], src, ACT.Ln, bias=e, scale=scale).then_inc(s[ln], 1)
                st.wait(ln, stage)
                A_(dst_[1], dst_[0], ACT.Exp, scale=-0.5).then_inc(s[done], 1)

            def tiles(bank):
                return bank.rearrange("p (k t) -> p k t", t=P)

            def step(st):
                if st.on(C2):
                    st.wait("hT_ps", C2)
                    copy(hT[:], tiles(TB[:, 0:D]), "hT_ok")
                if st.on(C2):
                    st.wait("gu_ps", C2)
                    A_(eg[:], KK[:, 0:P], ACT.Exp, scale=-1.0).then_inc(s["eg_ok"], 1)
                    st.wait("eg_ok", C2)
                    A_(gs[:], eg[:], ACT.Ln, bias=ones[:, 0:1]).then_inc(s["lne_ok"], 1)
                    st.wait("lne_ok", C2)
                    A_(eg[:], gs[:], ACT.Exp, scale=-1.0).then_inc(s["sig_ok"], 1)
                if st.on(B):
                    st.wait("kv_ps", B)
                    st.wait("kvb_ok", B + 1)
                    nc.scalar.copy(qkv_raw[:, 1, :], TA[:, 0:D])
                    copy(qkv_raw[:, 2, :].rearrange("p (d h) -> p h d", h=H),
                         TA[:, D:2 * D].rearrange("p (h d) -> p h d", h=H), "kv_cp")
                if st.on(C1):
                    st.wait("attT_ps", C1)
                    copy(attT[:], tiles(S[:, 1, 0:D]), "attT_ok")
                if st.on(A1):
                    st.wait("mv_a_ok", A1)
                    rsqrt((r_a[:, 0:1], r_a[:, 1:2]), mv_a[:, 1:2], eps[:, 0:1], 1.0, st, "ln_a_ok", "r_a_ok", A1)
                if st.on(B):
                    st.wait("mv_b_ok", B)
                    rsqrt((r_b[:, 0:1], r_b[:, 1:2]), mv_b[:, 1:2], eps[:, 0:1], 1.0, st, "ln_b_ok", "r_b_ok", B)
                if st.on(A1):
                    st.wait("xT_ps", A1)
                    copy(xT[:], tiles(S[:, 2, 0:D]), "xT_ok")
                if st.on(B):
                    st.wait("x1T_ps", B)
                    copy(x1T[:], tiles(TB[:, 0:D]), "x1T_ok")
                if st.on(A2):
                    st.wait("o_ps", A2)
                    A_(osq[:], S[:, 0, 0:D], ACT.Square).then_inc(s["osq_ok"], 1)
                if st.on(C2):
                    st.wait("dl_ok", C2)
                    A_(ew[:], dl[:], ACT.Exp, accum_out=es[:]).then_inc(s["ew_ok"], 1)
                if st.on(C1):
                    st.wait("mv_c_ok", C1)
                    rsqrt((r_c[:, 0:1], r_c[:, 1:2]), mv_c[:, 1:2], eps[:, 0:1], 1.0, st, "ln_c_ok", "r_c_ok", C1)
                if st.on(B):
                    st.wait("Q_ps", B)
                    st.wait("qb_ok", B + 1)
                    copy(qkv_raw[:, 0, :], S[:, 1, 0:D], "Q_cp")
                if st.on(A2):
                    st.wait("ms_ps", A2)
                    rsqrt((r_o[:, 0, :], r_o[:, 1, :]), S[:, 0, D:2 * D], eps[:, 0:1], 1.0 / DK, st, "ln_o_ok", "r_o_ok", A2)
                if st.on(C1):
                    st.wait("v2_ok", C1)
                    rsqrt((r2[:, 0:1], r2[:, 1:2]), v2[:], eps[:, 1:2], 1.0, st, "ln_2_ok", "r2_ok", C1)
                if st.on(A1):
                    st.wait("q_ps", A1)
                    st.wait("qf_ok", A1 + 1)
                    A_(tq[:], tiles(QQ[:, D:2 * D]), ACT.Identity, bias=f_b2[:, 0:1], scale=DK ** -0.5).then_inc(s["tq_ok"], 1)
                    st.wait("k_ps", A1)
                    st.wait("kf_ok", A1 + 1)
                    for m_ in range(2):
                        last = A_(tk[:, m_], tiles(KK[:, D:2 * D]), ACT.Identity, bias=f_b2[:, 1 + m_:2 + m_],
                                  scale=parmask[:, m_:m_ + 1])
                    last.then_inc(s["tk_ok"], 1)
                if st.on(TT):
                    st.wait("scm_ok", TT)
                    st.wait("ao_ok", TT + 1)
                    A_(pr[:], scm[:], ACT.Exp).then_inc(s["pr_ok"], 1)
                if st.on(A1):
                    st.wait("v_ps", A1)
                    st.wait("o_ps", A1 + 1)
                    for b in range(2):
                        for h in range(2):
                            last = nc.scalar.copy(
                                vblk[h * L:(h + 1) * L, b, :, h * DK:(h + 1) * DK],
                                S[b * L:(b + 1) * L, 2, 0:D].rearrange("p (g h d) -> p g h d", h=2, d=DK)[:, :, h, :])
                    last.then_inc(s["v_ok"], 1)

            pipeline(act, step)

            act.wait_ge(s["plan_ok"], 1)

            def rows_of(st_n, buf):
                nc.scalar.copy(gcol[:, buf:buf + 1], gidx[:, bass.ds(st_n, 1)]).then_inc(s["gcol_ok"], 1)

            for n in range(3):
                rows_of(n, n)

            def step2(st):
                if st.on(0):
                    st.wait("gx_ps", 0)
                    st.wait("gg_ps", 2)
                    copy(xgT[:, st.par(0)], tiles((TA, TB)[st.par(0)][:, 0:D]), "gx_ok")
                    rows_of(st.n + 3, (st.q + 3) % 4)
                if st.on(1):
                    st.wait("gg_ps", 1)
                    st.wait("ag_ok", 3)
                    A_(sg[:, st.par(1), :], (QQ, KK)[st.par(1)][:, 0:FF], ACT.Silu).then_inc(s["sg_ok"], 1)
                if st.on(2):
                    st.wait("agT_ps", 2)
                    st.wait("dn2_ps", 4)
                    copy(agT[:, st.par(2), :], S[:, st.par(2), 0:P], "agT_ok")

            row_tiles(act, step2)

            act.wait_ge(s["cidx_ok"], 1)

            def step3(st):
                st.wait("fin_ok", 2)
                w_of = lambda ap: ap.rearrange("p o k -> p (o k)")
                nc.scalar.copy(wcol[:, st.par(0), :], w_of(route[:, bass.ds(st.n, 1), 2, :]))
                nc.scalar.copy(ccol[:, st.par(0), :], w_of(cidx[:, bass.ds(st.n, 1), :])).then_inc(s["ccol_ok"], 1)

            token_tiles(act, step3)

        @block.vector
        def _(v):
            tt = nc.vector.tensor_tensor
            ts = nc.vector.tensor_scalar
            stt = nc.vector.scalar_tensor_tensor

            links = [0]

            def link():
                links[0] += 1
                v.wait_ge(s["linked"], links[0])

            v.wait_ge(s["c_setup"], 1)
            v.wait_ge(s["fold_in"], 16 * 9)
            for n in range(4):
                last = tt(f_bd[:, n, :], f_t[:, n, :], headmask[:], ALU.mult)
            last.then_inc(s["c_bd"], 1)
            for k in range(KC):
                ts(w_o[:, k, :], w_o_raw[:, k, :], hn_w[:, 0:1], None, ALU.mult)
            ts(f_b2[:, 0:1], f_b[:, 1:2], DK ** -0.5, None, ALU.mult)
            nc.vector.tensor_reduce(parmask[:, 0:1], evens[:], X, ALU.add).then_inc(s["linked"], 1)
            link()
            ts(parmask[:, 1:2], parmask[:, 0:1], -1.0, 1.0, ALU.mult, ALU.add)
            ts(jend[:], expert_row[:], float(J), float(J), ALU.mult, ALU.add).then_inc(s["linked"], 1)
            link()
            for m_ in range(2):
                tt(f_b2[:, 1 + m_:2 + m_], f_b[:, 3:4], parmask[:, m_:m_ + 1], ALU.mult)
            for c in range(EC):
                last = ts(past[:, c, :], jend[:], rcol[:, c:c + 1], None, ALU.is_le)
            last.then_inc(s["linked"], 1)
            link()
            for n in range(2):
                last = nc.vector.tensor_reduce(ecol[:, :, n], past[:], X, ALU.add)
            last.then_inc(s["linked"], 1)
            link()
            stt(jcol[:], ecol[:, :, 0], -float(J), rcol[:], ALU.mult, ALU.add)
            nc.vector.memset(seen[:, 0, :], 0.0)
            nc.vector.memset(vblk[:], 0.0).then_inc(s["setup_done"], 1)
            v.wait_ge(s["setup_done"], 1)
            v.wait_ge(s["w_in"], 16 * 11)

            def heads(ap):
                return ap.rearrange("p (h d) -> p h d", h=H)

            def step(st):
                at = st.par(TT)

                def k_mult(c):
                    if c == 0:
                        st.wait("ao_ok", TT + 1)
                    if c >= 2:
                        st.wait(f"ks{c - 2}", TT)
                    q_ = qkv[:, at, 0, :].rearrange("p (h o d) -> p h o d", h=H, o=1)[:, c * HC:(c + 1) * HC]
                    k_ = qkv[:, at, 1, :].rearrange("p (o g d) -> p o g d", g=H, o=1)
                    last = tt(prod[:, c % 2, :].rearrange("p (h g d) -> p h g d", h=HC, g=H),
                       q_.to_broadcast([P, HC, H, DK]), k_.to_broadcast([P, HC, H, DK]), ALU.mult)
                    if c:
                        last.then_inc(s[f"kp{c}"], 1)

                def k_sum(c):
                    st.wait(f"kp{max(c, 1)}", TT)
                    last = nc.vector.tensor_reduce(
                        sc[:, c * HC:(c + 1) * HC, :],
                        prod[:, c % 2, :].rearrange("p (h g d) -> p h g d", h=HC, g=H), X, ALU.add)
                    if c != 2:
                        last.then_inc(s["sc_ok" if c == NCH - 1 else f"ks{c}"], 1)

                def v_mult(c):
                    if c == 0:
                        st.wait("sc_ok", TT)
                    if c >= 2:
                        st.wait(f"vs{c - 2}", TT)
                    p_ = pr[:, c * HC:(c + 1) * HC, :].rearrange("p h (o g) -> p h o g", o=1)
                    v_ = qkv[:, at, 2, :].rearrange("p (o d g) -> p o d g", g=H, o=1)
                    last = tt(prod[:, c % 2, :].rearrange("p (h d g) -> p h d g", h=HC, g=H),
                       p_.to_broadcast([P, HC, DK, H]), v_.to_broadcast([P, HC, DK, H]), ALU.mult)
                    if c:
                        last.then_inc(s[f"vp{c}"], 1)

                def v_sum(c):
                    st.wait(f"vp{max(c, 1)}", TT)
                    last = nc.vector.tensor_reduce(
                        ao[:, c * HC:(c + 1) * HC, :],
                        prod[:, c % 2, :].rearrange("p (h d g) -> p h d g", h=HC, g=H), X, ALU.add)
                    if c != 2:
                        last.then_inc(s["ao_ok" if c == NCH - 1 else f"vs{c}"], 1)

                T_ = st.on(TT)
                if st.on(B):
                    st.wait("x1_ok", B)
                    nc.vector.bn_stats(st_b[:], x1[:, st.par(B), :]).then_inc(s["st_b_ok"], 1)
                if st.on(A1):
                    v.wait_ge(x_in[st.par(A1)], st.dma(A1))
                    gate(v, s["tick"])
                    nc.vector.bn_stats(st_a[:], x_t[:, st.par(A1), :]).then_inc(s["st_a_ok"], 1)
                if st.on(B):
                    st.wait("st_b_ok", B)
                    gate(v, s["tick"])
                    nc.vector.bn_aggr(mv_b[:], st_b[:]).then_inc(s["mv_b_ok"], 1)
                if st.on(A1):
                    st.wait("st_a_ok", A1)
                    gate(v, s["tick"])
                    nc.vector.bn_aggr(mv_a[:], st_a[:]).then_inc(s["mv_a_ok"], 1)
                if st.on(C2):
                    st.wait("lg_ps", C2)
                    gate(v, s["tick"])
                    nc.vector.max(top[:], TB[:, 0:E]).then_inc(s["top_ok"], 1)
                if st.on(A2):
                    st.wait("s_ps", A2)
                    st.wait("o_ps", A2 + 1)
                    tt(sm[:].rearrange("p j c l -> p j (c l)"), S[:, :, 0:2 * KC * L],
                       causal4(causal), ALU.mult).then_inc(s["s_ok"], 1)
                if st.on(C2):
                    st.wait("top_ok", C2)
                    gate(v, s["tick"])
                    nc.vector.max_index(topi[:], top[:], TB[:, 0:E]).then_inc(s["topi_ok"], 1)
                    ts(dl[:], top[:, 0:TOPK], top[:, 0:1], None, ALU.subtract).then_inc(s["dl_ok"], 1)
                if T_:
                    st.wait("kvb_ok", TT)
                    st.wait("qb_ok", TT)
                    k_mult(0)
                if st.on(A1):
                    st.wait("r_a_ok", A1)
                    ts(xn[:], x_t[:, st.par(A1), :], mv_a[:, 0:1], r_a[:, 1:2], ALU.subtract, ALU.mult
                       ).then_inc(s["xn_ok"], 1)
                if st.on(B):
                    st.wait("r_b_ok", B)
                    ts(x1n[:], x1[:, st.par(B), :], mv_b[:, 0:1], r_b[:, 1:2], ALU.subtract, ALU.mult
                       ).then_inc(s["x1n_ok"], 1)
                if st.on(C2):
                    st.wait("sig_ok", C2)
                    tt(gs[:], KK[:, 0:P], eg[:], ALU.mult).then_inc(s["gs_ok"], 1)
                    st.wait("gs_ok", C2)
                    tt(act_s[:], KK[:, P:2 * P], gs[:], ALU.mult).then_inc(s["act_ok"], 1)
                    st.wait("topi_ok", C2)
                    nc.vector.tensor_copy(topf[:], topi[:, 0:TOPK]).then_inc(s["topf_ok"], 1)
                if T_:
                    k_mult(1)
                if st.on(C1):
                    st.wait("Wo_ps", C1)
                    st.wait("xb_ok", C1)
                    st.wait("res_ok", C1 + 1)
                    tt(x2[:], xb[:, st.par(C1), :], QQ[:, 0:D], ALU.add).then_inc(s["x2_ok"], 1)
                    st.wait("x2_ok", C1)
                    nc.vector.bn_stats(st_c[:], x2[:]).then_inc(s["st_c_ok"], 1)
                if st.on(C2):
                    st.wait("topf_ok", C2)
                    tt(oh[:], expert_row[:].rearrange("p (o e) -> p o e", o=1).to_broadcast([P, TOPK, E]),
                       topf[:].rearrange("p (k o) -> p k o", o=1).to_broadcast([P, TOPK, E]), ALU.is_equal
                       ).then_inc(s["oh_ok"], 1)
                if T_:
                    k_sum(0)
                if st.on(C1):
                    st.wait("st_c_ok", C1)
                    gate(v, s["tick"])
                    nc.vector.bn_aggr(mv_c[:], st_c[:]).then_inc(s["mv_c_ok"], 1)
                if st.on(C2):
                    st.wait("oh_ok", C2)
                    st.wait("seen_ok", C2 + 1)
                    with nc.allow_low_precision(reason="zeros and ones"):
                        nc.vector.tensor_reduce(mask_h[:], oh[:].rearrange("p k e -> p e k"), X, ALU.add
                                                ).then_inc(s["mask_ok"], 1)
                if T_:
                    k_mult(2)
                    k_sum(1)
                if st.on(C1):
                    st.wait("r_c_ok", C1)
                    stt(v2[:], mv_c[:, 1:2], r_c[:, 1:2], r_c[:, 1:2], ALU.mult, ALU.mult).then_inc(s["v2_ok"], 1)
                    ts(y[:], x2[:], mv_c[:, 0:1], r_c[:, 1:2], ALU.subtract, ALU.mult).then_inc(s["y_ok"], 1)
                if T_:
                    k_mult(3)
                    k_sum(2)
                if st.on(A2):
                    st.wait("r_o_ok", A2)
                    tt(oT[:].rearrange("p k t -> p (k t)"), S[:, 0, 0:D], r_o[:, 1, :], ALU.mult).then_inc(s["oT_ok"], 1)
                if st.on(C1):
                    st.wait("r2_ok", C1)
                    st.wait("y_ok", C1)
                    if st.on(C1 + 2):
                        v.wait_ge(h_out[st.par(C1)], st.dma(C1 + 2))
                    st.wait("hT_ps", C1 + 2)
                    stt(hrow[:, st.par(C1), :], y[:], r2[:, 1:2], nw[:], ALU.mult, ALU.mult).then_inc(s["h_ok"], 1)
                if st.on(C2):
                    st.wait("ew_ok", C2)
                    nc.vector.reciprocal(rs[:], es[:]).then_inc(s["rs_ok"], 1)
                if T_:
                    k_sum(3)
                if st.on(C2):
                    st.wait("dn_ps", C2)
                    st.wait("res_ok", C2)
                    if st.on(C2 + 2):
                        v.wait_ge(acc_out[st.par(C2)], st.dma(C2 + 2))
                    tt(acc[:, st.par(C2), :], res[:, st.par(C2), :], TB[:, 0:D], ALU.add
                       ).then_inc(s["acc_ok"], 1)
                    st.wait("pos_ps", C2)
                    tt(pk[:], oh[:], S[:, 1, 0:E].rearrange("p (o e) -> p o e", o=1).to_broadcast([P, TOPK, E]), ALU.mult
                       ).then_inc(s["pk_ok"], 1)
                    tt(seen[:, 1 - st.par(C2), :], seen[:, st.par(C2), :], mask_h[:], ALU.add).then_inc(s["seen_ok"], 1)
                if T_:
                    st.wait("sc_ok", TT)
                    nc.vector.tensor_reduce(mx[:], sc[:], X, ALU.max).then_inc(s["mx_ok"], 1)
                if st.on(A2):
                    st.wait("wo_ps", A2)
                    st.wait("xb_ok", A2 + 2)
                    tt(x1[:, st.par(A2), :], x_t[:, st.par(A2), :], S[:, 3, 0:D], ALU.add).then_inc(s["x1_ok"], 1)
                if T_:
                    st.wait("mx_ok", TT)
                    tt(scm[:], sc[:], mx[:].rearrange("p (h o) -> p h o", o=1).to_broadcast([P, H, H]), ALU.subtract
                       ).then_inc(s["scm_ok"], 1)
                if st.on(A1):
                    st.wait("tq_ok", A1)
                    st.wait("s_ps", A1 + 1)
                    stt(qf[:], QQ[:, 0:D].rearrange("p (k t) -> p k t", t=P), f_b[:, 0:1], tq[:], ALU.add, ALU.mult
                        ).then_inc(s["qf_ok"], 1)
                if st.on(C2):
                    st.wait("pk_ok", C2)
                    nc.vector.tensor_reduce(pos[:], pk[:], X, ALU.add).then_inc(s["pos_ok"], 1)
                if st.on(A1):
                    st.wait("tk_ok", A1)
                    for m_ in range(2):
                        last = stt(kblk[:, :, m_, :], KK[:, 0:D].rearrange("p (c l) -> p c l", l=L), f_b[:, 2:3],
                                   tk[:, m_].rearrange("p k (b l) -> p (k b) l", l=L), ALU.add, ALU.mult)
                    last.then_inc(s["kf_ok"], 1)
                if st.on(C2):
                    rt = lambda n: route[:, bass.ds(st.tile(C2), 1), n, :].rearrange("p o k -> p (o k)")
                    st.wait("pos_ok", C2)
                    ts(over[:], pos[:], float(CAP), None, ALU.is_ge)
                    stt(row[:], topf[:], float(CAP), pos[:], ALU.mult, ALU.add).then_inc(s["row_ok"], 1)
                    ts(rt(1), pos[:], float(CAP - 1), None, ALU.min)
                    ts(rt(0), topf[:], 1.0, None, ALU.mult)
                    st.wait("row_ok", C2)
                    tt(gap[:], trash_row[:, bass.ds(st.tile(C2), 1), :].rearrange("p o k -> p (o k)"), row[:], ALU.subtract
                       ).then_inc(s["gap_ok"], 1)
                    st.wait("rs_ok", C2)
                    ts(rt(2), ew[:], rs[:, 0:1], None, ALU.mult)
                if T_:
                    st.wait("pr_ok", TT)
                    v_mult(0)
                    v_mult(1)
                if st.on(C2):
                    st.wait("gap_ok", C2)
                    tt(over[:], over[:], gap[:], ALU.mult).then_inc(s["gapo_ok"], 1)
                    if st.on(C2 + 2):
                        v.wait_ge(sent[st.par(C2)], st.dma(C2 + 2) * TOPK)
                        gate(v, s["tick"])
                    nc.vector.tensor_copy(tid[:, st.par(C2):st.par(C2) + 1], tok_id[:, bass.ds(st.tile(C2), 1)])
                    st.wait("gapo_ok", C2)
                    tt(slot[:, st.par(C2), :], row[:], over[:], ALU.add).then_inc(s["slot_ok"], 1)
                if T_:
                    v_sum(0)
                    v_mult(2)
                    v_sum(1)
                    nc.vector.tensor_reduce(psm[:], pr[:], X, ALU.add).then_inc(s["psm_ok"], 1)
                    v_mult(3)
                    v_sum(2)
                    st.wait("psm_ok", TT)
                    nc.vector.reciprocal(pri[:], psm[:]).then_inc(s["pri_ok"], 1)
                    v_sum(3)
                    st.wait("ao_ok", TT)
                    st.wait("pri_ok", TT)
                    st.wait("attT_ps", TT + 1)
                    tt(heads(att[:]), ao[:], pri[:].rearrange("p (h o) -> p h o", o=1).to_broadcast([P, H, DK]), ALU.mult
                       ).then_inc(s["att_ok"], 1)

            def causal4(m_):
                return m_[:].rearrange("p (j c l) -> p j c l", j=1, c=1).to_broadcast([P, 4, 2 * KC, L])

            pipeline(v, step)

            v.wait_ge(s["table_ps"], 1)
            ts(cnt_c[:], TA[0:E, 0:1], float(CAP), None, ALU.min).then_inc(s["linked"], 1)
            link()
            ts(have[:], jrow[:], cnt_c[:, 0:1], None, ALU.is_lt).then_inc(s["linked"], 1)
            link()
            nc.vector.tensor_reduce(nt_c[:], have[:], X, ALU.add).then_inc(s["linked"], 1)
            link()
            nc.vector.tensor_copy(nt_b[:], nt_c[:].to_broadcast([E, P])).then_inc(s["table_ok"], 1)
            v.wait_ge(s["table_ps"], 2)
            nc.vector.tensor_copy(base[:], TB[:, 0:E])
            tt(dst[0:ER, :], jcol[0:ER, :], QQ[0:ER, 0:EC], ALU.add)
            tt(nov[0:ER, :], jcol[0:ER, :], KK[0:ER, 0:EC], ALU.is_ge).then_inc(s["linked"], 1)
            link()
            stt(dstv[0:ER, :], nov[0:ER, :], float(2 * MT), dst[0:ER, :], ALU.mult, ALU.add).then_inc(s["linked"], 1)
            link()
            for c in range(EC):
                last = ts(hot[0:ER, c, :], tcol[0:ER, :], dstv[0:ER, c:c + 1], None, ALU.is_equal)
            last.then_inc(s["table_ok"], 1)
            v.wait_ge(s["lists_in"], 16)
            nc.vector.tensor_copy(list_f[0:ER], list_i[0:ER]).then_inc(s["table_ok"], 1)
            v.wait_ge(s["table_ps"], 3)
            nc.vector.tensor_copy(gidx[:, 0:MT], S[:, 0, 0:MT])
            nc.vector.tensor_copy(eid[:], S[0:2, 1, 0:MT]).then_inc(s["plan_ok"], 1)
            G = NT // 4
            for c in range(4):
                tiles_ = slice(c * G, (c + 1) * G)
                g4 = bk_e[:].rearrange("p (t k) e -> p t k e", k=TOPK)
                e_in = route[:, tiles_, 0, :].rearrange("p t (k o) -> p t k o", o=1).to_broadcast([P, G, TOPK, E])
                tt(g4, expert_row[:].rearrange("p (a b e) -> p a b e", a=1, b=1).to_broadcast([P, G, TOPK, E]),
                   e_in, ALU.is_equal).then_inc(s["linked"], 1)
                link()
                tt(g4, g4, base[:].rearrange("p (a b e) -> p a b e", a=1, b=1).to_broadcast([P, G, TOPK, E]),
                   ALU.mult).then_inc(s["linked"], 1)
                link()
                nc.vector.tensor_reduce(cb[:, tiles_, :], g4, X, ALU.add).then_inc(s["linked"], 1)
                link()
            stt(cidx[:], cb[:], float(P), route[:, :, 1, :], ALU.mult, ALU.add).then_inc(s["cidx_ok"], 1)

            def step2(st):
                if st.on(1):
                    st.wait("sg_ok", 1)
                    st.wait("agT_ps", 3)
                    tt(ag[:, st.par(1), :], (QQ, KK)[st.par(1)][:, FF:2 * FF], sg[:, st.par(1), :], ALU.mult
                       ).then_inc(s["ag_ok"], 1)
                if st.on(3):
                    st.wait("dn2_ps", 3)
                    if st.on(5):
                        v.wait_ge(eo_out[st.par(3)], eo_value(st))
                        gate(v, s["tick"])
                    nc.vector.tensor_copy(eo[:, st.par(3), :], S[:, 2 + st.par(3), 0:D]).then_inc(s["eo_ok"], 1)

            def eo_value(st):
                return (st.turn * 2 + (st.q - 5) // 2 + 1) * 16

            row_tiles(v, step2)

            def step3(st):
                b = st.par(0)
                v.wait_ge(er_in[b], st.dma(0) * TOPK)
                st.wait("ccol_ok", 0)
                if st.on(2):
                    v.wait_ge(out_done[b], st.dma(2))
                v.wait_ge(acc_in[b], st.dma(0))
                stt(part[:, 0, :], er[:, b, 0, :], wcol[:, b, 0:1], acc[:, b, :], ALU.mult, ALU.add).then_inc(s["part_ok"], 1)
                for k in range(1, TOPK):
                    v.wait_ge(s["part_ok"], st.n * (TOPK - 1) + k)
                    to = part[:, k, :] if k < TOPK - 1 else fin[:, b, :]
                    stt(to, er[:, b, k, :], wcol[:, b, k:k + 1], part[:, k - 1, :], ALU.mult, ALU.add
                        ).then_inc(s["part_ok" if k < TOPK - 1 else "fin_ok"], 1)

            token_tiles(v, step3)

        @block.gpsimd
        def _(g):
            gp = nc.gpsimd
            tt = gp.tensor_tensor

            def among(ap, pattern, base, mult, op, fill=0.0):
                gp.affine_select(out=ap, in_=ap, compare_op=op, fill=fill, base=base, pattern=pattern,
                                 channel_multiplier=mult).then_inc(s["c_small"], 1)
                count[0] += 1
                g.wait_ge(s["c_small"], count[0])

            count = [1]
            gp.memset(ones[:], 1.0)
            for ap in (ident[:], causal[:], headmask[:], evens[:], before[:], ones_h[:], e_lt[:], r_lt[:], r_eq[:]):
                gp.memset(ap, 1.0)
            gp.memset(eps[:, 0:1], LN_EPS)
            gp.memset(eps[:, 1:2], RMS_EPS)
            gp.memset(zeros_i[:], 0)
            gp.memset(gidx[:, MT:MT + 4], 0).then_inc(s["c_small"], 1)
            g.wait_ge(s["c_small"], 1)
            among(ident[:], [[-1, P]], 0, 1, ALU.is_equal)
            for b in range(2):
                among(causal[b * L:(b + 1) * L, :], [[1, L]], 0, -1, ALU.is_ge)
            hm = headmask[:].rearrange("p (b j) -> p b j", j=DK)
            among(hm, [[-DK, P // DK], [0, DK]], 0, 1, ALU.is_ge)
            among(hm, [[DK, P // DK], [0, DK]], DK - 1, -1, ALU.is_ge)
            among(evens[:], [[-2 * DK, 4]], 0, 1, ALU.is_ge)
            among(evens[:], [[2 * DK, 4]], DK - 1, -1, ALU.is_ge)
            among(before[:], [[1, P]], 0, -1, ALU.is_gt)
            among(e_lt[:], [[1, E]], 0, -1, ALU.is_gt)
            among(r_lt[:], [[1, EJ]], -J, -J, ALU.is_ge)
            among(r_eq[:], [[1, EJ]], 0, -J, ALU.is_ge)
            among(r_eq[:], [[-1, EJ]], J - 1, J, ALU.is_ge)
            small = dict(allow_small_or_imprecise_dtypes=True)
            gp.iota(expert_row[:], pattern=[[1, E]], base=0, channel_multiplier=0, **small)
            gp.iota(tok_id[:], pattern=[[P, NT]], base=0, channel_multiplier=1)
            gp.iota(trash_row[:], pattern=[[TOPK * P, NT], [P, TOPK]], base=TRASH, channel_multiplier=1, **small)
            gp.iota(jrow[:], pattern=[[P, J]], base=0, channel_multiplier=0, **small)
            gp.iota(tcol[:], pattern=[[1, MT]], base=0, channel_multiplier=0, **small)
            gp.iota(rcol[:], pattern=[[ER, EC]], base=0, channel_multiplier=1, **small).then_inc(s["c_setup"], 1)
            g.wait_ge(s["setup_done"], 1)
            g.wait_ge(s["w_in"], 16 * 11)
            g.wait_ge(s["zero_in"], 16)

            def step(st):
                if st.on(B):
                    st.wait("x1_ok", B)
                    st.wait("x2_ok", C1)
                    tt(xb[:, st.par(B), :], x1[:, st.par(B), :], b_x[:, 3, :], ALU.add).then_inc(s["xb_ok"], 1)
                if st.on(B):
                    st.wait("kv_cp", B)
                    st.wait("att_ok", C1)
                    tt(qkv[:, st.par(B), 1, :], qkv_raw[:, 1, :], b_x[:, 1, :], ALU.add)
                    tt(qkv[:, st.par(B), 2, :].rearrange("p (d h) -> p d h", h=H),
                       qkv_raw[:, 2, :].rearrange("p (d h) -> p d h", h=H),
                       b_x[:, 2, :].rearrange("p (h d) -> p d h", d=DK), ALU.add).then_inc(s["kvb_ok"], 1)
                if st.on(C1):
                    st.wait("y_ok", C1)
                    st.wait("acc_ok", C1 + 2)
                    tt(res[:, st.par(C1), :], x2[:], y[:], ALU.add).then_inc(s["res_ok"], 1)
                if st.on(B):
                    st.wait("Q_cp", B)
                    tt(qkv[:, st.par(B), 0, :], qkv_raw[:, 0, :], b_x[:, 0, :], ALU.add).then_inc(s["qb_ok"], 1)
                if st.on(C2):
                    st.wait("slot_ok", C2)
                    gate(g, s["tick"])
                    for k in range(TOPK):
                        gp.indirect_dma_start(
                            out=list_d, out_offset=bass.IndirectOffsetOnAxis(ap=slot[:, st.par(C2), k:k + 1], axis=0),
                            in_=tid[:, st.par(C2):st.par(C2) + 1], in_offset=None).then_inc(sent[st.par(C2)], 16)

            pipeline(g, step)

            for par in range(2):
                g.wait_ge(h_out[par], 16 * (NT // 2))

            def gather(st):
                if st.on(0):
                    st.wait("gcol_ok", 0)
                    st.wait("gx_ps", 4)
                    gate(g, s["tick"])
                    gp.indirect_dma_start(
                        out=xg[:, st.par(0, 4), :], out_offset=None, in_=h_d,
                        in_offset=bass.IndirectOffsetOnAxis(ap=gcol[:, st.par(0, 4):st.par(0, 4) + 1], axis=0)
                    ).then_inc(g_in[st.par(0, 4)], 16)

            row_tiles(g, gather)

            for par in range(2):
                g.wait_ge(eo_out[par], 16 * (MT // 2))

            def fetch(st):
                st.wait("ccol_ok", 0)
                st.wait("fin_ok", 2)
                gate(g, s["tick"])
                for k in range(TOPK):
                    gp.indirect_dma_start(
                        out=er[:, st.par(0), k, :], out_offset=None, in_=eo_d,
                        in_offset=bass.IndirectOffsetOnAxis(ap=ccol[:, st.par(0), k:k + 1], axis=0)
                    ).then_inc(er_in[st.par(0)], 16)

            token_tiles(g, fetch)


_IN = {
    "x": lambda i: i["x"], "ctxT": lambda i: _flat(i["ctx_2048"]).T,
    "wq": lambda i: i["L0_attn_wq"], "wk": lambda i: i["L0_attn_wk"],
    "wvT": lambda i: i["L0_attn_wv"].T, "woT": lambda i: i["L0_attn_wo"].T,
    "fq1": lambda i: _tile(i["L0_attn_fq1_w"].T, (8, 8)), "fq2": lambda i: _tile(i["L0_attn_fq2_w"].T, (8, 8)),
    "fk1": lambda i: _tile(i["L0_attn_fk1_w"].T, (8, 8)), "fk2": lambda i: _tile(i["L0_attn_fk2_w"].T, (8, 8)),
    "fb": lambda i: _tile(_stack([i["L0_attn_fq1_b"], i["L0_attn_fq2_b"], i["L0_attn_fk1_b"], i["L0_attn_fk2_b"]]).T, (8, 1)),
    "hn_w": lambda i: _tile(i["L0_attn_norm_w"].reshape(-1, 1), (8, 1)),
    "WqT": lambda i: i["L0_xattn_Wq"].T, "WkT": lambda i: i["L0_xattn_Wk"].T,
    "WvT": lambda i: i["L0_xattn_Wv"].T, "WoT": lambda i: i["L0_xattn_Wo"].T,
    "xb": lambda i: _stack([i["L0_xattn_bq"], i["L0_xattn_bk"], i["L0_xattn_bv"], i["L0_xattn_bo"]]),
    "nw": lambda i: i["L0_ffn_norm_w"].reshape(1, -1), "gateT": lambda i: i["L0_ffn_gate_w"].T,
    "w13": lambda i: i["L0_ffn_w13"], "w2": lambda i: i["L0_ffn_w2"],
    "sg": lambda i: i["L0_ffn_shared_gate_w"], "su": lambda i: i["L0_ffn_shared_up_w"],
    "sd": lambda i: i["L0_ffn_shared_down_w"],
}


def _flat(a):
    return a.reshape(-1, a.shape[-1])


def _tile(a, n):
    import numpy as np
    return np.tile(a, n)


def _stack(a):
    import numpy as np
    return np.stack(a)


def kernel(**inputs):
    import numpy as np
    import concourse.bacc as bacc
    from concourse.bass_utils import run_bass_kernel_spmd

    host = {k: np.asarray(v) for k, v in inputs.items()}
    nc = bacc.Bacc("TRN2", target_bir_lowering=False, num_devices=1)
    arrays, aps = {}, {}
    for name, lay in _IN.items():
        arrays[f"in_{name}"] = np.ascontiguousarray(lay(host))
        arr = arrays[f"in_{name}"]
        aps[name] = nc.dram_tensor(f"in_{name}", arr.shape, mybir.dt.from_np(arr.dtype), kind="ExternalInput").ap()
    out = nc.dram_tensor("out", host["x"].shape, F32, kind="ExternalOutput").ap()
    decoder_layer_kernel(nc, aps, out)
    return run_bass_kernel_spmd(nc, [arrays], core_ids=[0]).results[0]["out"]
```

```python
from contextlib import ExitStack

import concourse.bass as bass
from concourse import mybir

F32 = mybir.dt.float32
BF16 = mybir.dt.bfloat16
I32 = mybir.dt.int32
U32 = mybir.dt.uint32
ALU = mybir.AluOpType
ACT = mybir.ActivationFunctionType
X = mybir.AxisListType.X

P = 128
L = 64
D = 256
H = 16
DK = D // H
KC = D // P
E = 32
TOPK = 4
FF = 128
NCH = 4
HC = H // NCH
LN_EPS = 1e-5
RMS_EPS = 1e-6
HEAD_EPS = 1e-5


def decoder_layer_kernel(nc, a, out):
    NB, _, _ = a["x"].shape
    T = NB * L
    NT = T // P
    CAP = TOPK * T * 2 // E
    J = (CAP + P - 1) // P
    EJ = E * J
    EC = (EJ + P - 1) // P
    ER = min(EJ, P)
    MT = min(EJ, (TOPK * T + E * (P - 1)) // P)
    MT += -MT % 4
    TRASH = E * CAP
    assert NT >= 10 and NT % 4 == 0 and CAP % P == 0 and EJ % ER == 0

    x_d = a["x"].rearrange("b l d -> (b l) d")
    out_d = out.rearrange("b l d -> (b l) d")
    ctxT_d = a["ctxT"].rearrange("(k p) t -> p k t", p=P)
    h_d = nc.dram_tensor("h_rows", (T, D), F32, kind="Internal").ap()
    list_d = nc.dram_tensor("token_lists", (E * CAP + TOPK * T, 1), I32, kind="Internal").ap()
    acc_d = nc.dram_tensor("acc_rows", (T, D), F32, kind="Internal").ap()
    eo_d = nc.dram_tensor("expert_rows", (MT * P, D), F32, kind="Internal").ap()

    with ExitStack() as ctx:
        def sb(name, shape, dt=F32):
            return ctx.enter_context(nc.sbuf_tensor(name, shape, dt))

        def ps(name, shape, dt=F32):
            return ctx.enter_context(nc.psum_tensor(name, shape, dt))

        def sem(name):
            return ctx.enter_context(nc.semaphore(name))

        ident = sb("ident", [P, P])
        ones = sb("ones", [P, P])
        causal = sb("causal", [P, L])
        headmask = sb("headmask", [P, P])
        evens = sb("evens", [P, 4])
        parmask = sb("parmask", [P, 2])
        before = sb("before", [P, P], BF16)
        ones_h = sb("ones_h", [P, P], BF16)
        expert_row = sb("expert_row", [P, E])
        eps = sb("eps", [P, 2])
        tok_id = sb("tok_id", [P, NT], I32)
        trash_row = sb("trash_row", [P, NT, TOPK])
        zeros_i = sb("zeros_i", [P, (E * CAP + P - 1) // P], I32)
        w_f = sb("w_f", [P, 4, KC, D])
        f_b = sb("f_b", [P, 4])
        f_b2 = sb("f_b2", [P, 1])
        hn_w = sb("hn_w", [P, 1])
        w_v = sb("w_v", [P, KC, D])
        w_o = sb("w_o", [P, KC, D])
        W_q = sb("W_q", [P, KC, D])
        W_kv = sb("W_kv", [P, KC, 2, D])
        W_o = sb("W_o", [P, KC, D])
        b_x = sb("b_x", [P, 4, D])
        nw = sb("nw", [P, D])
        w_gate = sb("w_gate", [P, KC, E])
        w_sgu = sb("w_sgu", [P, KC, 2, FF])
        w_sd = sb("w_sd", [P, D])
        w13 = sb("w13", [P, E, KC, 2 * FF])
        w2 = sb("w2", [P, E, D])

        x_t = sb("x_t", [P, 2, D])
        st_a = sb("st_a", [P, 6])
        mv_a = sb("mv_a", [P, 2])
        r_a = sb("r_a", [P, 2])
        xn = sb("xn", [P, D])
        xT = sb("xT", [P, KC, P])
        tq = sb("tq", [P, KC, P])
        tk = sb("tk", [P, KC, P])
        kf = sb("kf", [P, KC, P])
        qf = sb("qf", [P, KC, P])
        kblk = sb("kblk", [P, KC * 2, 2, L])
        vblk = sb("vblk", [P, 2, H // 2, 2 * DK])
        sm = sb("sm", [P, 4, 2 * KC, L])
        osq = sb("osq", [P, D])
        r_o = sb("r_o", [P, D])
        oT = sb("oT", [P, KC, P])
        x1 = sb("x1", [P, 2, D])
        st_b = sb("st_b", [P, 6])
        mv_b = sb("mv_b", [P, 2])
        r_b = sb("r_b", [P, 2])
        x1n = sb("x1n", [P, D])
        x1T = sb("x1T", [P, KC, P])
        c_t = sb("c_t", [P, 2, KC, P])
        qkv_raw = sb("qkv_raw", [P, 3, D])
        qkv = sb("qkv", [P, 2, 3, D])
        xb = sb("xb", [P, 2, D])
        prod = sb("prod", [P, NCH, HC * H * DK])
        sc = sb("sc", [P, H, H])
        mx = sb("mx", [P, H])
        scm = sb("scm", [P, H, H])
        pr = sb("pr", [P, H, H])
        psm = sb("psm", [P, H])
        pri = sb("pri", [P, H])
        ao = sb("ao", [P, H, DK])
        att = sb("att", [P, D])
        attT = sb("attT", [P, KC, P])
        x2 = sb("x2", [P, D])
        st_c = sb("st_c", [P, 6])
        mv_c = sb("mv_c", [P, 2])
        r_c = sb("r_c", [P, 2])
        v2 = sb("v2", [P, 1])
        r2 = sb("r2", [P, 2])
        y = sb("y", [P, D])
        hrow = sb("hrow", [P, 2, D])
        res = sb("res", [P, 2, D])
        hT = sb("hT", [P, KC, P])
        eg = sb("eg", [P, P])
        gs = sb("gs", [P, P])
        act_s = sb("act_s", [P, P])
        top = sb("top", [P, 8])
        topi = sb("topi", [P, 8], U32)
        topf = sb("topf", [P, TOPK])
        dl = sb("dl", [P, TOPK])
        ew = sb("ew", [P, TOPK])
        es = sb("es", [P, 1])
        rs = sb("rs", [P, 1])
        oh = sb("oh", [P, TOPK, E])
        mask_h = sb("mask_h", [P, E], BF16)
        seen = sb("seen", [P, 2, E], BF16)
        pk = sb("pk", [P, TOPK, E])
        pos = sb("pos", [P, TOPK])
        over = sb("over", [P, TOPK])
        row = sb("row", [P, TOPK])
        gap = sb("gap", [P, TOPK])
        slot = sb("slot", [P, 2, TOPK], U32)
        tid = sb("tid", [P, 2], I32)
        route = sb("route", [P, NT, 3, TOPK])
        acc = sb("acc", [P, 2, D])
        cnt_c = sb("cnt_c", [E, 1])
        jrow = sb("jrow", [E, J])
        have = sb("have", [E, J])
        nt_c = sb("nt_c", [E, 1])
        nt_b = sb("nt_b", [E, P])
        e_lt = sb("e_lt", [E, E])
        r_lt = sb("r_lt", [E, EJ])
        r_eq = sb("r_eq", [E, EJ])
        rcol = sb("rcol", [P, EC])
        past = sb("past", [P, EC, E])
        jend = sb("jend", [P, E])
        ecol = sb("ecol", [P, EC, 2])
        jcol = sb("jcol", [P, EC])
        base = sb("base", [P, E])
        dst = sb("dst", [P, EC])
        nov = sb("nov", [P, EC])
        dstv = sb("dstv", [P, EC])
        tcol = sb("tcol", [P, MT])
        gidx = sb("gidx", [P, MT + 4], U32)
        eid = sb("eid", [2, MT + 2], I32)
        gcol = sb("gcol", [P, 4], U32)
        cidx = sb("cidx", [P, NT, TOPK], U32)
        ccol = sb("ccol", [P, 2, TOPK], U32)
        wcol = sb("wcol", [P, 2, TOPK])

        early = w13[:].rearrange("p e k f -> p (e k f)")
        w_nat = early[:, 0:2 * KC * D].rearrange("p (n k d) -> p n k d", n=2, k=KC)
        early = early[:, 2 * KC * D:]
        w_o_raw = early[:, 0:KC * D].rearrange("p (k d) -> p k d", k=KC)
        early = early[:, KC * D:]
        f_t = early[:, 0:4 * P].rearrange("p (n m) -> p n m", n=4)
        f_bd = early[:, 4 * P:8 * P].rearrange("p (n m) -> p n m", n=4)
        list_f = prod[:, 2, 0:EC * P].rearrange("p (c l) -> p c l", c=EC)
        list_i = prod[:, 1, 0:EC * P].rearrange("p (c l) -> p c l", c=EC).bitcast(I32)
        cb = prod[:, 0, 0:NT * TOPK].rearrange("p (t k) -> p t k", k=TOPK)
        hot = prod[:, 2, EC * P:EC * (P + MT)].rearrange("p (c t) -> p c t", c=EC)
        sg = prod[:, 3, 0:2 * FF].rearrange("p (b f) -> p b f", b=2)
        ag = prod[:, 3, 2 * FF:4 * FF].rearrange("p (b f) -> p b f", b=2)
        agT = prod[:, 3, 4 * FF:4 * FF + 2 * P].rearrange("p (b t) -> p b t", b=2)
        er = prod[:, 0:2].rearrange("p b (k d) -> p b k d", k=TOPK)
        part = sm[:].rearrange("p j c l -> p (j c l)").rearrange("p (k d) -> p k d", k=4)
        fin = x1
        xg = qkv[:].rearrange("p b n d -> p (b n) d")
        xgT = kblk[:].rearrange("p c m l -> p (c m l)").rearrange("p (n k t) -> p n k t", n=2, k=KC)
        eo = xb
        bk_e = W_kv[:].rearrange("p k n d -> p (k n d)")[:, 0:NT * TOPK // 4 * E].rearrange("p (t e) -> p t e", e=E)

        TA = ps("TA", [P, 512])
        TB = ps("TB", [P, 512])
        QQ = ps("QQ", [P, 512])
        KK = ps("KK", [P, 512])
        S = ps("S", [P, 4, 512])

        names = """w_in fold_in zero_in experts_in c_setup c_bd fold_ps fold_done setup_done
            st_a_ok mv_a_ok ln_a_ok r_a_ok xn_ok xT_ps xT_ok q_ps k_ps v_ps tq_ok tk_ok v_ok qf_ok kp_ok kf_ok s_ps s_ok
            o_ps osq_ok ms_ps ln_o_ok r_o_ok oT_ok wo_ps x1_ok
            st_b_ok mv_b_ok ln_b_ok r_b_ok x1n_ok x1T_ps x1T_ok kv_ps kv_cp Q_ps Q_cp kvb_ok qb_ok xb_ok
            kp0 kp1 kp2 kp3 sc_ok mx_ok scm_ok pr_ok psm_ok pri_ok vp0 vp1 vp2 vp3 ao_ok att_ok
            attT_ps attT_ok Wo_ps x2_ok st_c_ok mv_c_ok ln_c_ok r_c_ok y_ok v2_ok ln_2_ok r2_ok h_ok res_ok
            hT_ps hT_ok gu_ps eg_ok lne_ok sig_ok gs_ok act_ok top_ok topi_ok dl_ok ew_ok rs_ok
            topf_ok oh_ok mask_ok seen_ok dn_ps acc_ok pos_ps pk_ok pos_ok row_ok gap_ok gapo_ok slot_ok
            tick lists_in c_small
            table_ps table_ok linked plan_ok
            gcol_ok gx_ps gx_ok gg_ps sg_ok ag_ok agT_ps agT_ok dn2_ps eo_ok
            cidx_ok ccol_ok part_ok fin_ok""".split()
        s = {n: sem(n) for n in names}
        x_in = [sem("x_in0"), sem("x_in1")]
        c_in = [sem("c_in0"), sem("c_in1")]
        h_out = [sem("h_out0"), sem("h_out1")]
        acc_out = [sem("acc_out0"), sem("acc_out1")]
        acc_in = [sem("acc_in0"), sem("acc_in1")]
        sent = [sem("sent0"), sem("sent1")]
        g_in = [sem(f"g_in{n}") for n in range(4)]
        eo_out = [sem("eo_out0"), sem("eo_out1")]
        er_in = [sem("er_in0"), sem("er_in1")]
        out_done = [sem("out_done0"), sem("out_done1")]

        class Step:

            def __init__(self, eng, turn, q, unroll=2, count=NT):
                self.eng, self.turn, self.q, self.unroll, self.count = eng, turn, q, unroll, count
                self.n = turn * unroll + q
                self.fixed = isinstance(turn, int)
                self.kept = {}

            def on(self, lag):
                return not self.fixed or 0 <= self.n - lag < self.count

            def tile(self, lag):
                return self.n - lag

            def par(self, lag, of=2):
                return (self.q - lag) % of

            def done(self, lag):
                if self.fixed:
                    return self.n - lag + 1
                if lag not in self.kept:
                    self.kept[lag] = self.eng.snap(self.n - lag + 1)
                return self.kept[lag]

            def dma(self, lag, of=2):
                return (self.turn * (self.unroll // of) + (self.q - lag) // of + 1) * 16

            def wait(self, name, lag):
                if self.on(lag):
                    self.eng.wait_ge(s[name], self.done(lag))

        A0, A1, A2, B, TT, C1, C2 = range(7)
        GP_K, GP_V = (2, 3), (2, 3)
        STEPS = NT + C2
        HEAD = 8

        def pipeline(eng, step):
            for n in range(HEAD):
                step(Step(eng, n // 2, n % 2))
            with eng.Fori(HEAD // 2, NT // 2) as half:
                for q in range(2):
                    step(Step(eng, half, q))
            for n in range(NT, STEPS):
                step(Step(eng, n // 2, n % 2))

        UNROLL = 8

        def row_tiles(eng, step):
            for n in range(UNROLL):
                step(Step(eng, 0, n, UNROLL, MT))
            with eng.Fori(1, MT // UNROLL) as turn:
                for q in range(UNROLL):
                    step(Step(eng, turn, q, UNROLL, MT))
            for n in range(3):
                step(Step(eng, MT // UNROLL, n, UNROLL, MT))

        def token_tiles(eng, step):
            for q in range(2):
                step(Step(eng, 0, q))
            with eng.Fori(1, NT // 2) as turn:
                for q in range(2):
                    step(Step(eng, turn, q))

        def gate(eng, tick):
            eng.sem_inc(tick, 1)

        block = ctx.enter_context(nc.Block())

        @block.sync
        def _(sp):
            sp.dma_start(w_nat[:, 0, :, :], a["wq"].rearrange("(k p) d -> p k d", p=P)).then_inc(s["fold_in"], 16)
            sp.dma_start(w_nat[:, 1, :, :], a["wk"].rearrange("(k p) d -> p k d", p=P)).then_inc(s["fold_in"], 16)
            for n, name in enumerate(("fq1", "fq2", "fk1", "fk2")):
                sp.dma_start(f_t[:, n, :], a[name]).then_inc(s["fold_in"], 16)
            sp.dma_start(f_b[:], a["fb"]).then_inc(s["fold_in"], 16)
            sp.dma_start(hn_w[:], a["hn_w"]).then_inc(s["fold_in"], 16)
            sp.dma_start(w_o_raw[:], a["woT"].rearrange("(k p) d -> p k d", p=P)).then_inc(s["fold_in"], 16)
            sp.dma_start(w_v[:], a["wvT"].rearrange("(k p) d -> p k d", p=P)).then_inc(s["w_in"], 16)
            sp.dma_start(W_q[:], a["WqT"].rearrange("(k p) d -> p k d", p=P)).then_inc(s["w_in"], 16)
            sp.dma_start(W_kv[:, :, 0, :], a["WkT"].rearrange("(k p) d -> p k d", p=P)).then_inc(s["w_in"], 16)
            sp.dma_start(W_kv[:, :, 1, :], a["WvT"].rearrange("(k p) d -> p k d", p=P)).then_inc(s["w_in"], 16)
            sp.dma_start(W_o[:], a["WoT"].rearrange("(k p) d -> p k d", p=P)).then_inc(s["w_in"], 16)
            sp.dma_start(b_x[:], a["xb"].rearrange("(o n) d -> o n d", o=1).to_broadcast([P, 4, D])).then_inc(s["w_in"], 16)
            sp.dma_start(nw[:], a["nw"].to_broadcast([P, D])).then_inc(s["w_in"], 16)
            sp.dma_start(w_gate[:], a["gateT"].rearrange("(k p) e -> p k e", p=P)).then_inc(s["w_in"], 16)
            sp.dma_start(w_sgu[:, :, 0, :], a["sg"].rearrange("(k p) f -> p k f", p=P)).then_inc(s["w_in"], 16)
            sp.dma_start(w_sgu[:, :, 1, :], a["su"].rearrange("(k p) f -> p k f", p=P)).then_inc(s["w_in"], 16)
            sp.dma_start(w_sd[:], a["sd"]).then_inc(s["w_in"], 16)

            def load_tile(t, par):
                sp.dma_start(x_t[:, par, :], x_d[bass.ds(t * P, P), :]).then_inc(x_in[par], 16)
                sp.dma_start(c_t[:, par, :, :], ctxT_d[:, :, bass.ds(t * P, P)]).then_inc(c_in[par], 16)

            for t in range(2):
                load_tile(t, t)
            sp.wait_ge(s["setup_done"], 1)
            sp.wait_ge(s["fold_done"], 4)
            sp.dma_start(list_d[0:E * CAP, :].rearrange("(p c) o -> p (c o)", p=P), zeros_i[:]).then_inc(s["zero_in"], 16)
            for e in range(0, E, 8):
                sp.dma_start(w13[:, e:e + 8, :, :],
                             a["w13"][e:e + 8].rearrange("e (k p) f -> p e k f", p=P)).then_inc(s["experts_in"], 16)
                sp.dma_start(w2[:, e:e + 8, :], a["w2"][e:e + 8].rearrange("e p d -> p e d")).then_inc(s["experts_in"], 16)

            def step(st):
                if not st.fixed or 2 <= st.n < NT:
                    st.wait("x1_ok", A2)
                    gate(sp, s["tick"])
                    sp.dma_start(x_t[:, st.q, :], x_d[bass.ds(st.n * P, P), :]).then_inc(x_in[st.q], 16)
                if not st.fixed or 2 <= st.n < NT:
                    st.wait("kv_ps", A2)
                    gate(sp, s["tick"])
                    sp.dma_start(c_t[:, st.q, :, :], ctxT_d[:, :, bass.ds(st.n * P, P)]).then_inc(c_in[st.q], 16)
                if st.on(C1):
                    st.wait("h_ok", C1)
                    gate(sp, s["tick"])
                    sp.dma_start(h_d[bass.ds(st.tile(C1) * P, P), :], hrow[:, st.par(C1), :]).then_inc(h_out[st.par(C1)], 16)
                if st.on(C2):
                    st.wait("acc_ok", C2)
                    gate(sp, s["tick"])
                    sp.dma_start(acc_d[bass.ds(st.tile(C2) * P, P), :], acc[:, st.par(C2), :]).then_inc(acc_out[st.par(C2)], 16)

            pipeline(sp, step)

            sp.wait_ge(sent[0], 16 * TOPK * (NT // 2))
            sp.wait_ge(sent[1], 16 * TOPK * (NT // 2))
            sp.dma_start(list_i[0:ER, :, :], list_d[0:E * CAP, :].rearrange("(c r p) o -> r c (p o)", c=EC, p=P)
                         ).then_inc(s["lists_in"], 16)
            with sp.Fori(0, MT // 2) as half:
                for q in range(2):
                    t = half * 2 + q
                    sp.wait_ge(s["eo_ok"], t + 1)
                    gate(sp, s["tick"])
                    sp.dma_start(eo_d[bass.ds(t * P, P), :], eo[:, q, :]).then_inc(eo_out[q], 16)
            for par in range(2):
                sp.wait_ge(acc_out[par], 16 * (NT // 2))
                sp.dma_start(acc[:, par, :], acc_d[par * P:(par + 1) * P, :]).then_inc(acc_in[par], 16)

            def finish(st):
                sp.wait_ge(s["fin_ok"], st.done(0))
                gate(sp, s["tick"])
                sp.dma_start(out_d[bass.ds(st.n * P, P), :], fin[:, st.q, :]).then_inc(out_done[st.q], 16)
                if not st.fixed:
                    sp.dma_start(acc[:, st.q, :], acc_d[bass.ds((st.n + 2) * P, P), :]).then_inc(acc_in[st.q], 16)

            with sp.Fori(0, NT // 2 - 1) as half:
                for q in range(2):
                    finish(Step(sp, half, q))
            for n in range(NT - 2, NT):
                finish(Step(sp, n // 2, n % 2))
            sp.wait_ge(out_done[0], 16 * (NT // 2))
            sp.wait_ge(out_done[1], 16 * (NT // 2))

        @block.tensor
        def _(pe):
            mm = nc.tensor.matmul

            pe.wait_ge(s["fold_in"], 16 * 9)
            pe.wait_ge(s["c_bd"], 1)
            for n in range(4):
                if n >= 2:
                    pe.wait_ge(s["fold_done"], n - 1)
                bank = S[:, n % 2, :].rearrange("p (k d) -> p k d", k=KC)
                for k in range(KC):
                    for c in range(KC):
                        last = mm(bank[:, k, c * P:(c + 1) * P], w_nat[:, n // 2, c, k * P:(k + 1) * P],
                                  f_bd[:, n, :], start=True, stop=True)
                last.then_inc(s["fold_ps"], 1)
            pe.wait_ge(s["setup_done"], 1)
            pe.wait_ge(s["fold_done"], 4)
            pe.wait_ge(s["w_in"], 16 * 11)

            def flip(bank, src, done):
                for k in range(KC):
                    last = nc.tensor.transpose(bank[:, k * P:(k + 1) * P], src[:, k * P:(k + 1) * P], ident[:])
                last.then_inc(s[done], 1)

            def project(bank, lhs, w, done):
                for k in range(KC):
                    last = mm(bank, lhs[:, k, :], w[:, k], start=(k == 0), stop=(k == KC - 1))
                last.then_inc(s[done], 1)

            def step(st):
                if st.on(A1):
                    st.wait("xT_ok", A1)
                    for n, bank, done in ((0, QQ, "q_ps"), (2, KK, "k_ps")):
                        if n == 2:
                            st.wait("kp_ok", A1 + 1)
                        for f in range(2):
                            for c in range(KC):
                                for k in range(KC):
                                    last = mm(bank[:, (f * KC + c) * P:(f * KC + c + 1) * P],
                                              w_f[:, n + f, k, c * P:(c + 1) * P], xT[:, k, :],
                                              start=(k == 0), stop=(k == KC - 1))
                        last.then_inc(s[done], 1)
                if st.on(C1):
                    st.wait("att_ok", C1)
                    st.wait("s_ok", A2)
                    st.wait("Q_cp", B + 1)
                    flip(S[:, 1, :], att, "attT_ps")
                if st.on(B):
                    st.wait("x1n_ok", B)
                    st.wait("topi_ok", C2)
                    st.wait("act_ok", C2)
                    flip(TB, x1n, "x1T_ps")
                if st.on(C1):
                    st.wait("attT_ok", C1)
                    st.wait("s_ok", A2)
                    st.wait("v_ok", A1 + 1)
                    project(S[:, 2, 0:D], attT, W_o, "Wo_ps")
                if st.on(A2):
                    st.wait("oT_ok", A2)
                    project(S[:, 3, 0:D], oT, w_o, "wo_ps")
                if st.on(B):
                    st.wait("x1T_ok", B)
                    st.wait("attT_ok", C1)
                    project(S[:, 1, 0:D], x1T, W_q, "Q_ps")
                if st.on(A1):
                    st.wait("x2_ok", C1)
                    st.wait("s_ok", A2)
                    project(S[:, 2, 0:D], xT, w_v, "v_ps")
                if st.on(C2):
                    st.wait("act_ok", C2)
                    st.wait("x1T_ok", B)
                    mm(TB[:, 0:D], act_s[:], w_sd[:], start=True, stop=True).then_inc(s["dn_ps"], 1)
                    st.wait("mask_ok", C2)
                    st.wait("seen_ok", C2 + 1)
                    st.wait("Q_cp", B)
                    mm(S[:, 1, 0:E], before[:], mask_h[:], start=True, stop=False)
                    mm(S[:, 1, 0:E], ones_h[:], seen[:, st.par(C2), :], start=False, stop=True).then_inc(s["pos_ps"], 1)
                if st.on(A2):
                    pe.wait_ge(c_in[st.par(A2)], st.dma(A2))
                    st.wait("kv_cp", B)
                    project(TA[:], c_t[:, st.par(A2)], W_kv[:].rearrange("p k n d -> p k (n d)"), "kv_ps")
                if st.on(A1):
                    st.wait("qf_ok", A1)
                    st.wait("kf_ok", A1)
                    st.wait("oT_ok", A2)
                    st.wait("Q_cp", B)
                    st.wait("pk_ok", C2)
                    st.wait("v_ok", A1)
                    st.wait("x1_ok", A2)
                    for b in range(2):
                        for c in range(KC):
                            for j in range(4):
                                r = slice(32 * j, 32 * j + 32)
                                last = mm(S[:, j, (b * KC + c) * L:(b * KC + c + 1) * L],
                                          kblk[r, c * 2 + b].rearrange("p m l -> p (m l)"), qf[r, c, b * L:(b + 1) * L],
                                          start=True, stop=True)
                    last.then_inc(s["s_ps"], 1)
                if st.on(C1):
                    st.wait("h_ok", C1)
                    st.wait("acc_ok", C2)
                    st.wait("x1T_ok", B)
                    flip(TB, hrow[:, st.par(C1), :], "hT_ps")
                if st.on(A0):
                    st.wait("xn_ok", A0)
                    st.wait("qf_ok", A1)
                    flip(QQ, xn, "xT_ps")
                if st.on(C1):
                    st.wait("hT_ok", C1)
                    for f in range(2):
                        for k in range(KC):
                            mm(TB[:, f * P:(f + 1) * P], w_sgu[:, k, f, :], hT[:, k, :],
                               start=(k == 0), stop=(k == KC - 1))
                    project(TB[:, D:D + E], hT, w_gate, "gu_ps")
                if st.on(A1):
                    st.wait("oT_ok", A2)
                    st.wait("s_ok", A1)
                    st.wait("v_ok", A1)
                    for b in range(2):
                        for c in range(KC):
                            for j in range(4):
                                last = mm(S[32 * j:32 * j + 32, 0, c * P + b * L:c * P + (b + 1) * L],
                                          vblk[:, b, 4 * c + j, :], sm[:, j, b * KC + c, :], start=True, stop=True)
                    last.then_inc(s["o_ps"], 1)
                if st.on(A1):
                    st.wait("osq_ok", A1)
                    mm(S[:, 0, D:2 * D], headmask[:], osq[:], start=True, stop=True).then_inc(s["ms_ps"], 1)

            pipeline(pe, step)

            pe.wait_ge(s["seen_ok"], NT)
            mm(TA[0:E, 0:1], seen[:, 0, :], ones_h[:, 0:1], start=True, stop=True).then_inc(s["table_ps"], 1)
            pe.wait_ge(s["table_ok"], 1)
            mm(TB[:, 0:E], nt_b[:], e_lt[:], start=True, stop=True)
            for c in range(EC):
                mm(QQ[0:ER, c:c + 1], r_lt[:, c * ER:(c + 1) * ER], nt_c[:], start=True, stop=True)
                last = mm(KK[0:ER, c:c + 1], r_eq[:, c * ER:(c + 1) * ER], nt_c[:], start=True, stop=True)
            last.then_inc(s["table_ps"], 1)
            pe.wait_ge(s["table_ok"], 2)
            pe.wait_ge(s["table_ok"], 3)
            for c in range(EC):
                mm(S[:, 0, 0:MT], list_f[0:ER, c, :], hot[0:ER, c, :], start=(c == 0), stop=(c == EC - 1))
            for c in range(EC):
                last = mm(S[0:2, 1, 0:MT], ecol[0:ER, c, :], hot[0:ER, c, :], start=(c == 0), stop=(c == EC - 1))
            last.then_inc(s["table_ps"], 1)
            pe.wait_ge(s["plan_ok"], 1)
            pe.wait_ge(s["experts_in"], 16 * 2 * (E // 8))

            def expert(st, lag):
                return pe.value_load(eid[0:1, bass.ds(st.tile(lag), 1)], min_val=0, max_val=E - 1)

            held = {}

            def step2(st):
                if st.q == 0:
                    held.clear()
                    if st.on(1):
                        held[-1] = expert(st, 1)
                if st.on(0):
                    pe.wait_ge(g_in[st.par(0, 4)], st.dma(0, 4))
                    st.wait("gx_ok", 2)
                    flip((TA, TB)[st.par(0)], xg[:, st.par(0, 4), :], "gx_ps")
                if st.on(1):
                    e = held[st.q - 1]
                    st.wait("gx_ok", 1)
                    st.wait("ag_ok", 3)
                    bank = (QQ, KK)[st.par(1)]
                    for k in range(KC):
                        last = mm(bank[:, 0:D], xgT[:, st.par(1), k, :],
                                  w13[:, bass.ds(e, 1), k, :].rearrange("p o f -> p (o f)"),
                                  start=(k == 0), stop=(k == KC - 1))
                    last.then_inc(s["gg_ps"], 1)
                if st.q == 0:
                    for lag in (3, 2):
                        if st.on(lag):
                            held[-lag] = expert(st, lag)
                if st.on(0) and st.q < UNROLL - 1:
                    held[st.q] = expert(st, 0)
                if st.on(2):
                    st.wait("ag_ok", 2)
                    st.wait("agT_ok", 4)
                    nc.tensor.transpose(S[:, st.par(2), 0:P], ag[:, st.par(2), :], ident[:]).then_inc(s["agT_ps"], 1)
                if st.on(3):
                    e = held[st.q - 3]
                    st.wait("agT_ok", 3)
                    st.wait("eo_ok", 5)
                    mm(S[:, 2 + st.par(3), 0:D], agT[:, st.par(3), :],
                       w2[:, bass.ds(e, 1), :].rearrange("p o d -> p (o d)"), start=True, stop=True
                       ).then_inc(s["dn2_ps"], 1)

            row_tiles(pe, step2)

        @block.scalar
        def _(act):
            A_ = nc.scalar.activation
            act.preload_act_table_set("natural_log_exp_and_others")
            for n in range(4):
                act.wait_ge(s["fold_ps"], n + 1)
                nc.scalar.copy(w_f[:, n, :, :], S[:, n % 2, :].rearrange("p (k d) -> p k d", k=KC)
                               ).then_inc(s["fold_done"], 1)
            act.wait_ge(s["setup_done"], 1)

            def copy(dst_, src, done):
                nc.scalar.copy(dst_, src).then_inc(s[done], 1)

            def rsqrt(dst_, src, e, scale, st, ln, done, stage):
                A_(dst_[0], src, ACT.Ln, bias=e, scale=scale).then_inc(s[ln], 1)
                st.wait(ln, stage)
                A_(dst_[1], dst_[0], ACT.Exp, scale=-0.5).then_inc(s[done], 1)

            def tiles(bank):
                return bank.rearrange("p (k t) -> p k t", t=P)

            def step(st):
                if st.on(B):
                    st.wait("mv_b_ok", B)
                    rsqrt((r_b[:, 0:1], r_b[:, 1:2]), mv_b[:, 1:2], eps[:, 0:1], 1.0, st, "ln_b_ok", "r_b_ok", B)
                if st.on(C1):
                    st.wait("attT_ps", C1)
                    copy(attT[:], tiles(S[:, 1, 0:D]), "attT_ok")
                if st.on(B):
                    st.wait("kv_ps", B)
                    st.wait("kvb_ok", B + 1)
                    nc.scalar.copy(qkv_raw[:, 1, :], TA[:, 0:D])
                    copy(qkv_raw[:, 2, :].rearrange("p (d h) -> p h d", h=H),
                         TA[:, D:2 * D].rearrange("p (h d) -> p h d", h=H), "kv_cp")
                if st.on(B):
                    st.wait("x1T_ps", B)
                    copy(x1T[:], tiles(TB[:, 0:D]), "x1T_ok")
                if st.on(A1):
                    st.wait("q_ps", A1)
                    st.wait("qf_ok", A1 + 1)
                    A_(tq[:], tiles(QQ[:, D:2 * D]), ACT.Identity, bias=f_b2[:, 0:1], scale=DK ** -0.5).then_inc(s["tq_ok"], 1)
                    st.wait("k_ps", A1)
                    st.wait("kp_ok", A1 + 1)
                    A_(tk[:], tiles(KK[:, D:2 * D]), ACT.Identity, bias=f_b[:, 3:4]).then_inc(s["tk_ok"], 1)
                if st.on(A1):
                    st.wait("kp_ok", A1)
                    st.wait("s_ps", A1 + 1)
                    for m_ in range(2):
                        last = A_(kblk[:, :, m_, :], kf[:].rearrange("p k (b l) -> p (k b) l", l=L), ACT.Identity,
                                  scale=parmask[:, m_:m_ + 1])
                    last.then_inc(s["kf_ok"], 1)
                if st.on(C2):
                    st.wait("dl_ok", C2)
                    A_(ew[:], dl[:], ACT.Exp, accum_out=es[:]).then_inc(s["ew_ok"], 1)
                if st.on(C1):
                    st.wait("mv_c_ok", C1)
                    rsqrt((r_c[:, 0:1], r_c[:, 1:2]), mv_c[:, 1:2], eps[:, 0:1], 1.0, st, "ln_c_ok", "r_c_ok", C1)
                if st.on(B):
                    st.wait("Q_ps", B)
                    st.wait("qb_ok", B + 1)
                    copy(qkv_raw[:, 0, :], S[:, 1, 0:D], "Q_cp")
                if st.on(C1):
                    st.wait("v2_ok", C1)
                    rsqrt((r2[:, 0:1], r2[:, 1:2]), v2[:], eps[:, 1:2], 1.0, st, "ln_2_ok", "r2_ok", C1)
                if st.on(A1):
                    st.wait("v_ps", A1)
                    st.wait("o_ps", A1 + 1)
                    for b in range(2):
                        for h in range(2):
                            last = nc.scalar.copy(
                                vblk[h * L:(h + 1) * L, b, :, h * DK:(h + 1) * DK],
                                S[b * L:(b + 1) * L, 2, 0:D].rearrange("p (g h d) -> p g h d", h=2, d=DK)[:, :, h, :])
                    last.then_inc(s["v_ok"], 1)
                if st.on(TT):
                    st.wait("scm_ok", TT)
                    st.wait("ao_ok", TT + 1)
                    A_(pr[:], scm[:], ACT.Exp).then_inc(s["pr_ok"], 1)
                if st.on(A0):
                    st.wait("mv_a_ok", A0)
                    rsqrt((r_a[:, 0:1], r_a[:, 1:2]), mv_a[:, 1:2], eps[:, 0:1], 1.0, st, "ln_a_ok", "r_a_ok", A0)
                if st.on(C1):
                    st.wait("hT_ps", C1)
                    copy(hT[:], tiles(TB[:, 0:D]), "hT_ok")
                if st.on(A0):
                    st.wait("xT_ps", A0)
                    copy(xT[:], tiles(QQ[:, 0:D]), "xT_ok")
                if st.on(C1):
                    st.wait("gu_ps", C1)
                    A_(eg[:], TB[:, 0:P], ACT.Exp, scale=-1.0).then_inc(s["eg_ok"], 1)
                    st.wait("eg_ok", C1)
                    A_(gs[:], eg[:], ACT.Ln, bias=ones[:, 0:1]).then_inc(s["lne_ok"], 1)
                    st.wait("lne_ok", C1)
                    A_(eg[:], gs[:], ACT.Exp, scale=-1.0).then_inc(s["sig_ok"], 1)
                if st.on(A1):
                    st.wait("o_ps", A1)
                    A_(osq[:], S[:, 0, 0:D], ACT.Square).then_inc(s["osq_ok"], 1)
                if st.on(A1):
                    st.wait("ms_ps", A1)
                    rsqrt((osq[:], r_o[:]), S[:, 0, D:2 * D], eps[:, 0:1], 1.0 / DK, st, "ln_o_ok", "r_o_ok", A1)

            pipeline(act, step)

            act.wait_ge(s["plan_ok"], 1)

            def rows_of(st_n, buf):
                nc.scalar.copy(gcol[:, buf:buf + 1], gidx[:, bass.ds(st_n, 1)]).then_inc(s["gcol_ok"], 1)

            for n in range(3):
                rows_of(n, n)

            def step2(st):
                if st.on(0):
                    st.wait("gx_ps", 0)
                    st.wait("gg_ps", 2)
                    copy(xgT[:, st.par(0)], tiles((TA, TB)[st.par(0)][:, 0:D]), "gx_ok")
                    rows_of(st.n + 3, (st.q + 3) % 4)
                if st.on(1):
                    st.wait("gg_ps", 1)
                    st.wait("ag_ok", 3)
                    A_(sg[:, st.par(1), :], (QQ, KK)[st.par(1)][:, 0:FF], ACT.Silu).then_inc(s["sg_ok"], 1)
                if st.on(2):
                    st.wait("agT_ps", 2)
                    st.wait("dn2_ps", 4)
                    copy(agT[:, st.par(2), :], S[:, st.par(2), 0:P], "agT_ok")

            row_tiles(act, step2)

            act.wait_ge(s["cidx_ok"], 1)

            def step3(st):
                st.wait("fin_ok", 2)
                w_of = lambda ap: ap.rearrange("p o k -> p (o k)")
                nc.scalar.copy(wcol[:, st.par(0), :], w_of(route[:, bass.ds(st.n, 1), 2, :]))
                nc.scalar.copy(ccol[:, st.par(0), :], w_of(cidx[:, bass.ds(st.n, 1), :])).then_inc(s["ccol_ok"], 1)

            token_tiles(act, step3)

        @block.vector
        def _(v):
            tt = nc.vector.tensor_tensor
            ts = nc.vector.tensor_scalar
            stt = nc.vector.scalar_tensor_tensor

            links = [0]

            def link():
                links[0] += 1
                v.wait_ge(s["linked"], links[0])

            v.wait_ge(s["c_setup"], 1)
            v.wait_ge(s["fold_in"], 16 * 9)
            for n in range(4):
                last = tt(f_bd[:, n, :], f_t[:, n, :], headmask[:], ALU.mult)
            last.then_inc(s["c_bd"], 1)
            for k in range(KC):
                ts(w_o[:, k, :], w_o_raw[:, k, :], hn_w[:, 0:1], None, ALU.mult)
            ts(f_b2[:, 0:1], f_b[:, 1:2], DK ** -0.5, None, ALU.mult)
            nc.vector.tensor_reduce(parmask[:, 0:1], evens[:], X, ALU.add).then_inc(s["linked"], 1)
            link()
            ts(parmask[:, 1:2], parmask[:, 0:1], -1.0, 1.0, ALU.mult, ALU.add)
            ts(jend[:], expert_row[:], float(J), float(J), ALU.mult, ALU.add).then_inc(s["linked"], 1)
            link()
            for c in range(EC):
                last = ts(past[:, c, :], jend[:], rcol[:, c:c + 1], None, ALU.is_le)
            last.then_inc(s["linked"], 1)
            link()
            for n in range(2):
                last = nc.vector.tensor_reduce(ecol[:, :, n], past[:], X, ALU.add)
            last.then_inc(s["linked"], 1)
            link()
            stt(jcol[:], ecol[:, :, 0], -float(J), rcol[:], ALU.mult, ALU.add)
            nc.vector.memset(seen[:, 0, :], 0.0)
            nc.vector.memset(vblk[:], 0.0).then_inc(s["setup_done"], 1)
            v.wait_ge(s["setup_done"], 1)
            v.wait_ge(s["w_in"], 16 * 11)

            def heads(ap):
                return ap.rearrange("p (h d) -> p h d", h=H)

            def step(st):
                at = st.par(TT)

                def k_mult(c):
                    if c == 0:
                        st.wait("ao_ok", TT + 1)
                    q_ = qkv[:, at, 0, :].rearrange("p (h o d) -> p h o d", h=H, o=1)[:, c * HC:(c + 1) * HC]
                    k_ = qkv[:, at, 1, :].rearrange("p (o g d) -> p o g d", g=H, o=1)
                    last = tt(prod[:, c, :].rearrange("p (h g d) -> p h g d", h=HC, g=H),
                       q_.to_broadcast([P, HC, H, DK]), k_.to_broadcast([P, HC, H, DK]), ALU.mult)
                    last.then_inc(s[f"kp{c}"], 1)

                def k_sum(c):
                    st.wait(f"kp{c}", TT)
                    last = nc.vector.tensor_reduce(
                        sc[:, c * HC:(c + 1) * HC, :],
                        prod[:, c, :].rearrange("p (h g d) -> p h g d", h=HC, g=H), X, ALU.add)
                    if c == NCH - 1:
                        last.then_inc(s["sc_ok"], 1)

                def v_mult(c):
                    if c == 0:
                        st.wait("sc_ok", TT)
                    p_ = pr[:, c * HC:(c + 1) * HC, :].rearrange("p h (o g) -> p h o g", o=1)
                    v_ = qkv[:, at, 2, :].rearrange("p (o d g) -> p o d g", g=H, o=1)
                    last = tt(prod[:, c, :].rearrange("p (h d g) -> p h d g", h=HC, g=H),
                       p_.to_broadcast([P, HC, DK, H]), v_.to_broadcast([P, HC, DK, H]), ALU.mult)
                    last.then_inc(s[f"vp{c}"], 1)

                def v_sum(c):
                    st.wait(f"vp{c}", TT)
                    last = nc.vector.tensor_reduce(
                        ao[:, c * HC:(c + 1) * HC, :],
                        prod[:, c, :].rearrange("p (h d g) -> p h d g", h=HC, g=H), X, ALU.add)
                    if c == NCH - 1:
                        last.then_inc(s["ao_ok"], 1)

                T_ = st.on(TT)
                if st.on(B):
                    st.wait("x1_ok", B)
                    nc.vector.bn_stats(st_b[:], x1[:, st.par(B), :]).then_inc(s["st_b_ok"], 1)
                    st.wait("st_b_ok", B)
                    gate(v, s["tick"])
                    nc.vector.bn_aggr(mv_b[:], st_b[:]).then_inc(s["mv_b_ok"], 1)
                if T_:
                    st.wait("kvb_ok", TT)
                    st.wait("qb_ok", TT)
                    k_mult(0)
                if st.on(A2):
                    st.wait("r_o_ok", A2)
                    tt(oT[:].rearrange("p k t -> p (k t)"), S[:, 0, 0:D], r_o[:], ALU.mult).then_inc(s["oT_ok"], 1)
                if st.on(B):
                    st.wait("r_b_ok", B)
                    ts(x1n[:], x1[:, st.par(B), :], mv_b[:, 0:1], r_b[:, 1:2], ALU.subtract, ALU.mult
                       ).then_inc(s["x1n_ok"], 1)
                if st.on(C2):
                    st.wait("sig_ok", C2)
                    tt(gs[:], TB[:, 0:P], eg[:], ALU.mult).then_inc(s["gs_ok"], 1)
                    st.wait("gs_ok", C2)
                    tt(act_s[:], TB[:, P:2 * P], gs[:], ALU.mult).then_inc(s["act_ok"], 1)
                    st.wait("topi_ok", C2)
                    nc.vector.tensor_copy(topf[:], topi[:, 0:TOPK]).then_inc(s["topf_ok"], 1)
                if T_:
                    k_mult(1)
                    k_sum(0)
                if st.on(C2):
                    st.wait("topf_ok", C2)
                    tt(oh[:], expert_row[:].rearrange("p (o e) -> p o e", o=1).to_broadcast([P, TOPK, E]),
                       topf[:].rearrange("p (k o) -> p k o", o=1).to_broadcast([P, TOPK, E]), ALU.is_equal
                       ).then_inc(s["oh_ok"], 1)
                    st.wait("oh_ok", C2)
                    st.wait("seen_ok", C2 + 1)
                    with nc.allow_low_precision(reason="zeros and ones"):
                        nc.vector.tensor_reduce(mask_h[:], oh[:].rearrange("p k e -> p e k"), X, ALU.add
                                                ).then_inc(s["mask_ok"], 1)
                if st.on(C1):
                    st.wait("Wo_ps", C1)
                    st.wait("xb_ok", C1)
                    st.wait("res_ok", C1 + 1)
                    tt(x2[:], xb[:, st.par(C1), :], S[:, 2, 0:D], ALU.add).then_inc(s["x2_ok"], 1)
                    st.wait("x2_ok", C1)
                    nc.vector.bn_stats(st_c[:], x2[:]).then_inc(s["st_c_ok"], 1)
                if T_:
                    k_sum(1)
                if st.on(C1):
                    st.wait("st_c_ok", C1)
                    gate(v, s["tick"])
                    nc.vector.bn_aggr(mv_c[:], st_c[:]).then_inc(s["mv_c_ok"], 1)
                if st.on(A2):
                    st.wait("wo_ps", A2)
                    st.wait("xb_ok", A2 + 2)
                    tt(x1[:, st.par(A2), :], x_t[:, st.par(A2), :], S[:, 3, 0:D], ALU.add).then_inc(s["x1_ok"], 1)
                if st.on(A1):
                    st.wait("tq_ok", A1)
                    st.wait("s_ps", A1 + 1)
                    stt(qf[:], QQ[:, 0:D].rearrange("p (k t) -> p k t", t=P), f_b[:, 0:1], tq[:], ALU.add, ALU.mult
                        ).then_inc(s["qf_ok"], 1)
                    st.wait("tk_ok", A1)
                    st.wait("kf_ok", A1 + 1)
                    stt(kf[:], KK[:, 0:D].rearrange("p (k t) -> p k t", t=P), f_b[:, 2:3], tk[:], ALU.add, ALU.mult
                        ).then_inc(s["kp_ok"], 1)
                if T_:
                    k_sum(2)
                if st.on(C1):
                    st.wait("r_c_ok", C1)
                    stt(v2[:], mv_c[:, 1:2], r_c[:, 1:2], r_c[:, 1:2], ALU.mult, ALU.mult).then_inc(s["v2_ok"], 1)
                    ts(y[:], x2[:], mv_c[:, 0:1], r_c[:, 1:2], ALU.subtract, ALU.mult).then_inc(s["y_ok"], 1)
                if st.on(C2):
                    st.wait("dn_ps", C2)
                    st.wait("res_ok", C2)
                    if st.on(C2 + 2):
                        v.wait_ge(acc_out[st.par(C2)], st.dma(C2 + 2))
                    tt(acc[:, st.par(C2), :], res[:, st.par(C2), :], TB[:, 0:D], ALU.add
                       ).then_inc(s["acc_ok"], 1)
                    st.wait("pos_ps", C2)
                    tt(pk[:], oh[:], S[:, 1, 0:E].rearrange("p (o e) -> p o e", o=1).to_broadcast([P, TOPK, E]), ALU.mult
                       ).then_inc(s["pk_ok"], 1)
                    tt(seen[:, 1 - st.par(C2), :], seen[:, st.par(C2), :], mask_h[:], ALU.add).then_inc(s["seen_ok"], 1)
                if T_:
                    k_sum(3)
                if st.on(C1):
                    st.wait("r2_ok", C1)
                    st.wait("y_ok", C1)
                    if st.on(C1 + 2):
                        v.wait_ge(h_out[st.par(C1)], st.dma(C1 + 2))
                    st.wait("hT_ps", C1 + 2)
                    stt(hrow[:, st.par(C1), :], y[:], r2[:, 1:2], nw[:], ALU.mult, ALU.mult).then_inc(s["h_ok"], 1)
                if st.on(C2):
                    st.wait("ew_ok", C2)
                    nc.vector.reciprocal(rs[:], es[:]).then_inc(s["rs_ok"], 1)
                if T_:
                    st.wait("sc_ok", TT)
                    nc.vector.tensor_reduce(mx[:], sc[:], X, ALU.max).then_inc(s["mx_ok"], 1)
                if st.on(C2):
                    st.wait("pk_ok", C2)
                    nc.vector.tensor_reduce(pos[:], pk[:], X, ALU.add).then_inc(s["pos_ok"], 1)
                if T_:
                    st.wait("mx_ok", TT)
                    tt(scm[:], sc[:], mx[:].rearrange("p (h o) -> p h o", o=1).to_broadcast([P, H, H]), ALU.subtract
                       ).then_inc(s["scm_ok"], 1)
                if st.on(C2):
                    rt = lambda n: route[:, bass.ds(st.tile(C2), 1), n, :].rearrange("p o k -> p (o k)")
                    st.wait("pos_ok", C2)
                    ts(over[:], pos[:], float(CAP), None, ALU.is_ge)
                    stt(row[:], topf[:], float(CAP), pos[:], ALU.mult, ALU.add).then_inc(s["row_ok"], 1)
                    ts(rt(1), pos[:], float(CAP - 1), None, ALU.min)
                    ts(rt(0), topf[:], 1.0, None, ALU.mult)
                    st.wait("row_ok", C2)
                    tt(gap[:], trash_row[:, bass.ds(st.tile(C2), 1), :].rearrange("p o k -> p (o k)"), row[:], ALU.subtract
                       ).then_inc(s["gap_ok"], 1)
                    st.wait("rs_ok", C2)
                    ts(rt(2), ew[:], rs[:, 0:1], None, ALU.mult)
                if st.on(A0):
                    v.wait_ge(x_in[st.par(A0)], st.dma(A0))
                    gate(v, s["tick"])
                    nc.vector.bn_stats(st_a[:], x_t[:, st.par(A0), :]).then_inc(s["st_a_ok"], 1)
                    st.wait("st_a_ok", A0)
                    gate(v, s["tick"])
                    nc.vector.bn_aggr(mv_a[:], st_a[:]).then_inc(s["mv_a_ok"], 1)
                if T_:
                    st.wait("pr_ok", TT)
                    v_mult(0)
                    v_mult(1)
                if st.on(C2):
                    st.wait("gap_ok", C2)
                    tt(over[:], over[:], gap[:], ALU.mult).then_inc(s["gapo_ok"], 1)
                    if st.on(C2 + 2):
                        v.wait_ge(sent[st.par(C2)], st.dma(C2 + 2) * TOPK)
                        gate(v, s["tick"])
                    nc.vector.tensor_copy(tid[:, st.par(C2):st.par(C2) + 1], tok_id[:, bass.ds(st.tile(C2), 1)])
                    st.wait("gapo_ok", C2)
                    tt(slot[:, st.par(C2), :], row[:], over[:], ALU.add).then_inc(s["slot_ok"], 1)
                if st.on(A0):
                    st.wait("r_a_ok", A0)
                    ts(xn[:], x_t[:, st.par(A0), :], mv_a[:, 0:1], r_a[:, 1:2], ALU.subtract, ALU.mult
                       ).then_inc(s["xn_ok"], 1)
                if T_:
                    v_sum(0)
                if st.on(A1):
                    st.wait("s_ps", A1)
                    st.wait("o_ps", A1 + 1)
                    tt(sm[:].rearrange("p j c l -> p j (c l)"), S[:, :, 0:2 * KC * L],
                       causal4(causal), ALU.mult).then_inc(s["s_ok"], 1)
                if T_:
                    v_sum(1)
                    nc.vector.tensor_reduce(psm[:], pr[:], X, ALU.add).then_inc(s["psm_ok"], 1)
                    v_sum(2)
                    st.wait("psm_ok", TT)
                    nc.vector.reciprocal(pri[:], psm[:]).then_inc(s["pri_ok"], 1)
                if st.on(C1):
                    st.wait("eg_ok", C1)
                    gate(v, s["tick"])
                    nc.vector.max(top[:], TB[:, D:D + E]).then_inc(s["top_ok"], 1)
                    st.wait("top_ok", C1)
                    gate(v, s["tick"])
                    nc.vector.max_index(topi[:], top[:], TB[:, D:D + E]).then_inc(s["topi_ok"], 1)
                    ts(dl[:], top[:, 0:TOPK], top[:, 0:1], None, ALU.subtract).then_inc(s["dl_ok"], 1)
                if T_:
                    v_sum(3)
                    st.wait("ao_ok", TT)
                    st.wait("pri_ok", TT)
                    st.wait("attT_ps", TT + 1)
                    tt(heads(att[:]), ao[:], pri[:].rearrange("p (h o) -> p h o", o=1).to_broadcast([P, H, DK]), ALU.mult
                       ).then_inc(s["att_ok"], 1)

            def causal4(m_):
                return m_[:].rearrange("p (j c l) -> p j c l", j=1, c=1).to_broadcast([P, 4, 2 * KC, L])

            pipeline(v, step)

            v.wait_ge(s["table_ps"], 1)
            ts(cnt_c[:], TA[0:E, 0:1], float(CAP), None, ALU.min).then_inc(s["linked"], 1)
            link()
            ts(have[:], jrow[:], cnt_c[:, 0:1], None, ALU.is_lt).then_inc(s["linked"], 1)
            link()
            nc.vector.tensor_reduce(nt_c[:], have[:], X, ALU.add).then_inc(s["linked"], 1)
            link()
            nc.vector.tensor_copy(nt_b[:], nt_c[:].to_broadcast([E, P])).then_inc(s["table_ok"], 1)
            v.wait_ge(s["table_ps"], 2)
            nc.vector.tensor_copy(base[:], TB[:, 0:E])
            tt(dst[0:ER, :], jcol[0:ER, :], QQ[0:ER, 0:EC], ALU.add)
            tt(nov[0:ER, :], jcol[0:ER, :], KK[0:ER, 0:EC], ALU.is_ge).then_inc(s["linked"], 1)
            link()
            stt(dstv[0:ER, :], nov[0:ER, :], float(2 * MT), dst[0:ER, :], ALU.mult, ALU.add).then_inc(s["linked"], 1)
            link()
            for c in range(EC):
                last = ts(hot[0:ER, c, :], tcol[0:ER, :], dstv[0:ER, c:c + 1], None, ALU.is_equal)
            last.then_inc(s["table_ok"], 1)
            v.wait_ge(s["lists_in"], 16)
            nc.vector.tensor_copy(list_f[0:ER], list_i[0:ER]).then_inc(s["table_ok"], 1)
            v.wait_ge(s["table_ps"], 3)
            nc.vector.tensor_copy(gidx[:, 0:MT], S[:, 0, 0:MT])
            nc.vector.tensor_copy(eid[:, 0:MT], S[0:2, 1, 0:MT]).then_inc(s["plan_ok"], 1)
            G = NT // 4
            for c in range(4):
                tiles_ = slice(c * G, (c + 1) * G)
                g4 = bk_e[:].rearrange("p (t k) e -> p t k e", k=TOPK)
                e_in = route[:, tiles_, 0, :].rearrange("p t (k o) -> p t k o", o=1).to_broadcast([P, G, TOPK, E])
                tt(g4, expert_row[:].rearrange("p (a b e) -> p a b e", a=1, b=1).to_broadcast([P, G, TOPK, E]),
                   e_in, ALU.is_equal).then_inc(s["linked"], 1)
                link()
                tt(g4, g4, base[:].rearrange("p (a b e) -> p a b e", a=1, b=1).to_broadcast([P, G, TOPK, E]),
                   ALU.mult).then_inc(s["linked"], 1)
                link()
                nc.vector.tensor_reduce(cb[:, tiles_, :], g4, X, ALU.add).then_inc(s["linked"], 1)
                link()
            stt(cidx[:], cb[:], float(P), route[:, :, 1, :], ALU.mult, ALU.add).then_inc(s["cidx_ok"], 1)

            def step2(st):
                if st.on(1):
                    st.wait("sg_ok", 1)
                    st.wait("agT_ps", 3)
                    tt(ag[:, st.par(1), :], (QQ, KK)[st.par(1)][:, FF:2 * FF], sg[:, st.par(1), :], ALU.mult
                       ).then_inc(s["ag_ok"], 1)
                if st.on(3):
                    st.wait("dn2_ps", 3)
                    if st.on(5):
                        v.wait_ge(eo_out[st.par(3)], st.dma(5))
                        gate(v, s["tick"])
                    nc.vector.tensor_copy(eo[:, st.par(3), :], S[:, 2 + st.par(3), 0:D]).then_inc(s["eo_ok"], 1)

            row_tiles(v, step2)

            def step3(st):
                b = st.par(0)
                v.wait_ge(er_in[b], st.dma(0) * TOPK)
                st.wait("ccol_ok", 0)
                if st.on(2):
                    v.wait_ge(out_done[b], st.dma(2))
                v.wait_ge(acc_in[b], st.dma(0))
                stt(part[:, 0, :], er[:, b, 0, :], wcol[:, b, 0:1], acc[:, b, :], ALU.mult, ALU.add).then_inc(s["part_ok"], 1)
                for k in range(1, TOPK):
                    v.wait_ge(s["part_ok"], st.n * (TOPK - 1) + k)
                    to = part[:, k, :] if k < TOPK - 1 else fin[:, b, :]
                    stt(to, er[:, b, k, :], wcol[:, b, k:k + 1], part[:, k - 1, :], ALU.mult, ALU.add
                        ).then_inc(s["part_ok" if k < TOPK - 1 else "fin_ok"], 1)

            token_tiles(v, step3)

        @block.gpsimd
        def _(g):
            gp = nc.gpsimd
            tt = gp.tensor_tensor

            def among(ap, pattern, base, mult, op, fill=0.0):
                gp.affine_select(out=ap, in_=ap, compare_op=op, fill=fill, base=base, pattern=pattern,
                                 channel_multiplier=mult).then_inc(s["c_small"], 1)
                count[0] += 1
                g.wait_ge(s["c_small"], count[0])

            count = [1]
            gp.memset(ones[:], 1.0)
            for ap in (ident[:], causal[:], headmask[:], evens[:], before[:], ones_h[:], e_lt[:], r_lt[:], r_eq[:]):
                gp.memset(ap, 1.0)
            gp.memset(eps[:, 0:1], LN_EPS)
            gp.memset(eps[:, 1:2], RMS_EPS)
            gp.memset(zeros_i[:], 0)
            gp.memset(eid[:], 0)
            gp.memset(gidx[:, MT:MT + 4], 0).then_inc(s["c_small"], 1)
            g.wait_ge(s["c_small"], 1)
            among(ident[:], [[-1, P]], 0, 1, ALU.is_equal)
            for b in range(2):
                among(causal[b * L:(b + 1) * L, :], [[1, L]], 0, -1, ALU.is_ge)
            hm = headmask[:].rearrange("p (b j) -> p b j", j=DK)
            among(hm, [[-DK, P // DK], [0, DK]], 0, 1, ALU.is_ge)
            among(hm, [[DK, P // DK], [0, DK]], DK - 1, -1, ALU.is_ge)
            among(evens[:], [[-2 * DK, 4]], 0, 1, ALU.is_ge)
            among(evens[:], [[2 * DK, 4]], DK - 1, -1, ALU.is_ge)
            among(before[:], [[1, P]], 0, -1, ALU.is_gt)
            among(e_lt[:], [[1, E]], 0, -1, ALU.is_gt)
            among(r_lt[:], [[1, EJ]], -J, -J, ALU.is_ge)
            among(r_eq[:], [[1, EJ]], 0, -J, ALU.is_ge)
            among(r_eq[:], [[-1, EJ]], J - 1, J, ALU.is_ge)
            small = dict(allow_small_or_imprecise_dtypes=True)
            gp.iota(expert_row[:], pattern=[[1, E]], base=0, channel_multiplier=0, **small)
            gp.iota(tok_id[:], pattern=[[P, NT]], base=0, channel_multiplier=1)
            gp.iota(trash_row[:], pattern=[[TOPK * P, NT], [P, TOPK]], base=TRASH, channel_multiplier=1, **small)
            gp.iota(jrow[:], pattern=[[P, J]], base=0, channel_multiplier=0, **small)
            gp.iota(tcol[:], pattern=[[1, MT]], base=0, channel_multiplier=0, **small)
            gp.iota(rcol[:], pattern=[[ER, EC]], base=0, channel_multiplier=1, **small).then_inc(s["c_setup"], 1)
            g.wait_ge(s["setup_done"], 1)
            g.wait_ge(s["w_in"], 16 * 11)
            g.wait_ge(s["zero_in"], 16)

            def step(st):
                at = st.par(TT)
                if st.on(TT):
                    st.wait("qb_ok", TT)
                    st.wait("ao_ok", TT + 1)
                    for c in GP_K:
                        q_ = qkv[:, at, 0, :].rearrange("p (h o d) -> p h o d", h=H, o=1)[:, c * HC:(c + 1) * HC]
                        k_ = qkv[:, at, 1, :].rearrange("p (o g d) -> p o g d", g=H, o=1)
                        tt(prod[:, c, :].rearrange("p (h g d) -> p h g d", h=HC, g=H),
                           q_.to_broadcast([P, HC, H, DK]), k_.to_broadcast([P, HC, H, DK]), ALU.mult
                           ).then_inc(s[f"kp{c}"], 1)
                if st.on(B):
                    st.wait("x1_ok", B)
                    st.wait("x2_ok", C1)
                    tt(xb[:, st.par(B), :], x1[:, st.par(B), :], b_x[:, 3, :], ALU.add).then_inc(s["xb_ok"], 1)
                if st.on(B):
                    st.wait("kv_cp", B)
                    st.wait("att_ok", C1)
                    tt(qkv[:, st.par(B), 1, :], qkv_raw[:, 1, :], b_x[:, 1, :], ALU.add)
                    tt(qkv[:, st.par(B), 2, :].rearrange("p (d h) -> p d h", h=H),
                       qkv_raw[:, 2, :].rearrange("p (d h) -> p d h", h=H),
                       b_x[:, 2, :].rearrange("p (h d) -> p d h", d=DK), ALU.add).then_inc(s["kvb_ok"], 1)
                if st.on(C1):
                    st.wait("y_ok", C1)
                    st.wait("acc_ok", C1 + 2)
                    tt(res[:, st.par(C1), :], x2[:], y[:], ALU.add).then_inc(s["res_ok"], 1)
                if st.on(B):
                    st.wait("Q_cp", B)
                    tt(qkv[:, st.par(B), 0, :], qkv_raw[:, 0, :], b_x[:, 0, :], ALU.add).then_inc(s["qb_ok"], 1)
                if st.on(TT):
                    st.wait("pr_ok", TT)
                    st.wait("sc_ok", TT)
                    for c in GP_V:
                        p_ = pr[:, c * HC:(c + 1) * HC, :].rearrange("p h (o g) -> p h o g", o=1)
                        v_ = qkv[:, at, 2, :].rearrange("p (o d g) -> p o d g", g=H, o=1)
                        tt(prod[:, c, :].rearrange("p (h d g) -> p h d g", h=HC, g=H),
                           p_.to_broadcast([P, HC, DK, H]), v_.to_broadcast([P, HC, DK, H]), ALU.mult
                           ).then_inc(s[f"vp{c}"], 1)
                if st.on(C2):
                    st.wait("slot_ok", C2)
                    gate(g, s["tick"])
                    for k in range(TOPK):
                        gp.indirect_dma_start(
                            out=list_d, out_offset=bass.IndirectOffsetOnAxis(ap=slot[:, st.par(C2), k:k + 1], axis=0),
                            in_=tid[:, st.par(C2):st.par(C2) + 1], in_offset=None).then_inc(sent[st.par(C2)], 16)

            pipeline(g, step)

            for par in range(2):
                g.wait_ge(h_out[par], 16 * (NT // 2))

            def gather(st):
                if st.on(0):
                    st.wait("gcol_ok", 0)
                    st.wait("gx_ps", 4)
                    gate(g, s["tick"])
                    gp.indirect_dma_start(
                        out=xg[:, st.par(0, 4), :], out_offset=None, in_=h_d,
                        in_offset=bass.IndirectOffsetOnAxis(ap=gcol[:, st.par(0, 4):st.par(0, 4) + 1], axis=0)
                    ).then_inc(g_in[st.par(0, 4)], 16)

            row_tiles(g, gather)

            for par in range(2):
                g.wait_ge(eo_out[par], 16 * (MT // 2))

            def fetch(st):
                st.wait("ccol_ok", 0)
                st.wait("fin_ok", 2)
                gate(g, s["tick"])
                for k in range(TOPK):
                    gp.indirect_dma_start(
                        out=er[:, st.par(0), k, :], out_offset=None, in_=eo_d,
                        in_offset=bass.IndirectOffsetOnAxis(ap=ccol[:, st.par(0), k:k + 1], axis=0)
                    ).then_inc(er_in[st.par(0)], 16)

            token_tiles(g, fetch)


_IN = {
    "x": lambda i: i["x"], "ctxT": lambda i: _flat(i["ctx_2048"]).T,
    "wq": lambda i: i["L0_attn_wq"], "wk": lambda i: i["L0_attn_wk"],
    "wvT": lambda i: i["L0_attn_wv"].T, "woT": lambda i: i["L0_attn_wo"].T,
    "fq1": lambda i: _tile(i["L0_attn_fq1_w"].T, (8, 8)), "fq2": lambda i: _tile(i["L0_attn_fq2_w"].T, (8, 8)),
    "fk1": lambda i: _tile(i["L0_attn_fk1_w"].T, (8, 8)), "fk2": lambda i: _tile(i["L0_attn_fk2_w"].T, (8, 8)),
    "fb": lambda i: _tile(_stack([i["L0_attn_fq1_b"], i["L0_attn_fq2_b"], i["L0_attn_fk1_b"], i["L0_attn_fk2_b"]]).T, (8, 1)),
    "hn_w": lambda i: _tile(i["L0_attn_norm_w"].reshape(-1, 1), (8, 1)),
    "WqT": lambda i: i["L0_xattn_Wq"].T, "WkT": lambda i: i["L0_xattn_Wk"].T,
    "WvT": lambda i: i["L0_xattn_Wv"].T, "WoT": lambda i: i["L0_xattn_Wo"].T,
    "xb": lambda i: _stack([i["L0_xattn_bq"], i["L0_xattn_bk"], i["L0_xattn_bv"], i["L0_xattn_bo"]]),
    "nw": lambda i: i["L0_ffn_norm_w"].reshape(1, -1), "gateT": lambda i: i["L0_ffn_gate_w"].T,
    "w13": lambda i: i["L0_ffn_w13"], "w2": lambda i: i["L0_ffn_w2"],
    "sg": lambda i: i["L0_ffn_shared_gate_w"], "su": lambda i: i["L0_ffn_shared_up_w"],
    "sd": lambda i: i["L0_ffn_shared_down_w"],
}


def _flat(a):
    return a.reshape(-1, a.shape[-1])


def _tile(a, n):
    import numpy as np
    return np.tile(a, n)


def _stack(a):
    import numpy as np
    return np.stack(a)


def kernel(**inputs):
    import numpy as np
    import concourse.bacc as bacc
    from concourse.bass_utils import run_bass_kernel_spmd

    host = {k: np.asarray(v) for k, v in inputs.items()}
    nc = bacc.Bacc("TRN2", target_bir_lowering=False, num_devices=1)
    arrays, aps = {}, {}
    for name, lay in _IN.items():
        arrays[f"in_{name}"] = np.ascontiguousarray(lay(host))
        arr = arrays[f"in_{name}"]
        aps[name] = nc.dram_tensor(f"in_{name}", arr.shape, mybir.dt.from_np(arr.dtype), kind="ExternalInput").ap()
    out = nc.dram_tensor("out", host["x"].shape, F32, kind="ExternalOutput").ap()
    decoder_layer_kernel(nc, aps, out)
    return run_bass_kernel_spmd(nc, [arrays], core_ids=[0]).results[0]["out"]
```

```python
from contextlib import ExitStack

import concourse.bass as bass
from concourse import mybir

F32 = mybir.dt.float32
BF16 = mybir.dt.bfloat16
I32 = mybir.dt.int32
U32 = mybir.dt.uint32
ALU = mybir.AluOpType
ACT = mybir.ActivationFunctionType
X = mybir.AxisListType.X

P = 128
L = 64
D = 256
H = 16
DK = D // H
KC = D // P
E = 32
TOPK = 4
FF = 128
NCH = 4
HC = H // NCH
LN_EPS = 1e-5
RMS_EPS = 1e-6
HEAD_EPS = 1e-5


def decoder_layer_kernel(nc, a, out):
    NB, _, _ = a["x"].shape
    T = NB * L
    NT = T // P
    CAP = TOPK * T * 2 // E
    J = (CAP + P - 1) // P
    EJ = E * J
    EC = (EJ + P - 1) // P
    ER = min(EJ, P)
    MT = min(EJ, (TOPK * T + E * (P - 1)) // P)
    MT += -MT % 4
    PAD = TOPK * T
    SPARE = PAD + E * CAP
    TRASH = E * CAP
    assert NT >= 10 and NT % 4 == 0 and CAP % P == 0 and EJ % ER == 0

    x_d = a["x"].rearrange("b l d -> (b l) d")
    out_d = out.rearrange("b l d -> (b l) d")
    ctxT_d = a["ctxT"].rearrange("(k p) t -> p k t", p=P)
    h_d = nc.dram_tensor("h_rows", (T, D), F32, kind="Internal").ap()
    list_d = nc.dram_tensor("token_lists", (E * CAP + TOPK * T, 1), I32, kind="Internal").ap()
    acc_d = nc.dram_tensor("acc_rows", (T, D), F32, kind="Internal").ap()
    eo_d = nc.dram_tensor("choice_rows", (SPARE + MT * P, D), F32, kind="Internal").ap()

    with ExitStack() as ctx:
        def sb(name, shape, dt=F32):
            return ctx.enter_context(nc.sbuf_tensor(name, shape, dt))

        def ps(name, shape, dt=F32):
            return ctx.enter_context(nc.psum_tensor(name, shape, dt))

        def sem(name):
            return ctx.enter_context(nc.semaphore(name))

        ident = sb("ident", [P, P])
        ones = sb("ones", [P, P])
        causal = sb("causal", [P, L])
        headmask = sb("headmask", [P, P])
        evens = sb("evens", [P, 4])
        parmask = sb("parmask", [P, 2])
        before = sb("before", [P, P], BF16)
        ones_h = sb("ones_h", [P, P], BF16)
        expert_row = sb("expert_row", [P, E])
        eps = sb("eps", [P, 2])
        number = sb("number", [P, NT, TOPK])
        trash_row = sb("trash_row", [P, NT, TOPK])
        pad_i = sb("pad_i", [P, E * CAP // P], I32)
        w_f = sb("w_f", [P, 4, KC, D])
        f_b = sb("f_b", [P, 4])
        f_b2 = sb("f_b2", [P, 1])
        hn_w = sb("hn_w", [P, 1])
        w_v = sb("w_v", [P, KC, D])
        w_o = sb("w_o", [P, KC, D])
        W_q = sb("W_q", [P, KC, D])
        W_kv = sb("W_kv", [P, KC, 2, D])
        W_o = sb("W_o", [P, KC, D])
        b_x = sb("b_x", [P, 4, D])
        nw = sb("nw", [P, D])
        w_gate = sb("w_gate", [P, KC, E])
        w_sgu = sb("w_sgu", [P, KC, 2, FF])
        w_sd = sb("w_sd", [P, D])
        w13 = sb("w13", [P, E, KC, 2 * FF])
        w2 = sb("w2", [P, E, D])

        x_t = sb("x_t", [P, 2, D])
        st_a = sb("st_a", [P, 6])
        mv_a = sb("mv_a", [P, 2])
        r_a = sb("r_a", [P, 2])
        xn = sb("xn", [P, D])
        xT = sb("xT", [P, KC, P])
        tq = sb("tq", [P, KC, P])
        tk = sb("tk", [P, KC, P])
        kf = sb("kf", [P, KC, P])
        qf = sb("qf", [P, KC, P])
        kblk = sb("kblk", [P, KC * 2, 2, L])
        vblk = sb("vblk", [P, 2, H // 2, 2 * DK])
        sm = sb("sm", [P, 4, 2 * KC, L])
        osq = sb("osq", [P, D])
        r_o = sb("r_o", [P, D])
        oT = sb("oT", [P, KC, P])
        x1 = sb("x1", [P, 2, D])
        st_b = sb("st_b", [P, 6])
        mv_b = sb("mv_b", [P, 2])
        r_b = sb("r_b", [P, 2])
        x1n = sb("x1n", [P, D])
        x1T = sb("x1T", [P, KC, P])
        c_t = sb("c_t", [P, 2, KC, P])
        qkv_raw = sb("qkv_raw", [P, 3, D])
        qkv = sb("qkv", [P, 2, 3, D])
        xb = sb("xb", [P, 2, D])
        prod = sb("prod", [P, NCH, HC * H * DK])
        sc = sb("sc", [P, H, H])
        mx = sb("mx", [P, H])
        scm = sb("scm", [P, H, H])
        pr = sb("pr", [P, H, H])
        psm = sb("psm", [P, H])
        pri = sb("pri", [P, H])
        ao = sb("ao", [P, H, DK])
        att = sb("att", [P, D])
        attT = sb("attT", [P, KC, P])
        x2 = sb("x2", [P, D])
        st_c = sb("st_c", [P, 6])
        mv_c = sb("mv_c", [P, 2])
        r_c = sb("r_c", [P, 2])
        v2 = sb("v2", [P, 1])
        r2 = sb("r2", [P, 2])
        y = sb("y", [P, D])
        hrow = sb("hrow", [P, 2, D])
        res = sb("res", [P, 2, D])
        hT = sb("hT", [P, KC, P])
        eg = sb("eg", [P, P])
        gs = sb("gs", [P, P])
        act_s = sb("act_s", [P, P])
        top = sb("top", [P, 8])
        topi = sb("topi", [P, 8], U32)
        topf = sb("topf", [P, TOPK])
        dl = sb("dl", [P, TOPK])
        ew = sb("ew", [P, TOPK])
        es = sb("es", [P, 1])
        rs = sb("rs", [P, 1])
        oh = sb("oh", [P, TOPK, E])
        mask_h = sb("mask_h", [P, E], BF16)
        seen = sb("seen", [P, 2, E], BF16)
        pk = sb("pk", [P, TOPK, E])
        pos = sb("pos", [P, TOPK])
        over = sb("over", [P, TOPK])
        row = sb("row", [P, TOPK])
        gap = sb("gap", [P, TOPK])
        slot = sb("slot", [P, 2, TOPK], U32)
        tid = sb("tid", [P, 2, TOPK], I32)
        route = sb("route", [P, NT, 3, TOPK])
        acc = sb("acc", [P, 2, D])
        cnt_c = sb("cnt_c", [E, 1])
        jrow = sb("jrow", [E, J])
        have = sb("have", [E, J])
        nt_c = sb("nt_c", [E, 1])
        nt_b = sb("nt_b", [E, P])
        e_lt = sb("e_lt", [E, E])
        r_lt = sb("r_lt", [E, EJ])
        r_eq = sb("r_eq", [E, EJ])
        rcol = sb("rcol", [P, EC])
        past = sb("past", [P, EC, E])
        jend = sb("jend", [P, E])
        ecol = sb("ecol", [P, EC, 2])
        jcol = sb("jcol", [P, EC])
        own_f = sb("own_f", [P, E])
        dst = sb("dst", [P, EC])
        nov = sb("nov", [P, EC])
        dstv = sb("dstv", [P, EC])
        tcol = sb("tcol", [P, MT])
        rows_u = sb("rows_u", [P, MT + 4, 2], U32)
        last_j = sb("last_j", [P, EC])
        over_e = sb("over_e", [E, 1])
        over_i = sb("over_i", [P, 1], I32)
        eid = sb("eid", [2, MT + 2], I32)
        gcol = sb("gcol", [P, 4], U32)
        dcol = sb("dcol", [P, 8], U32)
        cidx = sb("cidx", [P, NT, TOPK], U32)
        ccol = sb("ccol", [P, 2, TOPK], U32)
        wcol = sb("wcol", [P, 2, TOPK])

        early = w13[:].rearrange("p e k f -> p (e k f)")
        w_nat = early[:, 0:2 * KC * D].rearrange("p (n k d) -> p n k d", n=2, k=KC)
        early = early[:, 2 * KC * D:]
        w_o_raw = early[:, 0:KC * D].rearrange("p (k d) -> p k d", k=KC)
        early = early[:, KC * D:]
        f_t = early[:, 0:4 * P].rearrange("p (n m) -> p n m", n=4)
        f_bd = early[:, 4 * P:8 * P].rearrange("p (n m) -> p n m", n=4)
        list_f = prod[:, 2, 0:EC * P].rearrange("p (c l) -> p c l", c=EC)
        list_i = prod[:, 1, 0:EC * P].rearrange("p (c l) -> p c l", c=EC).bitcast(I32)
        cb = prod[:, 2, EC * (P + MT):EC * (P + MT) + NT * TOPK].rearrange("p (t k) -> p t k", k=TOPK)
        gap_all = prod[:, 1, 2 * EC * P:2 * EC * P + NT * TOPK].rearrange("p (t k) -> p t k", k=TOPK)
        hot = prod[:, 2, EC * P:EC * (P + MT)].rearrange("p (c t) -> p c t", c=EC)
        sg = prod[:, 3, 0:2 * FF].rearrange("p (b f) -> p b f", b=2)
        ag = prod[:, 3, 2 * FF:4 * FF].rearrange("p (b f) -> p b f", b=2)
        agT = prod[:, 3, 4 * FF:4 * FF + 2 * P].rearrange("p (b t) -> p b t", b=2)
        spare = w_f[:].rearrange("p n k d -> p (n k d)")[:, 0:MT]
        unused = w_f[:].rearrange("p n k d -> p (n k d)")[:, MT:2 * MT]
        lack = w_f[:].rearrange("p n k d -> p (n k d)")[:, 2 * MT:3 * MT]
        choice = w_f[:].rearrange("p n k d -> p (n k d)")[:, 3 * MT:4 * MT]
        blank = w_f[:].rearrange("p n k d -> p (n k d)")[:, 4 * MT:4 * MT + TOPK * D]
        er = prod[:].rearrange("p b (k d) -> p b k d", k=TOPK)
        part = sm[:].rearrange("p j c l -> p (j c l)").rearrange("p (k d) -> p k d", k=4)
        acc_p = W_kv[:].rearrange("p k n d -> p (k n) d")
        fin = qkv[:].rearrange("p b n d -> p (b n) d")
        xg = qkv[:].rearrange("p b n d -> p (b n) d")
        xgT = kblk[:].rearrange("p c m l -> p (c m l)").rearrange("p (n k t) -> p n k t", n=2, k=KC)
        eo = prod[:, 0, :].rearrange("p (b d) -> p b d", b=4)
        bk_e = W_kv[:].rearrange("p k n d -> p (k n d)")[:, 0:NT * TOPK // 4 * E].rearrange("p (t e) -> p t e", e=E)

        TA = ps("TA", [P, 512])
        TB = ps("TB", [P, 512])
        QQ = ps("QQ", [P, 512])
        KK = ps("KK", [P, 512])
        S = ps("S", [P, 4, 512])

        names = """w_in fold_in zero_in experts_in c_setup c_bd fold_ps fold_done setup_done
            st_a_ok mv_a_ok ln_a_ok r_a_ok xn_ok xT_ps xT_ok q_ps k_ps v_ps tq_ok tk_ok v_ok qf_ok kp_ok kf_ok s_ps s_ok
            o_ps osq_ok ms_ps ln_o_ok r_o_ok oT_ok wo_ps x1_ok
            st_b_ok mv_b_ok ln_b_ok r_b_ok x1n_ok x1T_ps x1T_ok kv_ps kv_cp Q_ps Q_cp kvb_ok qb_ok xb_ok
            kp0 kp1 kp2 kp3 sc_ok mx_ok scm_ok pr_ok psm_ok pri_ok vp0 vp1 vp2 vp3 ao_ok att_ok
            attT_ps attT_ok Wo_ps x2_ok st_c_ok mv_c_ok ln_c_ok r_c_ok y_ok v2_ok ln_2_ok r2_ok h_ok res_ok
            hT_ps hT_ok gu_ps eg_ok lne_ok sig_ok gs_ok act_ok top_ok topi_ok dl_ok ew_ok rs_ok
            topf_ok oh_ok mask_ok seen_ok dn_ps acc_ok pos_ps pk_ok pos_ok row_ok gap_ok gapo_ok slot_ok
            tick lists_in c_small
            table_ps table_ok linked plan_ok
            gcol_ok gx_ps gx_ok gg_ps sg_ok ag_ok agT_ps agT_ok dn2_ps eo_ok
            cidx_ok spare_ok rows_ready again_col again_in again_out wcol_ok part_ok fin_ok""".split()
        s = {n: sem(n) for n in names}
        x_in = [sem("x_in0"), sem("x_in1")]
        c_in = [sem("c_in0"), sem("c_in1")]
        h_out = [sem("h_out0"), sem("h_out1")]
        acc_out = [sem("acc_out0"), sem("acc_out1")]
        sent = [sem("sent0"), sem("sent1")]
        g_in = [sem(f"g_in{n}") for n in range(4)]
        eo_out = [sem(f"eo_out{n}") for n in range(4)]
        er_in = [sem(f"er_in{n}") for n in range(4)]
        out_done = [sem(f"out_done{n}") for n in range(4)]

        class Step:

            def __init__(self, eng, turn, q, unroll=2, count=NT):
                self.eng, self.turn, self.q, self.unroll, self.count = eng, turn, q, unroll, count
                self.n = turn * unroll + q
                self.fixed = isinstance(turn, int)
                self.kept = {}

            def on(self, lag):
                return not self.fixed or 0 <= self.n - lag < self.count

            def tile(self, lag):
                return self.n - lag

            def par(self, lag, of=2):
                return (self.q - lag) % of

            def done(self, lag):
                if self.fixed:
                    return self.n - lag + 1
                if lag not in self.kept:
                    self.kept[lag] = self.eng.snap(self.n - lag + 1)
                return self.kept[lag]

            def dma(self, lag, of=2):
                return (self.turn * (self.unroll // of) + (self.q - lag) // of + 1) * 16

            def wait(self, name, lag):
                if self.on(lag):
                    self.eng.wait_ge(s[name], self.done(lag))

        A0, A1, A2, B, TT, C1, C2 = range(7)
        GP_K, GP_V = (1, 2, 3), (1, 2, 3)
        STEPS = NT + C2
        HEAD = 8

        def pipeline(eng, step):
            for n in range(HEAD):
                step(Step(eng, n // 2, n % 2))
            with eng.Fori(HEAD // 2, NT // 2) as half:
                for q in range(2):
                    step(Step(eng, half, q))
            for n in range(NT, STEPS):
                step(Step(eng, n // 2, n % 2))

        UNROLL = 8
        SCATTER = 6

        def row_tiles(eng, step):
            for n in range(UNROLL):
                step(Step(eng, 0, n, UNROLL, MT))
            with eng.Fori(1, MT // UNROLL) as turn:
                for q in range(UNROLL):
                    step(Step(eng, turn, q, UNROLL, MT))
            for n in range(SCATTER):
                step(Step(eng, MT // UNROLL, n, UNROLL, MT))

        def token_tiles(eng, step):
            for q in range(4):
                step(Step(eng, 0, q, 4))
            with eng.Fori(1, NT // 4) as turn:
                for q in range(4):
                    step(Step(eng, turn, q, 4))

        def gate(eng, tick):
            eng.sem_inc(tick, 1)

        choices = eo_d[0:PAD, :].rearrange("(n k) d -> n k d", k=TOPK)

        block = ctx.enter_context(nc.Block())

        @block.sync
        def _(sp):
            sp.dma_start(w_nat[:, 0, :, :], a["wq"].rearrange("(k p) d -> p k d", p=P)).then_inc(s["fold_in"], 16)
            sp.dma_start(w_nat[:, 1, :, :], a["wk"].rearrange("(k p) d -> p k d", p=P)).then_inc(s["fold_in"], 16)
            for n, name in enumerate(("fq1", "fq2", "fk1", "fk2")):
                sp.dma_start(f_t[:, n, :], a[name]).then_inc(s["fold_in"], 16)
            sp.dma_start(f_b[:], a["fb"]).then_inc(s["fold_in"], 16)
            sp.dma_start(hn_w[:], a["hn_w"]).then_inc(s["fold_in"], 16)
            sp.dma_start(w_o_raw[:], a["woT"].rearrange("(k p) d -> p k d", p=P)).then_inc(s["fold_in"], 16)
            def load_tile(t, par):
                sp.dma_start(x_t[:, par, :], x_d[bass.ds(t * P, P), :]).then_inc(x_in[par], 16)
                sp.dma_start(c_t[:, par, :, :], ctxT_d[:, :, bass.ds(t * P, P)]).then_inc(c_in[par], 16)
            for t in range(2):
                load_tile(t, t)
            sp.dma_start(w_v[:], a["wvT"].rearrange("(k p) d -> p k d", p=P)).then_inc(s["w_in"], 16)
            sp.dma_start(W_q[:], a["WqT"].rearrange("(k p) d -> p k d", p=P)).then_inc(s["w_in"], 16)
            sp.dma_start(W_kv[:, :, 0, :], a["WkT"].rearrange("(k p) d -> p k d", p=P)).then_inc(s["w_in"], 16)
            sp.dma_start(W_kv[:, :, 1, :], a["WvT"].rearrange("(k p) d -> p k d", p=P)).then_inc(s["w_in"], 16)
            sp.dma_start(W_o[:], a["WoT"].rearrange("(k p) d -> p k d", p=P)).then_inc(s["w_in"], 16)
            sp.dma_start(b_x[:], a["xb"].rearrange("(o n) d -> o n d", o=1).to_broadcast([P, 4, D])).then_inc(s["w_in"], 16)
            sp.dma_start(nw[:], a["nw"].to_broadcast([P, D])).then_inc(s["w_in"], 16)
            sp.dma_start(w_gate[:], a["gateT"].rearrange("(k p) e -> p k e", p=P)).then_inc(s["w_in"], 16)
            sp.dma_start(w_sgu[:, :, 0, :], a["sg"].rearrange("(k p) f -> p k f", p=P)).then_inc(s["w_in"], 16)
            sp.dma_start(w_sgu[:, :, 1, :], a["su"].rearrange("(k p) f -> p k f", p=P)).then_inc(s["w_in"], 16)
            sp.dma_start(w_sd[:], a["sd"]).then_inc(s["w_in"], 16)

            sp.wait_ge(s["setup_done"], 1)
            sp.wait_ge(s["fold_done"], 4)
            sp.dma_start(list_d[0:E * CAP, :].rearrange("(p c) o -> p (c o)", p=P), pad_i[:]).then_inc(s["zero_in"], 16)

            def load_experts(e):
                sp.dma_start(w13[:, e:e + E // HEAD, :, :],
                             a["w13"][e:e + E // HEAD].rearrange("e (k p) f -> p e k f", p=P)).then_inc(s["experts_in"], 16)
                sp.dma_start(w2[:, e:e + E // HEAD, :], a["w2"][e:e + E // HEAD].rearrange("e p d -> p e d")
                             ).then_inc(s["experts_in"], 16)

            def step(st):
                if not st.fixed or 2 <= st.n < NT:
                    st.wait("x1_ok", A2)
                    gate(sp, s["tick"])
                    sp.dma_start(x_t[:, st.q, :], x_d[bass.ds(st.n * P, P), :]).then_inc(x_in[st.q], 16)
                if not st.fixed or 2 <= st.n < NT:
                    st.wait("kv_ps", A2)
                    gate(sp, s["tick"])
                    sp.dma_start(c_t[:, st.q, :, :], ctxT_d[:, :, bass.ds(st.n * P, P)]).then_inc(c_in[st.q], 16)
                if st.on(C1):
                    st.wait("h_ok", C1)
                    gate(sp, s["tick"])
                    sp.dma_start(h_d[bass.ds(st.tile(C1) * P, P), :], hrow[:, st.par(C1), :]).then_inc(h_out[st.par(C1)], 16)
                if st.on(C2):
                    st.wait("acc_ok", C2)
                    gate(sp, s["tick"])
                    sp.dma_start(acc_d[bass.ds(st.tile(C2) * P, P), :], acc[:, st.par(C2), :]).then_inc(acc_out[st.par(C2)], 16)
                if st.fixed and st.n < HEAD:
                    load_experts(st.n * (E // HEAD))

            pipeline(sp, step)

            sp.wait_ge(sent[0], 16 * TOPK * (NT // 2))
            sp.wait_ge(sent[1], 16 * TOPK * (NT // 2))
            sp.dma_start(list_i[0:ER, :, :], list_d[0:E * CAP, :].rearrange("(c r p) o -> r c (p o)", c=EC, p=P)
                         ).then_inc(s["lists_in"], 16)

            def load_tile3(n, buf):
                sp.dma_start(er[:, buf, :, :], choices[bass.ds(n * P, P)]).then_inc(er_in[buf], 16)
                sp.dma_start(acc_p[:, buf, :], acc_d[bass.ds(n * P, P), :]).then_inc(er_in[buf], 16)

            for par in range(2):
                sp.wait_ge(acc_out[par], 16 * (NT // 2))
            sp.wait_ge(s["rows_ready"], 1)
            for buf in range(4):
                load_tile3(buf, buf)

            def finish(st):
                sp.wait_ge(s["fin_ok"], st.done(0))
                gate(sp, s["tick"])
                sp.dma_start(out_d[bass.ds(st.n * P, P), :], fin[:, st.q, :]).then_inc(out_done[st.q], 16)
                if not st.fixed or st.n + 4 < NT:
                    load_tile3(st.n + 4, st.q)

            with sp.Fori(0, NT // 4 - 1) as turn:
                for q in range(4):
                    finish(Step(sp, turn, q, 4))
            for n in range(NT - 4, NT):
                finish(Step(sp, n // 4, n % 4, 4))
            for n in range(4):
                sp.wait_ge(out_done[n], 16 * (NT // 4))

        @block.tensor
        def _(pe):
            mm = nc.tensor.matmul

            pe.wait_ge(s["fold_in"], 16 * 9)
            pe.wait_ge(s["c_bd"], 1)
            for n in range(4):
                if n >= 2:
                    pe.wait_ge(s["fold_done"], n - 1)
                bank = S[:, n % 2, :].rearrange("p (k d) -> p k d", k=KC)
                for k in range(KC):
                    for c in range(KC):
                        last = mm(bank[:, k, c * P:(c + 1) * P], w_nat[:, n // 2, c, k * P:(k + 1) * P],
                                  f_bd[:, n, :], start=True, stop=True)
                last.then_inc(s["fold_ps"], 1)
            pe.wait_ge(s["setup_done"], 1)
            pe.wait_ge(s["fold_done"], 4)
            pe.wait_ge(s["w_in"], 16 * 11)

            def flip(bank, src, done):
                for k in range(KC):
                    last = nc.tensor.transpose(bank[:, k * P:(k + 1) * P], src[:, k * P:(k + 1) * P], ident[:])
                last.then_inc(s[done], 1)

            def project(bank, lhs, w, done):
                for k in range(KC):
                    last = mm(bank, lhs[:, k, :], w[:, k], start=(k == 0), stop=(k == KC - 1))
                last.then_inc(s[done], 1)

            def step(st):
                if st.on(A1):
                    st.wait("xT_ok", A1)
                    for n, bank, done in ((0, QQ, "q_ps"), (2, KK, "k_ps")):
                        if n == 2:
                            st.wait("kp_ok", A1 + 1)
                        for f in range(2):
                            for c in range(KC):
                                for k in range(KC):
                                    last = mm(bank[:, (f * KC + c) * P:(f * KC + c + 1) * P],
                                              w_f[:, n + f, k, c * P:(c + 1) * P], xT[:, k, :],
                                              start=(k == 0), stop=(k == KC - 1))
                        last.then_inc(s[done], 1)
                if st.on(C1):
                    st.wait("att_ok", C1)
                    st.wait("s_ok", A2)
                    st.wait("Q_cp", B + 1)
                    flip(S[:, 1, :], att, "attT_ps")
                if st.on(B):
                    st.wait("x1n_ok", B)
                    st.wait("topi_ok", C2)
                    st.wait("act_ok", C2)
                    flip(TB, x1n, "x1T_ps")
                if st.on(C1):
                    st.wait("attT_ok", C1)
                    st.wait("s_ok", A2)
                    st.wait("v_ok", A1 + 1)
                    project(S[:, 2, 0:D], attT, W_o, "Wo_ps")
                if st.on(A2):
                    st.wait("oT_ok", A2)
                    project(S[:, 3, 0:D], oT, w_o, "wo_ps")
                if st.on(B):
                    st.wait("x1T_ok", B)
                    st.wait("attT_ok", C1)
                    project(S[:, 1, 0:D], x1T, W_q, "Q_ps")
                if st.on(A1):
                    st.wait("x2_ok", C1)
                    st.wait("s_ok", A2)
                    project(S[:, 2, 0:D], xT, w_v, "v_ps")
                if st.on(C2):
                    st.wait("act_ok", C2)
                    st.wait("x1T_ok", B)
                    mm(TB[:, 0:D], act_s[:], w_sd[:], start=True, stop=True).then_inc(s["dn_ps"], 1)
                    st.wait("mask_ok", C2)
                    st.wait("seen_ok", C2 + 1)
                    st.wait("Q_cp", B)
                    mm(S[:, 1, 0:E], before[:], mask_h[:], start=True, stop=False)
                    mm(S[:, 1, 0:E], ones_h[:], seen[:, st.par(C2), :], start=False, stop=True).then_inc(s["pos_ps"], 1)
                if st.on(A2):
                    pe.wait_ge(c_in[st.par(A2)], st.dma(A2))
                    st.wait("kv_cp", B)
                    project(TA[:], c_t[:, st.par(A2)], W_kv[:].rearrange("p k n d -> p k (n d)"), "kv_ps")
                if st.on(A1):
                    st.wait("qf_ok", A1)
                    st.wait("kf_ok", A1)
                    st.wait("oT_ok", A2)
                    st.wait("Q_cp", B)
                    st.wait("pk_ok", C2)
                    st.wait("v_ok", A1)
                    st.wait("x1_ok", A2)
                    for b in range(2):
                        for c in range(KC):
                            for j in range(4):
                                r = slice(32 * j, 32 * j + 32)
                                last = mm(S[:, j, (b * KC + c) * L:(b * KC + c + 1) * L],
                                          kblk[r, c * 2 + b].rearrange("p m l -> p (m l)"), qf[r, c, b * L:(b + 1) * L],
                                          start=True, stop=True)
                    last.then_inc(s["s_ps"], 1)
                if st.on(C1):
                    st.wait("h_ok", C1)
                    st.wait("acc_ok", C2)
                    st.wait("x1T_ok", B)
                    flip(TB, hrow[:, st.par(C1), :], "hT_ps")
                if st.on(C1):
                    st.wait("hT_ok", C1)
                    for f in range(2):
                        for k in range(KC):
                            mm(TB[:, f * P:(f + 1) * P], w_sgu[:, k, f, :], hT[:, k, :],
                               start=(k == 0), stop=(k == KC - 1))
                    project(TB[:, D:D + E], hT, w_gate, "gu_ps")
                if st.on(A0):
                    st.wait("xn_ok", A0)
                    st.wait("qf_ok", A1)
                    flip(QQ, xn, "xT_ps")
                if st.on(A1):
                    st.wait("oT_ok", A2)
                    st.wait("s_ok", A1)
                    st.wait("v_ok", A1)
                    for b in range(2):
                        for c in range(KC):
                            for j in range(4):
                                last = mm(S[32 * j:32 * j + 32, 0, c * P + b * L:c * P + (b + 1) * L],
                                          vblk[:, b, 4 * c + j, :], sm[:, j, b * KC + c, :], start=True, stop=True)
                    last.then_inc(s["o_ps"], 1)
                if st.on(A1):
                    st.wait("osq_ok", A1)
                    mm(S[:, 0, D:2 * D], headmask[:], osq[:], start=True, stop=True).then_inc(s["ms_ps"], 1)

            pipeline(pe, step)

            pe.wait_ge(s["seen_ok"], NT)
            mm(TA[0:E, 0:1], seen[:, 0, :], ones_h[:, 0:1], start=True, stop=True).then_inc(s["table_ps"], 1)
            pe.wait_ge(s["table_ok"], 1)
            mm(TA[:, 0:1], ones[0:E, :], over_e[:], start=True, stop=True)
            for c in range(EC):
                mm(QQ[0:ER, c:c + 1], r_lt[:, c * ER:(c + 1) * ER], nt_c[:], start=True, stop=True)
                last = mm(KK[0:ER, c:c + 1], r_eq[:, c * ER:(c + 1) * ER], nt_c[:], start=True, stop=True)
            last.then_inc(s["table_ps"], 1)
            pe.wait_ge(s["table_ok"], 2)
            pe.wait_ge(s["table_ok"], 3)
            for c in range(EC):
                mm(S[:, 0, 0:MT], list_f[0:ER, c, :], hot[0:ER, c, :], start=(c == 0), stop=(c == EC - 1))
            for c in range(EC):
                mm(S[0:2, 1, 0:MT], ecol[0:ER, c, :], hot[0:ER, c, :], start=(c == 0), stop=(c == EC - 1))
            for c in range(EC):
                mm(S[:, 3, 0:E], ones[0:ER, :], past[0:ER, c, :], start=(c == 0), stop=(c == EC - 1))
            for c in range(EC):
                last = mm(S[:, 2, 0:MT], ones[0:ER, :], hot[0:ER, c, :], start=(c == 0), stop=(c == EC - 1))
            last.then_inc(s["table_ps"], 1)
            pe.wait_ge(s["plan_ok"], 1)
            pe.wait_ge(s["experts_in"], 16 * 2 * HEAD)

            def expert(st, lag):
                return pe.value_load(eid[0:1, bass.ds(st.tile(lag), 1)], min_val=0, max_val=E - 1)

            held = {}

            def step2(st):
                if st.q == 0:
                    held.clear()
                    if st.on(1):
                        held[-1] = expert(st, 1)
                if st.on(0):
                    pe.wait_ge(g_in[st.par(0, 4)], st.dma(0, 4))
                    st.wait("gx_ok", 2)
                    flip((TA, TB)[st.par(0)], xg[:, st.par(0, 4), :], "gx_ps")
                if st.on(1):
                    e = held[st.q - 1]
                    st.wait("gx_ok", 1)
                    st.wait("ag_ok", 3)
                    bank = (QQ, KK)[st.par(1)]
                    for k in range(KC):
                        last = mm(bank[:, 0:D], xgT[:, st.par(1), k, :],
                                  w13[:, bass.ds(e, 1), k, :].rearrange("p o f -> p (o f)"),
                                  start=(k == 0), stop=(k == KC - 1))
                    last.then_inc(s["gg_ps"], 1)
                if st.q == 0:
                    for lag in (3, 2):
                        if st.on(lag):
                            held[-lag] = expert(st, lag)
                if st.on(0) and st.q < UNROLL - 1:
                    held[st.q] = expert(st, 0)
                if st.on(2):
                    st.wait("ag_ok", 2)
                    st.wait("agT_ok", 4)
                    nc.tensor.transpose(S[:, st.par(2), 0:P], ag[:, st.par(2), :], ident[:]).then_inc(s["agT_ps"], 1)
                if st.on(3):
                    e = held[st.q - 3]
                    st.wait("agT_ok", 3)
                    st.wait("eo_ok", 5)
                    mm(S[:, 2 + st.par(3), 0:D], agT[:, st.par(3), :],
                       w2[:, bass.ds(e, 1), :].rearrange("p o d -> p (o d)"), start=True, stop=True
                       ).then_inc(s["dn2_ps"], 1)

            row_tiles(pe, step2)

        @block.scalar
        def _(act):
            A_ = nc.scalar.activation
            act.preload_act_table_set("natural_log_exp_and_others")
            for n in range(4):
                act.wait_ge(s["fold_ps"], n + 1)
                nc.scalar.copy(w_f[:, n, :, :], S[:, n % 2, :].rearrange("p (k d) -> p k d", k=KC)
                               ).then_inc(s["fold_done"], 1)
            act.wait_ge(s["setup_done"], 1)

            def copy(dst_, src, done):
                nc.scalar.copy(dst_, src).then_inc(s[done], 1)

            def rsqrt(dst_, src, e, scale, st, ln, done, stage):
                A_(dst_[0], src, ACT.Ln, bias=e, scale=scale).then_inc(s[ln], 1)
                st.wait(ln, stage)
                A_(dst_[1], dst_[0], ACT.Exp, scale=-0.5).then_inc(s[done], 1)

            def tiles(bank):
                return bank.rearrange("p (k t) -> p k t", t=P)

            def step(st):
                if st.on(B):
                    st.wait("mv_b_ok", B)
                    rsqrt((r_b[:, 0:1], r_b[:, 1:2]), mv_b[:, 1:2], eps[:, 0:1], 1.0, st, "ln_b_ok", "r_b_ok", B)
                if st.on(C1):
                    st.wait("attT_ps", C1)
                    copy(attT[:], tiles(S[:, 1, 0:D]), "attT_ok")
                if st.on(B):
                    st.wait("kv_ps", B)
                    st.wait("kvb_ok", B + 1)
                    nc.scalar.copy(qkv_raw[:, 1, :], TA[:, 0:D])
                    copy(qkv_raw[:, 2, :].rearrange("p (d h) -> p h d", h=H),
                         TA[:, D:2 * D].rearrange("p (h d) -> p h d", h=H), "kv_cp")
                if st.on(A1):
                    st.wait("q_ps", A1)
                    st.wait("qf_ok", A1 + 1)
                    A_(tq[:], tiles(QQ[:, D:2 * D]), ACT.Identity, bias=f_b2[:, 0:1], scale=DK ** -0.5).then_inc(s["tq_ok"], 1)
                    st.wait("k_ps", A1)
                    st.wait("kp_ok", A1 + 1)
                    A_(tk[:], tiles(KK[:, D:2 * D]), ACT.Identity, bias=f_b[:, 3:4]).then_inc(s["tk_ok"], 1)
                if st.on(B):
                    st.wait("x1T_ps", B)
                    copy(x1T[:], tiles(TB[:, 0:D]), "x1T_ok")
                if st.on(B):
                    st.wait("Q_ps", B)
                    st.wait("qb_ok", B + 1)
                    copy(qkv_raw[:, 0, :], S[:, 1, 0:D], "Q_cp")
                if st.on(C1):
                    st.wait("mv_c_ok", C1)
                    rsqrt((r_c[:, 0:1], r_c[:, 1:2]), mv_c[:, 1:2], eps[:, 0:1], 1.0, st, "ln_c_ok", "r_c_ok", C1)
                if st.on(A1):
                    st.wait("kp_ok", A1)
                    st.wait("s_ps", A1 + 1)
                    for m_ in range(2):
                        last = A_(kblk[:, :, m_, :], kf[:].rearrange("p k (b l) -> p (k b) l", l=L), ACT.Identity,
                                  scale=parmask[:, m_:m_ + 1])
                    last.then_inc(s["kf_ok"], 1)
                if st.on(C2):
                    st.wait("dl_ok", C2)
                    A_(ew[:], dl[:], ACT.Exp, accum_out=es[:]).then_inc(s["ew_ok"], 1)
                if st.on(C1):
                    st.wait("v2_ok", C1)
                    rsqrt((r2[:, 0:1], r2[:, 1:2]), v2[:], eps[:, 1:2], 1.0, st, "ln_2_ok", "r2_ok", C1)
                if st.on(A1):
                    st.wait("v_ps", A1)
                    st.wait("o_ps", A1 + 1)
                    for b in range(2):
                        for h in range(2):
                            last = nc.scalar.copy(
                                vblk[h * L:(h + 1) * L, b, :, h * DK:(h + 1) * DK],
                                S[b * L:(b + 1) * L, 2, 0:D].rearrange("p (g h d) -> p g h d", h=2, d=DK)[:, :, h, :])
                    last.then_inc(s["v_ok"], 1)
                if st.on(TT):
                    st.wait("scm_ok", TT)
                    st.wait("ao_ok", TT + 1)
                    A_(pr[:], scm[:], ACT.Exp).then_inc(s["pr_ok"], 1)
                if st.on(A0):
                    st.wait("mv_a_ok", A0)
                    rsqrt((r_a[:, 0:1], r_a[:, 1:2]), mv_a[:, 1:2], eps[:, 0:1], 1.0, st, "ln_a_ok", "r_a_ok", A0)
                if st.on(C1):
                    st.wait("hT_ps", C1)
                    copy(hT[:], tiles(TB[:, 0:D]), "hT_ok")
                if st.on(A0):
                    st.wait("xT_ps", A0)
                    copy(xT[:], tiles(QQ[:, 0:D]), "xT_ok")
                if st.on(C1):
                    st.wait("gu_ps", C1)
                    A_(eg[:], TB[:, 0:P], ACT.Exp, scale=-1.0).then_inc(s["eg_ok"], 1)
                    st.wait("eg_ok", C1)
                    A_(gs[:], eg[:], ACT.Ln, bias=ones[:, 0:1]).then_inc(s["lne_ok"], 1)
                    st.wait("lne_ok", C1)
                    A_(eg[:], gs[:], ACT.Exp, scale=-1.0).then_inc(s["sig_ok"], 1)
                if st.on(A1):
                    st.wait("o_ps", A1)
                    A_(osq[:], S[:, 0, 0:D], ACT.Square).then_inc(s["osq_ok"], 1)
                if st.on(A1):
                    st.wait("ms_ps", A1)
                    rsqrt((osq[:], r_o[:]), S[:, 0, D:2 * D], eps[:, 0:1], 1.0 / DK, st, "ln_o_ok", "r_o_ok", A1)

            pipeline(act, step)

            act.wait_ge(s["plan_ok"], 1)

            def rows_of(st_n, buf):
                nc.scalar.copy(gcol[:, buf:buf + 1], rows_u[:, bass.ds(st_n, 1), 0]).then_inc(s["gcol_ok"], 1)

            for n in range(3):
                rows_of(n, n)

            def step2(st):
                if st.on(0):
                    st.wait("gx_ps", 0)
                    st.wait("gg_ps", 2)
                    copy(xgT[:, st.par(0)], tiles((TA, TB)[st.par(0)][:, 0:D]), "gx_ok")
                    rows_of(st.n + 3, (st.q + 3) % 4)
                    if st.on(8):
                        act.wait_ge(eo_out[st.par(8, 4)], st.dma(8, 4))
                        gate(act, s["tick"])
                    nc.scalar.copy(dcol[:, st.q:st.q + 1], rows_u[:, bass.ds(st.n, 1), 1])
                if st.on(1):
                    st.wait("gg_ps", 1)
                    st.wait("ag_ok", 3)
                    A_(sg[:, st.par(1), :], (QQ, KK)[st.par(1)][:, 0:FF], ACT.Silu).then_inc(s["sg_ok"], 1)
                if st.on(2):
                    st.wait("agT_ps", 2)
                    st.wait("dn2_ps", 4)
                    copy(agT[:, st.par(2), :], S[:, st.par(2), 0:P], "agT_ok")

            row_tiles(act, step2)

            def step3(st):
                st.wait("fin_ok", 2)
                nc.scalar.copy(wcol[:, st.par(0), :], route[:, bass.ds(st.n, 1), 2, :].rearrange("p o k -> p (o k)")
                               ).then_inc(s["wcol_ok"], 1)

            token_tiles(act, step3)

        @block.vector
        def _(v):
            tt = nc.vector.tensor_tensor
            ts = nc.vector.tensor_scalar
            stt = nc.vector.scalar_tensor_tensor

            links = [0]

            def link():
                links[0] += 1
                v.wait_ge(s["linked"], links[0])

            v.wait_ge(s["c_setup"], 1)
            v.wait_ge(s["fold_in"], 16 * 9)
            for n in range(4):
                last = tt(f_bd[:, n, :], f_t[:, n, :], headmask[:], ALU.mult)
            last.then_inc(s["c_bd"], 1)
            for k in range(KC):
                ts(w_o[:, k, :], w_o_raw[:, k, :], hn_w[:, 0:1], None, ALU.mult)
            ts(f_b2[:, 0:1], f_b[:, 1:2], DK ** -0.5, None, ALU.mult)
            nc.vector.tensor_reduce(parmask[:, 0:1], evens[:], X, ALU.add).then_inc(s["linked"], 1)
            link()
            ts(parmask[:, 1:2], parmask[:, 0:1], -1.0, 1.0, ALU.mult, ALU.add)
            ts(jend[:], expert_row[:], float(J), float(J), ALU.mult, ALU.add).then_inc(s["linked"], 1)
            link()
            for c in range(EC):
                last = ts(past[:, c, :], jend[:], rcol[:, c:c + 1], None, ALU.is_le)
            last.then_inc(s["linked"], 1)
            link()
            for n in range(2):
                last = nc.vector.tensor_reduce(ecol[:, :, n], past[:], X, ALU.add)
            last.then_inc(s["linked"], 1)
            link()
            stt(jcol[:], ecol[:, :, 0], -float(J), rcol[:], ALU.mult, ALU.add)
            nc.vector.memset(seen[:, 0, :], 0.0)
            nc.vector.memset(vblk[:], 0.0).then_inc(s["setup_done"], 1)
            v.wait_ge(s["setup_done"], 1)
            v.wait_ge(s["w_in"], 16 * 11)

            def heads(ap):
                return ap.rearrange("p (h d) -> p h d", h=H)

            def step(st):
                at = st.par(TT)

                def k_mult(c):
                    if c == 0:
                        st.wait("ao_ok", TT + 1)
                    q_ = qkv[:, at, 0, :].rearrange("p (h o d) -> p h o d", h=H, o=1)[:, c * HC:(c + 1) * HC]
                    k_ = qkv[:, at, 1, :].rearrange("p (o g d) -> p o g d", g=H, o=1)
                    last = tt(prod[:, c, :].rearrange("p (h g d) -> p h g d", h=HC, g=H),
                       q_.to_broadcast([P, HC, H, DK]), k_.to_broadcast([P, HC, H, DK]), ALU.mult)
                    last.then_inc(s[f"kp{c}"], 1)

                def k_sum(c):
                    st.wait(f"kp{c}", TT)
                    last = nc.vector.tensor_reduce(
                        sc[:, c * HC:(c + 1) * HC, :],
                        prod[:, c, :].rearrange("p (h g d) -> p h g d", h=HC, g=H), X, ALU.add)
                    if c == NCH - 1:
                        last.then_inc(s["sc_ok"], 1)

                def v_mult(c):
                    if c == 0:
                        st.wait("sc_ok", TT)
                    p_ = pr[:, c * HC:(c + 1) * HC, :].rearrange("p h (o g) -> p h o g", o=1)
                    v_ = qkv[:, at, 2, :].rearrange("p (o d g) -> p o d g", g=H, o=1)
                    last = tt(prod[:, c, :].rearrange("p (h d g) -> p h d g", h=HC, g=H),
                       p_.to_broadcast([P, HC, DK, H]), v_.to_broadcast([P, HC, DK, H]), ALU.mult)
                    last.then_inc(s[f"vp{c}"], 1)

                def v_sum(c):
                    st.wait(f"vp{c}", TT)
                    last = nc.vector.tensor_reduce(
                        ao[:, c * HC:(c + 1) * HC, :],
                        prod[:, c, :].rearrange("p (h d g) -> p h d g", h=HC, g=H), X, ALU.add)
                    if c == NCH - 1:
                        last.then_inc(s["ao_ok"], 1)

                T_ = st.on(TT)
                if st.on(B):
                    st.wait("x1_ok", B)
                    nc.vector.bn_stats(st_b[:], x1[:, st.par(B), :]).then_inc(s["st_b_ok"], 1)
                if T_:
                    st.wait("kvb_ok", TT)
                    st.wait("qb_ok", TT)
                    k_mult(0)
                if st.on(B):
                    st.wait("st_b_ok", B)
                    gate(v, s["tick"])
                    nc.vector.bn_aggr(mv_b[:], st_b[:]).then_inc(s["mv_b_ok"], 1)
                if st.on(C2):
                    st.wait("sig_ok", C2)
                    tt(gs[:], TB[:, 0:P], eg[:], ALU.mult).then_inc(s["gs_ok"], 1)
                    st.wait("gs_ok", C2)
                    tt(act_s[:], TB[:, P:2 * P], gs[:], ALU.mult).then_inc(s["act_ok"], 1)
                if st.on(B):
                    st.wait("r_b_ok", B)
                    ts(x1n[:], x1[:, st.par(B), :], mv_b[:, 0:1], r_b[:, 1:2], ALU.subtract, ALU.mult
                       ).then_inc(s["x1n_ok"], 1)
                if st.on(C2):
                    st.wait("topi_ok", C2)
                    nc.vector.tensor_copy(topf[:], topi[:, 0:TOPK]).then_inc(s["topf_ok"], 1)
                    st.wait("topf_ok", C2)
                    tt(oh[:], expert_row[:].rearrange("p (o e) -> p o e", o=1).to_broadcast([P, TOPK, E]),
                       topf[:].rearrange("p (k o) -> p k o", o=1).to_broadcast([P, TOPK, E]), ALU.is_equal
                       ).then_inc(s["oh_ok"], 1)
                if st.on(A2):
                    st.wait("r_o_ok", A2)
                    tt(oT[:].rearrange("p k t -> p (k t)"), S[:, 0, 0:D], r_o[:], ALU.mult).then_inc(s["oT_ok"], 1)
                if T_:
                    k_sum(0)
                if st.on(C2):
                    st.wait("oh_ok", C2)
                    st.wait("seen_ok", C2 + 1)
                    with nc.allow_low_precision(reason="zeros and ones"):
                        nc.vector.tensor_reduce(mask_h[:], oh[:].rearrange("p k e -> p e k"), X, ALU.add
                                                ).then_inc(s["mask_ok"], 1)
                if T_:
                    k_sum(1)
                if st.on(A1):
                    st.wait("tq_ok", A1)
                    st.wait("s_ps", A1 + 1)
                    stt(qf[:], QQ[:, 0:D].rearrange("p (k t) -> p k t", t=P), f_b[:, 0:1], tq[:], ALU.add, ALU.mult
                        ).then_inc(s["qf_ok"], 1)
                if st.on(C1):
                    st.wait("Wo_ps", C1)
                    st.wait("xb_ok", C1)
                    st.wait("res_ok", C1 + 1)
                    tt(x2[:], xb[:, st.par(C1), :], S[:, 2, 0:D], ALU.add).then_inc(s["x2_ok"], 1)
                    st.wait("x2_ok", C1)
                    nc.vector.bn_stats(st_c[:], x2[:]).then_inc(s["st_c_ok"], 1)
                if st.on(A2):
                    st.wait("wo_ps", A2)
                    st.wait("xb_ok", A2 + 2)
                    tt(x1[:, st.par(A2), :], x_t[:, st.par(A2), :], S[:, 3, 0:D], ALU.add).then_inc(s["x1_ok"], 1)
                if st.on(C1):
                    st.wait("st_c_ok", C1)
                    gate(v, s["tick"])
                    nc.vector.bn_aggr(mv_c[:], st_c[:]).then_inc(s["mv_c_ok"], 1)
                if st.on(A1):
                    st.wait("tk_ok", A1)
                    st.wait("kf_ok", A1 + 1)
                    stt(kf[:], KK[:, 0:D].rearrange("p (k t) -> p k t", t=P), f_b[:, 2:3], tk[:], ALU.add, ALU.mult
                        ).then_inc(s["kp_ok"], 1)
                if T_:
                    k_sum(2)
                if st.on(C1):
                    st.wait("r_c_ok", C1)
                    stt(v2[:], mv_c[:, 1:2], r_c[:, 1:2], r_c[:, 1:2], ALU.mult, ALU.mult).then_inc(s["v2_ok"], 1)
                    ts(y[:], x2[:], mv_c[:, 0:1], r_c[:, 1:2], ALU.subtract, ALU.mult).then_inc(s["y_ok"], 1)
                if st.on(C2):
                    st.wait("dn_ps", C2)
                    st.wait("res_ok", C2)
                    if st.on(C2 + 2):
                        v.wait_ge(acc_out[st.par(C2)], st.dma(C2 + 2))
                    tt(acc[:, st.par(C2), :], res[:, st.par(C2), :], TB[:, 0:D], ALU.add
                       ).then_inc(s["acc_ok"], 1)
                    st.wait("pos_ps", C2)
                    tt(pk[:], oh[:], S[:, 1, 0:E].rearrange("p (o e) -> p o e", o=1).to_broadcast([P, TOPK, E]), ALU.mult
                       ).then_inc(s["pk_ok"], 1)
                    tt(seen[:, 1 - st.par(C2), :], seen[:, st.par(C2), :], mask_h[:], ALU.add).then_inc(s["seen_ok"], 1)
                if T_:
                    k_sum(3)
                if st.on(C1):
                    st.wait("r2_ok", C1)
                    st.wait("y_ok", C1)
                    if st.on(C1 + 2):
                        v.wait_ge(h_out[st.par(C1)], st.dma(C1 + 2))
                    st.wait("hT_ps", C1 + 2)
                    stt(hrow[:, st.par(C1), :], y[:], r2[:, 1:2], nw[:], ALU.mult, ALU.mult).then_inc(s["h_ok"], 1)
                if st.on(C2):
                    st.wait("ew_ok", C2)
                    nc.vector.reciprocal(rs[:], es[:]).then_inc(s["rs_ok"], 1)
                if T_:
                    st.wait("sc_ok", TT)
                    nc.vector.tensor_reduce(mx[:], sc[:], X, ALU.max).then_inc(s["mx_ok"], 1)
                if st.on(C2):
                    st.wait("pk_ok", C2)
                    nc.vector.tensor_reduce(pos[:], pk[:], X, ALU.add).then_inc(s["pos_ok"], 1)
                if T_:
                    st.wait("mx_ok", TT)
                    tt(scm[:], sc[:], mx[:].rearrange("p (h o) -> p h o", o=1).to_broadcast([P, H, H]), ALU.subtract
                       ).then_inc(s["scm_ok"], 1)
                if st.on(C2):
                    rt = lambda n: route[:, bass.ds(st.tile(C2), 1), n, :].rearrange("p o k -> p (o k)")
                    st.wait("pos_ok", C2)
                    ts(over[:], pos[:], float(CAP), None, ALU.is_ge)
                    stt(row[:], topf[:], float(CAP), pos[:], ALU.mult, ALU.add).then_inc(s["row_ok"], 1)
                    ts(rt(1), pos[:], float(CAP), None, ALU.is_ge)
                    ts(rt(0), topf[:], 1.0, None, ALU.mult)
                    st.wait("row_ok", C2)
                    tt(gap[:], trash_row[:, bass.ds(st.tile(C2), 1), :].rearrange("p o k -> p (o k)"), row[:], ALU.subtract
                       ).then_inc(s["gap_ok"], 1)
                    st.wait("rs_ok", C2)
                    ts(rt(2), ew[:], rs[:, 0:1], None, ALU.mult)
                if st.on(A0):
                    v.wait_ge(x_in[st.par(A0)], st.dma(A0))
                    gate(v, s["tick"])
                    nc.vector.bn_stats(st_a[:], x_t[:, st.par(A0), :]).then_inc(s["st_a_ok"], 1)
                    st.wait("st_a_ok", A0)
                    gate(v, s["tick"])
                    nc.vector.bn_aggr(mv_a[:], st_a[:]).then_inc(s["mv_a_ok"], 1)
                if T_:
                    st.wait("pr_ok", TT)
                    v_mult(0)
                if st.on(C2):
                    st.wait("gap_ok", C2)
                    tt(over[:], over[:], gap[:], ALU.mult).then_inc(s["gapo_ok"], 1)
                    if st.on(C2 + 2):
                        v.wait_ge(sent[st.par(C2)], st.dma(C2 + 2) * TOPK)
                        gate(v, s["tick"])
                    nc.vector.tensor_copy(tid[:, st.par(C2), :], number[:, bass.ds(st.tile(C2), 1), :].rearrange("p o k -> p (o k)"))
                    st.wait("gapo_ok", C2)
                    tt(slot[:, st.par(C2), :], row[:], over[:], ALU.add).then_inc(s["slot_ok"], 1)
                if st.on(A0):
                    st.wait("r_a_ok", A0)
                    ts(xn[:], x_t[:, st.par(A0), :], mv_a[:, 0:1], r_a[:, 1:2], ALU.subtract, ALU.mult
                       ).then_inc(s["xn_ok"], 1)
                if T_:
                    v_sum(0)
                if st.on(A1):
                    st.wait("s_ps", A1)
                    st.wait("o_ps", A1 + 1)
                    tt(sm[:].rearrange("p j c l -> p j (c l)"), S[:, :, 0:2 * KC * L],
                       causal4(causal), ALU.mult).then_inc(s["s_ok"], 1)
                if T_:
                    v_sum(1)
                    nc.vector.tensor_reduce(psm[:], pr[:], X, ALU.add).then_inc(s["psm_ok"], 1)
                    v_sum(2)
                    st.wait("psm_ok", TT)
                    nc.vector.reciprocal(pri[:], psm[:]).then_inc(s["pri_ok"], 1)
                if st.on(C1):
                    st.wait("eg_ok", C1)
                    gate(v, s["tick"])
                    nc.vector.max(top[:], TB[:, D:D + E]).then_inc(s["top_ok"], 1)
                if T_:
                    v_sum(3)
                if st.on(C1):
                    st.wait("top_ok", C1)
                    gate(v, s["tick"])
                    nc.vector.max_index(topi[:], top[:], TB[:, D:D + E]).then_inc(s["topi_ok"], 1)
                    ts(dl[:], top[:, 0:TOPK], top[:, 0:1], None, ALU.subtract).then_inc(s["dl_ok"], 1)
                if T_:
                    st.wait("ao_ok", TT)
                    st.wait("pri_ok", TT)
                    st.wait("attT_ps", TT + 1)
                    tt(heads(att[:]), ao[:], pri[:].rearrange("p (h o) -> p h o", o=1).to_broadcast([P, H, DK]), ALU.mult
                       ).then_inc(s["att_ok"], 1)

            def causal4(m_):
                return m_[:].rearrange("p (j c l) -> p j c l", j=1, c=1).to_broadcast([P, 4, 2 * KC, L])

            pipeline(v, step)

            v.wait_ge(s["table_ps"], 1)
            ts(over_e[:], TA[0:E, 0:1], float(CAP), None, ALU.is_gt)
            ts(cnt_c[:], TA[0:E, 0:1], float(CAP), None, ALU.min).then_inc(s["linked"], 1)
            link()
            ts(have[:], jrow[:], cnt_c[:, 0:1], None, ALU.is_lt).then_inc(s["linked"], 1)
            link()
            nc.vector.tensor_reduce(nt_c[:], have[:], X, ALU.add).then_inc(s["linked"], 1)
            link()
            nc.vector.tensor_copy(nt_b[:], nt_c[:].to_broadcast([E, P])).then_inc(s["table_ok"], 1)
            v.wait_ge(s["table_ps"], 2)
            nc.vector.tensor_copy(over_i[:], TA[:, 0:1])
            tt(dst[0:ER, :], jcol[0:ER, :], QQ[0:ER, 0:EC], ALU.add)
            tt(nov[0:ER, :], jcol[0:ER, :], KK[0:ER, 0:EC], ALU.is_ge).then_inc(s["linked"], 1)
            link()
            stt(dstv[0:ER, :], nov[0:ER, :], float(2 * MT), dst[0:ER, :], ALU.mult, ALU.add).then_inc(s["linked"], 1)
            link()
            for c in range(EC):
                last = ts(hot[0:ER, c, :], tcol[0:ER, :], dstv[0:ER, c:c + 1], None, ALU.is_equal)
            last.then_inc(s["table_ok"], 1)
            v.wait_ge(s["lists_in"], 16)
            nc.vector.tensor_copy(list_f[0:ER], list_i[0:ER])
            ts(last_j[0:ER], jcol[0:ER], float(J - 1), None, ALU.is_equal).then_inc(s["linked"], 1)
            link()
            for c in range(EC):
                last = ts(past[0:ER, c, :], expert_row[0:ER], ecol[0:ER, c, 0:1], last_j[0:ER, c:c + 1], ALU.is_equal, ALU.mult)
            last.then_inc(s["linked"], 1)
            link()
            for c in range(EC):
                last = ts(past[0:ER, c, :], past[0:ER, c, :], list_f[0:ER, c, P - 1:P], None, ALU.mult)
            last.then_inc(s["table_ok"], 1)
            v.wait_ge(s["table_ps"], 3)
            nc.vector.tensor_copy(eid[:, 0:MT], S[0:2, 1, 0:MT])
            v.wait_ge(s["spare_ok"], 1)
            ts(unused[:], S[:, 2, 0:MT], -1.0, 1.0, ALU.mult, ALU.add).then_inc(s["linked"], 1)
            link()
            tt(lack[:], unused[:], spare[:], ALU.mult).then_inc(s["linked"], 1)
            link()
            tt(choice[:], lack[:], S[:, 0, 0:MT], ALU.add).then_inc(s["linked"], 1)
            link()
            nc.vector.tensor_copy(rows_u[:, 0:MT, 1], choice[:])
            ts(rows_u[:, 0:MT, 0], choice[:], float(PAD - 1), None, ALU.min).then_inc(s["linked"], 1)
            link()
            ts(rows_u[:, 0:MT, 0], rows_u[:, 0:MT, 0], 2, None, ALU.logical_shift_right).then_inc(s["plan_ok"], 1)
            any_over = v.value_load(over_i[0:1, 0:1], min_val=0, max_val=E)
            nc.vector.tensor_copy(own_f[:], S[:, 3, 0:E]).then_inc(s["linked"], 1)
            link()

            def step2(st):
                if st.on(1):
                    st.wait("sg_ok", 1)
                    st.wait("agT_ps", 3)
                    tt(ag[:, st.par(1), :], (QQ, KK)[st.par(1)][:, FF:2 * FF], sg[:, st.par(1), :], ALU.mult
                       ).then_inc(s["ag_ok"], 1)
                if st.on(3):
                    st.wait("dn2_ps", 3)
                    if st.on(7):
                        v.wait_ge(eo_out[st.par(3, 4)], st.dma(7, 4))
                        gate(v, s["tick"])
                    nc.vector.tensor_copy(eo[:, st.par(3, 4), :], S[:, 2 + st.par(3), 0:D]).then_inc(s["eo_ok"], 1)

            row_tiles(v, step2)

            with v.If(any_over > 0):
                G = NT // 4
                for c in range(4):
                    tiles_ = slice(c * G, (c + 1) * G)
                    g4 = bk_e[:].rearrange("p (t k) e -> p t k e", k=TOPK)
                    e_in = route[:, tiles_, 0, :].rearrange("p t (k o) -> p t k o", o=1).to_broadcast([P, G, TOPK, E])
                    tt(g4, expert_row[:].rearrange("p (a b e) -> p a b e", a=1, b=1).to_broadcast([P, G, TOPK, E]),
                       e_in, ALU.is_equal).then_inc(s["linked"], 1)
                    link()
                    tt(g4, g4, own_f[:].rearrange("p (a b e) -> p a b e", a=1, b=1).to_broadcast([P, G, TOPK, E]),
                       ALU.mult).then_inc(s["linked"], 1)
                    link()
                    nc.vector.tensor_reduce(cb[:, tiles_, :], g4, X, ALU.add).then_inc(s["linked"], 1)
                    link()
                tt(gap_all[:], cb[:], number[:], ALU.subtract).then_inc(s["linked"], 1)
                link()
                tt(cb[:], gap_all[:], route[:, :, 1, :], ALU.mult).then_inc(s["linked"], 1)
                link()
                tt(cidx[:], cb[:], number[:], ALU.add).then_inc(s["cidx_ok"], 1)

            def step3(st):
                b = st.par(0)
                rows = er[:, st.q]
                v.wait_ge(er_in[st.q], st.dma(0, 4) * 2)
                st.wait("wcol_ok", 0)
                if st.on(4):
                    v.wait_ge(out_done[st.q], st.dma(4, 4))
                stt(part[:, 0, :], rows[:, 0, :], wcol[:, b, 0:1], acc_p[:, st.q, :], ALU.mult, ALU.add).then_inc(s["part_ok"], 1)
                for k in range(1, TOPK):
                    v.wait_ge(s["part_ok"], st.n * (TOPK - 1) + k)
                    to = part[:, k, :] if k < TOPK - 1 else fin[:, st.q, :]
                    stt(to, rows[:, k, :], wcol[:, b, k:k + 1], part[:, k - 1, :], ALU.mult, ALU.add
                        ).then_inc(s["part_ok" if k < TOPK - 1 else "fin_ok"], 1)

            token_tiles(v, step3)

        @block.gpsimd
        def _(g):
            gp = nc.gpsimd
            tt = gp.tensor_tensor

            def among(ap, pattern, base, mult, op, fill=0.0):
                gp.affine_select(out=ap, in_=ap, compare_op=op, fill=fill, base=base, pattern=pattern,
                                 channel_multiplier=mult).then_inc(s["c_small"], 1)
                count[0] += 1
                g.wait_ge(s["c_small"], count[0])

            count = [1]
            gp.memset(ones[:], 1.0)
            for ap in (ident[:], causal[:], headmask[:], evens[:], before[:], ones_h[:], e_lt[:], r_lt[:], r_eq[:]):
                gp.memset(ap, 1.0)
            gp.memset(eps[:, 0:1], LN_EPS)
            gp.memset(eps[:, 1:2], RMS_EPS)
            gp.memset(eid[:], 0)
            gp.memset(rows_u[:, MT:MT + 4, :], 0).then_inc(s["c_small"], 1)
            g.wait_ge(s["c_small"], 1)
            among(ident[:], [[-1, P]], 0, 1, ALU.is_equal)
            for b in range(2):
                among(causal[b * L:(b + 1) * L, :], [[1, L]], 0, -1, ALU.is_ge)
            hm = headmask[:].rearrange("p (b j) -> p b j", j=DK)
            among(hm, [[-DK, P // DK], [0, DK]], 0, 1, ALU.is_ge)
            among(hm, [[DK, P // DK], [0, DK]], DK - 1, -1, ALU.is_ge)
            among(evens[:], [[-2 * DK, 4]], 0, 1, ALU.is_ge)
            among(evens[:], [[2 * DK, 4]], DK - 1, -1, ALU.is_ge)
            among(before[:], [[1, P]], 0, -1, ALU.is_gt)
            among(e_lt[:], [[1, E]], 0, -1, ALU.is_gt)
            among(r_lt[:], [[1, EJ]], -J, -J, ALU.is_ge)
            among(r_eq[:], [[1, EJ]], 0, -J, ALU.is_ge)
            among(r_eq[:], [[-1, EJ]], J - 1, J, ALU.is_ge)
            small = dict(allow_small_or_imprecise_dtypes=True)
            gp.iota(expert_row[:], pattern=[[1, E]], base=0, channel_multiplier=0, **small)
            gp.iota(pad_i[:], pattern=[[1, E * CAP // P]], base=PAD, channel_multiplier=E * CAP // P)
            gp.iota(number[:], pattern=[[TOPK * P, NT], [1, TOPK]], base=0, channel_multiplier=TOPK, **small)
            gp.iota(trash_row[:], pattern=[[TOPK * P, NT], [P, TOPK]], base=TRASH, channel_multiplier=1, **small)
            gp.iota(jrow[:], pattern=[[P, J]], base=0, channel_multiplier=0, **small)
            gp.iota(tcol[:], pattern=[[1, MT]], base=0, channel_multiplier=0, **small)
            gp.iota(rcol[:], pattern=[[ER, EC]], base=0, channel_multiplier=1, **small).then_inc(s["c_setup"], 1)
            g.wait_ge(s["setup_done"], 1)
            g.wait_ge(s["w_in"], 16 * 11)
            g.wait_ge(s["zero_in"], 16)

            def step(st):
                at = st.par(TT)
                if st.on(TT):
                    st.wait("qb_ok", TT)
                    st.wait("ao_ok", TT + 1)
                    for c in GP_K:
                        q_ = qkv[:, at, 0, :].rearrange("p (h o d) -> p h o d", h=H, o=1)[:, c * HC:(c + 1) * HC]
                        k_ = qkv[:, at, 1, :].rearrange("p (o g d) -> p o g d", g=H, o=1)
                        tt(prod[:, c, :].rearrange("p (h g d) -> p h g d", h=HC, g=H),
                           q_.to_broadcast([P, HC, H, DK]), k_.to_broadcast([P, HC, H, DK]), ALU.mult
                           ).then_inc(s[f"kp{c}"], 1)
                if st.on(B):
                    st.wait("x1_ok", B)
                    st.wait("x2_ok", C1)
                    tt(xb[:, st.par(B), :], x1[:, st.par(B), :], b_x[:, 3, :], ALU.add).then_inc(s["xb_ok"], 1)
                if st.on(B):
                    st.wait("kv_cp", B)
                    st.wait("att_ok", C1)
                    tt(qkv[:, st.par(B), 1, :], qkv_raw[:, 1, :], b_x[:, 1, :], ALU.add)
                    tt(qkv[:, st.par(B), 2, :].rearrange("p (d h) -> p d h", h=H),
                       qkv_raw[:, 2, :].rearrange("p (d h) -> p d h", h=H),
                       b_x[:, 2, :].rearrange("p (h d) -> p d h", d=DK), ALU.add).then_inc(s["kvb_ok"], 1)
                if st.on(C1):
                    st.wait("y_ok", C1)
                    st.wait("acc_ok", C1 + 2)
                    tt(res[:, st.par(C1), :], x2[:], y[:], ALU.add).then_inc(s["res_ok"], 1)
                if st.on(B):
                    st.wait("Q_cp", B)
                    tt(qkv[:, st.par(B), 0, :], qkv_raw[:, 0, :], b_x[:, 0, :], ALU.add).then_inc(s["qb_ok"], 1)
                if st.on(TT):
                    st.wait("pr_ok", TT)
                    st.wait("sc_ok", TT)
                    for c in GP_V:
                        p_ = pr[:, c * HC:(c + 1) * HC, :].rearrange("p h (o g) -> p h o g", o=1)
                        v_ = qkv[:, at, 2, :].rearrange("p (o d g) -> p o d g", g=H, o=1)
                        tt(prod[:, c, :].rearrange("p (h d g) -> p h d g", h=HC, g=H),
                           p_.to_broadcast([P, HC, DK, H]), v_.to_broadcast([P, HC, DK, H]), ALU.mult
                           ).then_inc(s[f"vp{c}"], 1)
                if st.on(C2):
                    st.wait("slot_ok", C2)
                    gate(g, s["tick"])
                    for k in range(TOPK):
                        gp.indirect_dma_start(
                            out=list_d, out_offset=bass.IndirectOffsetOnAxis(ap=slot[:, st.par(C2), k:k + 1], axis=0),
                            in_=tid[:, st.par(C2), k:k + 1], in_offset=None).then_inc(sent[st.par(C2)], 16)

            pipeline(g, step)

            for par in range(2):
                g.wait_ge(h_out[par], 16 * (NT // 2))

            gp.iota(spare[:], pattern=[[P, MT]], base=SPARE, channel_multiplier=1, **small).then_inc(s["spare_ok"], 1)

            g.wait_ge(s["plan_ok"], 1)
            over = g.value_load(over_i[0:1, 0:1], min_val=0, max_val=E)
            with g.If(over > 0):
                gp.memset(blank[:], 0.0).then_inc(s["again_col"], 1)
                g.wait_ge(s["again_col"], 1)
                with g.Fori(0, NT) as t:
                    gp.dma_start(choices[bass.ds(t * P, P)], blank.rearrange("p (k d) -> p k d", k=TOPK)
                                 ).then_inc(s["again_out"], 16)
                g.wait_ge(s["again_out"], 16 * NT)

            def move(st):
                if st.on(0):
                    st.wait("gcol_ok", 0)
                    st.wait("gx_ps", 4)
                    gate(g, s["tick"])
                    gp.indirect_dma_start(
                        out=xg[:, st.par(0, 4), :], out_offset=None, in_=h_d,
                        in_offset=bass.IndirectOffsetOnAxis(ap=gcol[:, st.par(0, 4):st.par(0, 4) + 1], axis=0)
                    ).then_inc(g_in[st.par(0, 4)], 16)
                if st.on(SCATTER):
                    st.wait("eo_ok", SCATTER)
                    gate(g, s["tick"])
                    gp.indirect_dma_start(
                        out=eo_d, out_offset=bass.IndirectOffsetOnAxis(ap=dcol[:, st.par(SCATTER, 8):st.par(SCATTER, 8) + 1], axis=0),
                        in_=eo[:, st.par(SCATTER, 4), :], in_offset=None
                    ).then_inc(eo_out[st.par(SCATTER, 4)], 16)

            row_tiles(g, move)
            for n in range(4):
                g.wait_ge(eo_out[n], 16 * (MT // 4))

            with g.If(over > 0):
                g.wait_ge(s["cidx_ok"], 1)
                with g.Fori(0, NT) as t:
                    for k in range(TOPK):
                        gp.tensor_copy(ccol[:, 0, 0:1], cidx[:, bass.ds(t, 1), k]).then_inc(s["again_col"], 1)
                        g.wait_ge(s["again_col"], t * TOPK + (k + 2))
                        gate(g, s["tick"])
                        gp.indirect_dma_start(
                            out=er[:, 0, 0, :], out_offset=None, in_=eo_d[0:PAD, :],
                            in_offset=bass.IndirectOffsetOnAxis(ap=ccol[:, 0, 0:1], axis=0)
                        ).then_inc(s["again_in"], 16)
                        g.wait_ge(s["again_in"], (t * TOPK + (k + 1)) * 16)
                        gate(g, s["tick"])
                        gp.dma_start(choices[bass.ds(t * P, P), k, :], er[:, 0, 0, :]).then_inc(s["again_out"], 16)
                        g.wait_ge(s["again_out"], (t * TOPK + (k + 1)) * 16 + 16 * NT)
                        gate(g, s["tick"])
            g.sem_inc(s["rows_ready"], 1)


_IN = {
    "x": lambda i: i["x"], "ctxT": lambda i: _flat(i["ctx_2048"]).T,
    "wq": lambda i: i["L0_attn_wq"], "wk": lambda i: i["L0_attn_wk"],
    "wvT": lambda i: i["L0_attn_wv"].T, "woT": lambda i: i["L0_attn_wo"].T,
    "fq1": lambda i: _tile(i["L0_attn_fq1_w"].T, (8, 8)), "fq2": lambda i: _tile(i["L0_attn_fq2_w"].T, (8, 8)),
    "fk1": lambda i: _tile(i["L0_attn_fk1_w"].T, (8, 8)), "fk2": lambda i: _tile(i["L0_attn_fk2_w"].T, (8, 8)),
    "fb": lambda i: _tile(_stack([i["L0_attn_fq1_b"], i["L0_attn_fq2_b"], i["L0_attn_fk1_b"], i["L0_attn_fk2_b"]]).T, (8, 1)),
    "hn_w": lambda i: _tile(i["L0_attn_norm_w"].reshape(-1, 1), (8, 1)),
    "WqT": lambda i: i["L0_xattn_Wq"].T, "WkT": lambda i: i["L0_xattn_Wk"].T,
    "WvT": lambda i: i["L0_xattn_Wv"].T, "WoT": lambda i: i["L0_xattn_Wo"].T,
    "xb": lambda i: _stack([i["L0_xattn_bq"], i["L0_xattn_bk"], i["L0_xattn_bv"], i["L0_xattn_bo"]]),
    "nw": lambda i: i["L0_ffn_norm_w"].reshape(1, -1), "gateT": lambda i: i["L0_ffn_gate_w"].T,
    "w13": lambda i: i["L0_ffn_w13"], "w2": lambda i: i["L0_ffn_w2"],
    "sg": lambda i: i["L0_ffn_shared_gate_w"], "su": lambda i: i["L0_ffn_shared_up_w"],
    "sd": lambda i: i["L0_ffn_shared_down_w"],
}


def _flat(a):
    return a.reshape(-1, a.shape[-1])


def _tile(a, n):
    import numpy as np
    return np.tile(a, n)


def _stack(a):
    import numpy as np
    return np.stack(a)


def kernel(**inputs):
    import numpy as np
    import concourse.bacc as bacc
    from concourse.bass_utils import run_bass_kernel_spmd

    host = {k: np.asarray(v) for k, v in inputs.items()}
    nc = bacc.Bacc("TRN2", target_bir_lowering=False, num_devices=1)
    arrays, aps = {}, {}
    for name, lay in _IN.items():
        arrays[f"in_{name}"] = np.ascontiguousarray(lay(host))
        arr = arrays[f"in_{name}"]
        aps[name] = nc.dram_tensor(f"in_{name}", arr.shape, mybir.dt.from_np(arr.dtype), kind="ExternalInput").ap()
    out = nc.dram_tensor("out", host["x"].shape, F32, kind="ExternalOutput").ap()
    decoder_layer_kernel(nc, aps, out)
    return run_bass_kernel_spmd(nc, [arrays], core_ids=[0]).results[0]["out"]
```
